# Optimizing a Trainium2 kernel written in Bass

```python
import numpy as np
import jax
import jax.numpy as jnp

def _softmax(x, axis=-1):
    return jax.nn.softmax(x, axis=axis)

def _gelu(x):
    return jax.nn.gelu(x, approximate=True)

def _silu(x):
    return jax.nn.silu(x)

def _sigmoid(x):
    return jax.nn.sigmoid(x)

def _layernorm(x, axis=-1, eps=1e-05):
    m = jnp.mean(x, axis=axis, keepdims=True)
    v = jnp.var(x, axis=axis, keepdims=True)
    return (x - m) / jnp.sqrt(v + eps)

def _scatter_add(tgt, idx, src, axis=0):
    return tgt.at[idx].add(src)

def _segment_sum(src, seg, n):
    return jax.ops.segment_sum(src, seg, n)
kernel_name = 'mk_vit_tower_d1_tok_img768_r4_dd46cb'

def setup_inputs(seed: int=0):
    np.random.seed(seed)
    _w = jnp.asarray

    def _rec_inputs():
        import jax
        import jax.numpy as jnp
        _rk = jax.random.key(seed)
        x = -0.000147625 + 0.999875 * jax.random.normal(jax.random.fold_in(_rk, 1), (128, 12, 224, 224), jnp.float32)
        return x
    x = _rec_inputs()

    def _L0_tok_setup():
        import jax, jax.numpy as jnp
        import numpy as np
        IMG = 224
        PATCH = 16
        EMBED = 192
        C = 12
        B = 64
        key = jax.random.key(seed)
        k1, k2 = jax.random.split(key)
        x = jax.random.normal(k1, (B, C, IMG, IMG), dtype=jnp.float32)
        channel_weights = jax.random.normal(k2, (C, EMBED), dtype=jnp.float32)
        return {'x': x, 'channel_weights': channel_weights}
    _L0_tok_all = _L0_tok_setup()
    _L0_tok_in = {k: v for k, v in _L0_tok_all.items() if k in ('channel_weights',)}
    del _L0_tok_all

    def _L0_attn_setup():
        import jax, jax.numpy as jnp
        import numpy as np
        N_HEAD = 12
        key = jax.random.key(seed)
        k1, k2, k3 = jax.random.split(key, 3)
        B, T, C = (8, 256, 192)
        x = jax.random.normal(k1, (B, T, C), dtype=jnp.float32)
        W_attn = jax.random.normal(k2, (3 * C, C), dtype=jnp.float32) * 0.02
        b_attn = jax.random.normal(k3, (3 * C,), dtype=jnp.float32) * 0.02
        return {'x': x, 'W_attn': W_attn, 'b_attn': b_attn}
    _L0_attn_all = _L0_attn_setup()
    _L0_attn_in = {k: v for k, v in _L0_attn_all.items() if k in ('W_attn', 'b_attn')}
    del _L0_attn_all

    def _L0_ffn_setup():
        import jax, jax.numpy as jnp
        import numpy as np
        ATOM = {'vm': 0, 'im': 1, 'cm': 2, 'sc': 3, 'cc': 4}
        TASK_PAIRS = [('vm', 'sc'), ('vm', 'cc'), ('im', 'sc'), ('im', 'cc'), ('cm', 'sc'), ('cm', 'cc')]
        SRC_IDX = np.array([[ATOM[l], ATOM[r]] for l, r in TASK_PAIRS], dtype=np.int32)
        DST_IDX = np.array([[ATOM[r], ATOM[l]] for l, r in TASK_PAIRS], dtype=np.int32)
        NCLS = 6
        NATOMS = 5

        def _l2norm(x, eps=1e-12):
            return x / jnp.clip(jnp.linalg.norm(x, axis=-1, keepdims=True), eps)
        key = jax.random.key(seed)
        ks = jax.random.split(key, 12)
        B, NPATCH, D, H = (64, 197, 192, 768)
        std = 0.02
        x = jax.random.normal(ks[0], (B, NCLS + NPATCH, D), dtype=jnp.float32)
        fc1_w = jax.random.normal(ks[1], (H, D), dtype=jnp.float32) * std
        fc1_b = jnp.zeros((H,), jnp.float32)
        fc2_w = jax.random.normal(ks[2], (D, H), dtype=jnp.float32) * std
        fc2_b = jnp.zeros((D,), jnp.float32)
        gate_pair = jax.random.normal(ks[3], (NCLS, 2, D), dtype=jnp.float32) * std
        atom_in_w = jax.random.normal(ks[4], (NATOMS, H, D), dtype=jnp.float32) * std
        atom_in_b = jax.random.normal(ks[5], (NATOMS, H), dtype=jnp.float32) * std
        atom_out_w = jax.random.normal(ks[6], (NATOMS, D, H), dtype=jnp.float32) * std
        atom_out_b = jax.random.normal(ks[7], (NATOMS, D), dtype=jnp.float32) * std
        balance_bias = jnp.zeros((NCLS, 2), jnp.float32)
        return {'x': x, 'fc1_w': fc1_w, 'fc1_b': fc1_b, 'fc2_w': fc2_w, 'fc2_b': fc2_b, 'gate_pair': gate_pair, 'atom_in_w': atom_in_w, 'atom_in_b': atom_in_b, 'atom_out_w': atom_out_w, 'atom_out_b': atom_out_b, 'balance_bias': balance_bias}
    _L0_ffn_all = _L0_ffn_setup()
    _L0_ffn_in = {k: v for k, v in _L0_ffn_all.items() if k in ('fc1_w', 'fc1_b', 'fc2_w', 'fc2_b', 'gate_pair', 'atom_in_w', 'atom_in_b', 'atom_out_w', 'atom_out_b', 'balance_bias')}
    del _L0_ffn_all
    return {'x': x, 'L0_tok_channel_weights': _L0_tok_in['channel_weights'], 'L0_attn_W_attn': _L0_attn_in['W_attn'], 'L0_attn_b_attn': _L0_attn_in['b_attn'], 'L0_ffn_fc1_w': _L0_ffn_in['fc1_w'], 'L0_ffn_fc1_b': _L0_ffn_in['fc1_b'], 'L0_ffn_fc2_w': _L0_ffn_in['fc2_w'], 'L0_ffn_fc2_b': _L0_ffn_in['fc2_b'], 'L0_ffn_gate_pair': _L0_ffn_in['gate_pair'], 'L0_ffn_atom_in_w': _L0_ffn_in['atom_in_w'], 'L0_ffn_atom_in_b': _L0_ffn_in['atom_in_b'], 'L0_ffn_atom_out_w': _L0_ffn_in['atom_out_w'], 'L0_ffn_atom_out_b': _L0_ffn_in['atom_out_b'], 'L0_ffn_balance_bias': _L0_ffn_in['balance_bias']}

def reference(x, L0_tok_channel_weights, L0_attn_W_attn, L0_attn_b_attn, L0_ffn_fc1_w, L0_ffn_fc1_b, L0_ffn_fc2_w, L0_ffn_fc2_b, L0_ffn_gate_pair, L0_ffn_atom_in_w, L0_ffn_atom_in_b, L0_ffn_atom_out_w, L0_ffn_atom_out_b, L0_ffn_balance_bias):
    import jax
    import jax.numpy as jnp

    def _L0_tok_ref(x, channel_weights):
        import jax, jax.numpy as jnp
        import numpy as np
        IMG = 224
        PATCH = 16
        EMBED = 192
        C = 12
        B = 64
        Bb, Cc, H, W = x.shape
        K = PATCH
        n = H // K
        pooled = x.reshape(Bb, Cc, n, K, n, K).sum(axis=(3, 5))
        out = jnp.einsum('bcij,ce->bije', pooled, channel_weights)
        return out.reshape(Bb, n * n, EMBED)

    def _L0_attn_ref(x, W_attn, b_attn):
        import jax, jax.numpy as jnp
        import numpy as np
        N_HEAD = 12
        B, T, C = x.shape
        hd = C // N_HEAD
        qkv = x @ W_attn.T + b_attn
        q, k, v = jnp.split(qkv, 3, axis=-1)

        def to_heads(t):
            return t.reshape(B, T, N_HEAD, hd).transpose(0, 2, 1, 3)
        q, k, v = (to_heads(q), to_heads(k), to_heads(v))
        scale = 1.0 / jnp.sqrt(jnp.asarray(hd, dtype=x.dtype))
        att = jnp.einsum('bhqd,bhkd->bhqk', q * scale, k)
        causal = jnp.tril(jnp.ones((T, T), dtype=bool))
        att = jnp.where(causal, jnp.maximum(att, 0.0), 0.0)
        y = jnp.einsum('bhqk,bhkd->bhqd', att, v)
        return y.transpose(0, 2, 1, 3).reshape(B, T, C)

    def _L0_ffn_ref(x, fc1_w, fc1_b, fc2_w, fc2_b, gate_pair, atom_in_w, atom_in_b, atom_out_w, atom_out_b, balance_bias):
        import jax, jax.numpy as jnp
        import numpy as np
        ATOM = {'vm': 0, 'im': 1, 'cm': 2, 'sc': 3, 'cc': 4}
        TASK_PAIRS = [('vm', 'sc'), ('vm', 'cc'), ('im', 'sc'), ('im', 'cc'), ('cm', 'sc'), ('cm', 'cc')]
        SRC_IDX = np.array([[ATOM[l], ATOM[r]] for l, r in TASK_PAIRS], dtype=np.int32)
        DST_IDX = np.array([[ATOM[r], ATOM[l]] for l, r in TASK_PAIRS], dtype=np.int32)
        NCLS = 6
        NATOMS = 5

        def _l2norm(x, eps=1e-12):
            return x / jnp.clip(jnp.linalg.norm(x, axis=-1, keepdims=True), eps)
        src = jnp.asarray(SRC_IDX)
        dst = jnp.asarray(DST_IDX)
        D = x.shape[-1]
        H = atom_in_w.shape[1]
        cls_tokens = x[:, :NCLS]
        patch_tokens = x[:, NCLS:]
        patch_out = jax.nn.gelu(patch_tokens @ fc1_w.T + fc1_b, approximate=False) @ fc2_w.T + fc2_b
        gate_in = _l2norm(cls_tokens.astype(jnp.float32))
        gate_w = _l2norm(gate_pair.astype(jnp.float32))
        gate_logits = jnp.einsum('bnd,nrd->bnr', gate_in, gate_w) + balance_bias[None]
        route_probs = jax.nn.softmax(gate_logits, axis=-1)
        chosen_route = jnp.argmax(route_probs, axis=-1)
        hid_all = jax.nn.gelu(jnp.einsum('bnd,ahd->bnah', cls_tokens, atom_in_w) + atom_in_b[None, None], approximate=False)
        sh_pair = hid_all[:, jnp.arange(NCLS)[:, None], src, :]
        route_out_w = atom_out_w[dst.reshape(-1)].reshape(NCLS, 2, D, H)
        route_candidates = jnp.einsum('bnrh,nrdh->bnrd', sh_pair, route_out_w) + atom_out_b[dst][None]
        chosen_w = jnp.take_along_axis(route_probs, chosen_route[..., None], axis=-1)
        chosen_cand = jnp.take_along_axis(route_candidates, chosen_route[:, :, None, None], axis=2)[:, :, 0]
        cls_out = chosen_cand * chosen_w.astype(chosen_cand.dtype)
        return jnp.concatenate([cls_out, patch_out], axis=1)
    h = _L0_tok_ref(x, L0_tok_channel_weights)
    h = h + _L0_attn_ref(_layernorm(h, axis=-1), L0_attn_W_attn, L0_attn_b_attn)
    h = h + _L0_ffn_ref(_layernorm(h, axis=-1), L0_ffn_fc1_w, L0_ffn_fc1_b, L0_ffn_fc2_w, L0_ffn_fc2_b, L0_ffn_gate_pair, L0_ffn_atom_in_w, L0_ffn_atom_in_b, L0_ffn_atom_out_w, L0_ffn_atom_out_b, L0_ffn_balance_bias)
    return h

_drawn_inputs = setup_inputs


def setup_inputs(seed=0):
    import zlib

    import numpy as np

    out = dict(_drawn_inputs(seed))
    spreads = {'L0_ffn_fc1_b': (0.0, 2.0), 'L0_ffn_fc2_b': (0.0, 2.0), 'L0_ffn_balance_bias': (0.0, 2.0)}
    factors = {'L0_attn_W_attn': 6.457,
     'L0_attn_b_attn': 8.0,
     'L0_ffn_fc1_w': 8.0,
     'L0_ffn_fc2_w': 8.0,
     'L0_ffn_gate_pair': 64.0,
     'L0_ffn_atom_in_w': 64.0,
     'L0_ffn_atom_in_b': 64.0,
     'L0_ffn_atom_out_w': 64.0,
     'L0_ffn_atom_out_b': 64.0}
    for name, (base, spread) in spreads.items():
        noise = np.random.default_rng([zlib.crc32(name.encode()), seed]).standard_normal(out[name].shape)
        drawn = base * np.exp(spread * noise) if base else spread * noise
        out[name] = jnp.asarray(drawn.astype(out[name].dtype))
    for name, factor in factors.items():
        out[name] = (out[name] * factor).astype(out[name].dtype)
    return out
```

```python
from contextlib import ExitStack

import numpy as np

import concourse.bass as bass
from concourse import mybir

F32 = mybir.dt.float32
F16 = mybir.dt.float16
ACT = mybir.ActivationFunctionType
ALU = mybir.AluOpType
AX = mybir.AxisListType

NIMG, NCH, SIDE, PATCH = 128, 12, 14, 16
TOK = SIDE * SIDE
PIX = PATCH * PATCH
EMB = 192
HEADS, HD = 12, 16
HID = 768
NCLS, NATOM = 6, 5
EPS = 1e-5

GI = 4
GT = GI * TOK
TP = 112
NT = GT // TP
NG = NIMG // GI
NHALF = 2 * NT
HCH = NCH // 2
RING = 7
ROW = NCH * PIX
K0, K1 = 128, TOK - 128
PAIRS = HEADS // 2
QUADS = HEADS // 4
SLOTS = GI * PAIRS
NQUAD = GI * QUADS
MT = HID // 128
EH = EMB // 2
HALF_T = GT // 2
CHUNKS = 2 * MT
WSCALE = 64.0

POOL_NEXT = {13: 0, 15: 1, 17: 2, 19: 3, 21: 4, 23: 5}
POOL_CUR = {0: 6, 1: 7, 2: 8, 4: 9, 5: 10, 6: 11, 8: 12, 9: 13}
NPAIR = (NT + 1) // 2
H2_SLOT, XT_SLOT, UT_SLOT, H1_SLOT, PT_SLOT = 1, 9, 13, 14, 23
FC1_SLOT = 12

SRC = [[n // 2, 3 + n % 2] for n in range(NCLS)]
DST = [[3 + n % 2, n // 2] for n in range(NCLS)]


def stages(t, python_t):
    def there(d):
        return 0 <= python_t + d < NG
    return {
        "pool_next": t + 2 if there(2) else None,
        "pool_cur": t + 1 if there(1) else None,
        "norm1": t + 1 if there(1) else None,
        "attend": t if there(0) else None,
        "last_av": t - 1 if there(-1) else None,
        "norm2": t - 1 if there(-1) else None,
        "fc1": t - 1 if there(-1) else None,
        "fc2": t - 2 if there(-2) else None,
        "par": python_t % 2,
    }


ATOM_TOKENS = [[0, 1], [2, 3], [4, 5], [0, 2, 4], [1, 3, 5]]
CANDS_BEFORE = [0, 2, 4, 6, 9, 12]
CLS_SS, CLS_LG = 4, 13


def shared_uses(st):
    uses = []
    for s in range(SLOTS):
        if st["attend"] is not None and s % PAIRS == 0:
            uses.append((s, "v", s // PAIRS, "attend"))
        if st["norm2"] is not None and 0 <= s - H2_SLOT < NPAIR:
            uses.append((s, "h2", s - H2_SLOT, "norm2"))
        if st["norm2"] is not None and 0 <= s - XT_SLOT < 3:
            uses.append((s, "xt", s - XT_SLOT, "norm2"))
        if st["norm1"] is not None and s == UT_SLOT:
            uses.append((s, "ut", 0, "norm1"))
        if st["norm1"] is not None and 0 <= s - H1_SLOT < NPAIR:
            uses.append((s, "h1", s - H1_SLOT, "norm1"))
        if st["norm1"] is not None and s == PT_SLOT:
            uses.append((s, "pt", 0, "norm1"))
    return uses


FIRST_T, LAST_T = -2, NG + 1
LOOP_T0, LOOP_T1 = 2, NG - 2


def iterations(eng, body):
    for t in range(FIRST_T, LOOP_T0):
        body(t, stages(t, t), stages(t - 1, t - 1))
    with eng.Fori(0, (LOOP_T1 - LOOP_T0) // 2) as turn:
        for half in range(2):
            t = turn * 2 + LOOP_T0
            body(t + half, stages(t + half, LOOP_T0 + half), stages(t + (half - 1), LOOP_T0 + half - 1))
    for t in range(LOOP_T1, LAST_T + 1):
        body(t, stages(t, t), stages(t - 1, t - 1))


def wait(eng, sem, value):
    if not (isinstance(value, int) and value <= 0):
        eng.wait_ge(sem, value)


def vit_tower_kernel(nc, d, out, cls_x, cls_h):
    with ExitStack() as ctx:
        def sb(name, shape, dt):
            return ctx.enter_context(nc.sbuf_tensor(name, shape, dt))

        def bank(name):
            return ctx.enter_context(nc.psum_tensor(name, [128, 512], F32))

        def sem(name):
            return ctx.enter_context(nc.semaphore(name))

        g_ps = bank("g_ps")
        s_ps = [bank("s_ps0"), bank("s_ps1")]
        k1_ps = bank("k1_ps")
        y_ps = bank("y_ps")
        f_ps = [bank("f_ps0"), bank("f_ps1")]
        m_ps = bank("m_ps")
        m_ps16 = m_ps[:, :].bitcast(F16)

        ident16 = sb("ident16", [128, 128], F16)
        ident32 = sb("ident32", [128, 128], F32)
        head_sel = sb("head_sel", [128, 64], F16)
        mask_k0 = sb("mask_k0", [128, 2 * TOK], F32)
        mask_k1 = sb("mask_k1", [K1, 4 * K1], F32)
        neg_lo = sb("neg_lo", [128, 1], F32)
        spread = sb("spread", [NCH, 64], F32)
        bias_row = sb("bias_row", [1, 64], F32)
        ones_pad = sb("ones_pad", [128, TP], F16)
        minus_half = sb("minus_half", [128, NT], F32)

        c_raw = sb("c_raw", [NCH, EMB], F32)
        c_cen = sb("c_cen", [NCH, EMB], F32)
        c_sum = sb("c_sum", [NCH, 2], F32)
        c_stack = sb("c_stack", [128, EMB], F16)
        cct = sb("cct", [128, 2, 64], F32)
        b_attn = sb("b_attn", [1, 3 * EMB], F32)
        mq_t = sb("mq_t", [HD, HEADS, 64], F32)
        mk_t = sb("mk_t", [HD, HEADS, 64], F32)
        a_stack = sb("a_stack", [128, HEADS * 64], F16)
        mv_stack = sb("mv_stack", [128, EMB], F16)
        setup16 = sb("setup16", [64, HEADS * 64], F16)
        w1_hi = sb("w1_hi", [128, 3, HID], F16)
        w1_lo = sb("w1_lo", [128, 2, HID], F16)
        w2_hi = sb("w2_hi", [128, MT, EMB], F16)
        w2_lo = sb("w2_lo", [128, MT, EMB], F16)
        b1 = sb("b1", [128, MT], F32)
        b2_raw = sb("b2_raw", [64, EMB], F32)
        b2_stack = sb("b2_stack", [128, EMB], F16)
        b2_tmp = sb("b2_tmp", [64, EMB], F16)

        x_ring = sb("x_ring", [TP, RING, HCH * PIX], F32)
        pooled = sb("pooled", [TP, 2, NT, NCH], F32)
        u_tok = sb("u_tok", [TP, NT, 8, 16], F16)
        u_stack = sb("u_stack", [128, GT], F16)
        h_tok = sb("h_tok", [128, 2, NT * EMB], F32)
        bn1 = sb("bn1", [TP, NT, 6], F32)
        st1s = sb("st1s", [TP, 3, NT], F32)
        var1 = sb("var1", [TP, NT], F32)
        rstd1 = sb("rstd1", [TP, NT], F32)
        pn = sb("pn", [TP, NT, NCH], F32)
        p_tok = sb("p_tok", [TP, NT, 8, 16], F16)
        p_stack = sb("p_stack", [128, 2, GT], F16)
        g_hi = sb("g_hi", [128, 2, TOK], F16)
        g_stack = sb("g_stack", [128, 2, TOK], F16)
        st0 = sb("st0", [128, 4, 2 * TOK], F32)
        st1 = sb("st1", [K1, 2, 4 * K1], F32)
        v0 = sb("v0", [128, 2, HEADS, 32], F32)
        v1 = sb("v1", [K1, 2, HEADS, 32], F32)
        y_t = sb("y_t", [128, 2, 2, QUADS, GT], F16)
        h2_tok = sb("h2_tok", [128, 2, NT * EMB], F32)
        bn2 = sb("bn2", [TP, NT, 6], F32)
        st2s = sb("st2s", [TP, 3, NT], F32)
        sum2 = sb("sum2", [TP, NT], F32)
        mean2 = sb("mean2", [TP, NT], F32)
        var2 = sb("var2", [TP, NT], F32)
        rstd2 = sb("rstd2", [TP, NT], F32)
        xhat = sb("xhat", [128, NT * EMB], F32)
        x_tok = sb("x_tok", [TP, NT, 2, EMB], F16)
        x_stack = sb("x_stack", [128, 3, GT], F16)
        gelu32 = sb("gelu32", [128, 3, HALF_T], F32)
        hid = sb("hid", [128, 2, MT, GT], F16)
        o_tok = sb("o_tok", [128, NT * EMB], F32)

        hid32 = hid[:, :, :, :].rearrange("p a m t -> p (a m t)").bitcast(F32)
        w1_raw = hid32[:, 0:3 * HID].rearrange("p (k n) -> p k n", k=3)
        w2_raw = hid32[:, 3 * HID:3 * HID + MT * EMB].rearrange("p (m n) -> p m n", m=MT)
        wa_raw = hid32[:, 3 * HID + MT * EMB:3 * HID + MT * EMB + 2 * 3 * EMB].rearrange("p (k n) -> p k n", k=2)

        a_in = x_ring[:, :, :].rearrange("p r n -> p (r n)")[0:EH, 0:2 * NATOM * HID].rearrange("p (k n) -> p k n", k=2)
        a_out = sb("a_out", [128, MT, NATOM * EMB], F32)
        cx = h_tok[:, 0, 0:NCLS * EMB].rearrange("p (n e) -> p n e", n=NCLS)
        ch = h_tok[:, 1, 0:NCLS * EMB].rearrange("p (n e) -> p n e", n=NCLS)
        y32 = y_t[:, :, :, :, :].rearrange("p a b q t -> p (a b q t)").bitcast(F32)
        gate_w = y32[:, 0:2 * NCLS * EMB].rearrange("p (n e) -> p n e", n=2 * NCLS)
        gate_tmp = y32[:, 2 * NCLS * EMB:4 * NCLS * EMB].rearrange("p (n e) -> p n e", n=2 * NCLS)
        b_out = h2_tok[:, 0, 0:NATOM * EMB].rearrange("p (a e) -> p a e", a=NATOM)
        cx_t = st0[:, :, :].rearrange("p a b -> p (a b)")[:, 0:2 * NCLS * 128].rearrange("p (k n b) -> p k n b", k=2, n=NCLS)
        c_hid = [hid32[:, i * MT * 3 * 128:(i + 1) * MT * 3 * 128].rearrange("p (m n) -> p m n", m=MT) for i in range(2)]
        c_acc = o_tok[:, 0:NCLS * EMB].rearrange("p (n e) -> p n e", n=NCLS)
        c_tmp = xhat[:, 0:2 * EMB].rearrange("p (n e) -> p n e", n=2)
        b_in = sb("b_in", [128, NATOM * MT], F32)
        bal = sb("bal", [128, 2 * NCLS], F32)
        ss = sb("ss", [128, 3 * NCLS], F32)
        nrm = sb("nrm", [128, 3 * NCLS], F32)
        half_c = sb("half_c", [128, 3 * NCLS], F32)
        lg = sb("lg", [128, NCLS, 2], F32)
        pr = sb("pr", [128, NCLS, 2], F32)
        gs = sb("gs", [128, 6, NCLS], F32)
        wgt = sb("wgt", [128, NCLS, 2], F32)

        const_in = sem("const_in")
        wts_in = sem("wts_in")
        const_set = sem("const_set")
        setup_v = sem("setup_v")
        setup_p = sem("setup_p")
        ready_v = sem("ready_v")
        x_in = [sem(f"x_in{i}") for i in range(RING)]
        x_halved = sem("x_halved")
        x_pooled = sem("x_pooled")
        v_full = sem("v_full")
        h2_full = sem("h2_full")
        xt_full = sem("xt_full")
        ut_full = sem("ut_full")
        h1_full = sem("h1_full")
        pt_full = sem("pt_full")
        u_hi_set = sem("u_hi_set")
        u_tok_set = sem("u_tok_set")
        u_stack_set = sem("u_stack_set")
        h_set = sem("h_set")
        bn1_set = sem("bn1_set")
        part1_set = sem("part1_set")
        sq1_set = sem("sq1_set")
        sq2_set = sem("sq2_set")
        var1_set = sem("var1_set")
        rstd1_set = sem("rstd1_set")
        pn_set = sem("pn_set")
        p_hi_set = sem("p_hi_set")
        p_tok_set = sem("p_tok_set")
        p_stack_set = sem("p_stack_set")
        g_full = sem("g_full")
        g_hi_set = sem("g_hi_set")
        g_split = sem("g_split")
        scores_full = sem("scores_full")
        relu0_set = sem("relu0_set")
        relu1_set = sem("relu1_set")
        v_set = sem("v_set")
        y_full = sem("y_full")
        y_hi_set = sem("y_hi_set")
        y_lo_set = sem("y_lo_set")
        h2_set = sem("h2_set")
        bn2_set = sem("bn2_set")
        part2_set = sem("part2_set")
        var2_set = sem("var2_set")
        mean2_set = sem("mean2_set")
        rstd2_set = sem("rstd2_set")
        xhat_set = sem("xhat_set")
        x_hi_set = sem("x_hi_set")
        x_lo_set = sem("x_lo_set")
        x_stack_set = sem("x_stack_set")
        fc1_full = sem("fc1_full")
        gelu_set = sem("gelu_set")
        hid_set = sem("hid_set")
        fc2_full = sem("fc2_full")
        o_set = sem("o_set")
        out_done = sem("out_done")
        cls_out = sem("cls_out")
        cls_w_in = sem("cls_w_in")
        cls_in = sem("cls_in")
        cls_v = sem("cls_v")
        cls_pow = sem("cls_pow")
        cls_exp = sem("cls_exp")
        ct_full = sem("ct_full")
        ct_set = sem("ct_set")
        ch_full = sem("ch_full")
        ch_set = sem("ch_set")
        cand_full = sem("cand_full")
        cand_tmp = sem("cand_tmp")
        cand_set = sem("cand_set")
        cls_done = sem("cls_done")

        CT_PARTS = [(s_ps[0], 0, 0, 4), (s_ps[1], 0, 4, 2), (f_ps[0], 1, 0, 4), (f_ps[1], 1, 4, 2)]
        CONSTS = 12
        WEIGHTS = 11

        def ring_reuse(g, hk):
            return NHALF * g + (hk - RING) + 1

        block = ctx.enter_context(nc.Block())

        @block.sync
        def _(sp):
            for dst, src in ((c_raw[:, :], d["cw"]), (spread[:, :], d["spread"]), (bias_row[:, :], d["bias_row"]),
                             (b_attn[:, :], d["b_attn"]), (wa_raw[:, 0, :], d["wa_t"][0:128, :]),
                             (wa_raw[0:64, 1, :], d["wa_t"][128:EMB, :]), (ident16[:, :], d["ident16"]),
                             (ident32[:, :], d["ident32"]), (head_sel[:, :], d["head_sel"]),
                             (mask_k0[:, :], d["mask_k0"]), (mask_k1[:, :], d["mask_k1"]),
                             (neg_lo[:, :], d["neg_lo"])):
                sp.dma_start(dst, src).then_inc(const_in, 16)

            def load_x(g, hk):
                wait(sp, x_pooled, ring_reuse(g, hk))
                src = d["x"][bass.ds(g * GT + (hk // 2) * TP, TP), (hk % 2) * HCH * PIX:(hk % 2 + 1) * HCH * PIX]
                sp.dma_start(x_ring[:, hk % RING, :], src).then_inc(x_in[hk % RING], 16)

            for hk in range(3):
                load_x(0, hk)
            for dst, src in ((w1_raw[:, 0, :], d["w1_t"][0:128, :]), (w1_raw[0:64, 1, :], d["w1_t"][128:EMB, :]),
                             (w1_raw[64:128, 1, :], d["w1_t"][0:64, :]), (w1_raw[:, 2, :], d["w1_t"][64:EMB, :]),
                             (w2_raw[:, :, :], d["w2_t"].rearrange("(m p) n -> p m n", p=128)),
                             (b1[:, :], d["b1"]), (b2_raw[0:1, :], d["b2"]), (b2_raw[32:33, :], d["b2"]),
                             (ones_pad[:, :], d["ones_pad"]),
                             (a_out[:, :, :], d["a_out_t"].rearrange("(m p) n -> p m n", p=128)),
                             (b_in[:, :], d["b_in"])):
                sp.dma_start(dst, src).then_inc(wts_in, 16)
            for hk in range(3, RING):
                load_x(0, hk)

            def body(t, st, before):
                par = st["par"]
                for s in range(SLOTS):
                    for stage, table in (("pool_cur", POOL_CUR), ("pool_next", POOL_NEXT)):
                        if st[stage] is not None and s in table:
                            g, hk = st[stage], table[s]
                            if hk + RING < NHALF:
                                load_x(g, hk + RING)
                            elif stage == "pool_next" or st["pool_next"] is not None:
                                load_x(g + 1, hk + RING - NHALF)
                    if s == 7 and st["fc2"] is not None:
                        g = st["fc2"]
                        sp.wait_ge(o_set, NT * g + NT)
                        sp.dma_start(out[bass.ds(g * GT, GT), :].rearrange("(k p) e -> p k e", p=TP),
                                     o_tok[0:TP, :].rearrange("p (k e) -> p k e", k=NT)).then_inc(out_done, 16)
                    if s == 8 and st["norm2"] is not None:
                        g = st["norm2"]
                        sp.wait_ge(xhat_set, g + 1)
                        for b in range(GI):
                            k, r = divmod(b * TOK, TP)
                            for buf, dst in ((xhat[:, :], cls_x), (h2_tok[:, (par + 1) % 2, :], cls_h)):
                                sp.dma_start(dst[bass.ds((g * GI + b) * NCLS, NCLS), :],
                                             buf[r:r + NCLS, k * EMB:(k + 1) * EMB]).then_inc(cls_out, 16)

            iterations(sp, body)

            sp.wait_ge(x_pooled, NHALF * NG)
            sp.dma_start(a_in[:, 0, :], d["a_in_t"][0:EH, :]).then_inc(cls_w_in, 16)
            sp.dma_start(a_in[:, 1, :], d["a_in_t"][EH:EMB, :]).then_inc(cls_w_in, 16)
            sp.wait_ge(h2_set, NPAIR * NG)
            sp.dma_start(gate_w, d["gate"].partition_broadcast(128).rearrange("p (n e) -> p n e", e=EMB)).then_inc(cls_w_in, 16)
            sp.dma_start(bal[:, :], d["bal"].partition_broadcast(128)).then_inc(cls_w_in, 16)
            sp.wait_ge(cls_out, 16 * 2 * GI * NG)
            sp.dma_start(cx, cls_x.rearrange("(b n) e -> b n e", n=NCLS)).then_inc(cls_in, 16)
            sp.dma_start(ch, cls_h.rearrange("(b n) e -> b n e", n=NCLS)).then_inc(cls_in, 16)
            sp.wait_ge(o_set, NT * NG)
            sp.dma_start(b_out, d["b_out"].partition_broadcast(128).rearrange("p (a e) -> p a e", e=EMB)).then_inc(cls_w_in, 16)
            sp.wait_ge(out_done, 16 * NG)
            sp.wait_ge(cand_set, 2 * NCLS)
            sp.dma_start(out.rearrange("(b t) e -> b t e", t=TOK)[:, 0:NCLS, :], c_acc).then_inc(cls_done, 16)
            sp.wait_ge(cls_done, 16)


        @block.gpsimd
        def _(pool):
            pool.wait_ge(ready_v, 1)

            def halve(g, hk):
                pool.wait_ge(x_in[hk % RING], 16 * (g * (NHALF // RING) + hk // RING + 1))
                w = x_ring[:, hk % RING, :].rearrange("p (c n) -> p c n", c=HCH)
                nc.gpsimd.tensor_tensor(w[:, :, 0:PIX // 2], w[:, :, 0:PIX // 2], w[:, :, PIX // 2:PIX],
                                        ALU.add).then_inc(x_halved, 1)

            def body(t, st, before):
                for s in range(SLOTS):
                    if st["pool_cur"] is not None and s in POOL_CUR:
                        halve(st["pool_cur"], POOL_CUR[s])
                    if st["pool_next"] is not None and s in POOL_NEXT:
                        halve(st["pool_next"], POOL_NEXT[s])
                    if st["norm2"] is not None and s == 5:
                        g = st["norm2"]
                        pool.wait_ge(var2_set, g + 1)
                        nc.gpsimd.tensor_tensor(rstd2[:, :], var2[:, :], minus_half[0:TP, :],
                                                ALU.pow).then_inc(rstd2_set, 1)
                    if st["norm2"] is not None and s == 7:
                        g = st["norm2"]
                        pool.wait_ge(x_hi_set, g + 1)
                        nc.gpsimd.tensor_tensor(x_tok[:, :, 1, :], xhat[0:TP, :].rearrange("p (k e) -> p k e", k=NT),
                                                x_tok[:, :, 0, :], ALU.subtract).then_inc(x_lo_set, 1)
                    if st["norm1"] is not None and s == 19:
                        g = st["norm1"]
                        pool.wait_ge(var1_set, g + 1)
                        nc.gpsimd.tensor_tensor(rstd1[:, :], var1[:, :], minus_half[0:TP, :],
                                                ALU.pow).then_inc(rstd1_set, 1)
                    if st["fc1"] is not None and s >= FC1_SLOT:
                        g, c = st["fc1"], s - FC1_SLOT
                        m, lo = c % MT, (c // MT) * HALF_T
                        pool.wait_ge(gelu_set, CHUNKS * g + c + 1)
                        nc.gpsimd.tensor_tensor(hid[:, 1, m, lo:lo + HALF_T], gelu32[:, c % 3, :],
                                                hid[:, 0, m, lo:lo + HALF_T], ALU.subtract).then_inc(hid_set, 1)

            iterations(pool, body)
            pool.wait_ge(cls_v, CLS_SS)
            nc.gpsimd.tensor_tensor(nrm[:, :], ss[:, :], half_c[:, :], ALU.pow).then_inc(cls_pow, 1)

        @block.scalar
        def _(act):
            act.wait_ge(ready_v, 1)

            def body(t, st, before):
                par = st["par"]
                g = st["attend"]

                def copy_g_hi(s):
                    act.wait_ge(g_full, SLOTS * g + s + 1)
                    wait(act, g_split, SLOTS * g + s - 1)
                    nc.scalar.activation(g_hi[:, s % 2, :], g_ps[:, 0:TOK], ACT.Copy).then_inc(g_hi_set, 1)

                def copy_y_hi(gy, q, gpar):
                    act.wait_ge(y_full, NQUAD * gy + q + 1)
                    wait(act, h2_set, NPAIR * (gy - 1))
                    b = q // QUADS
                    nc.scalar.activation(y_t[:, gpar, 0, q % QUADS, b * TOK:(b + 1) * TOK], y_ps[:, 0:TOK],
                                         ACT.Copy).then_inc(y_hi_set, 1)

                for s in range(SLOTS):
                    if s == 0 and st["last_av"] is not None:
                        copy_y_hi(st["last_av"], NQUAD - 1, 1 - par)
                    if g is not None:
                        if s == 0:
                            copy_g_hi(0)
                        if s + 1 < SLOTS:
                            copy_g_hi(s + 1)
                        if s % PAIRS == 0:
                            b = s // PAIRS
                            act.wait_ge(v_full, GI * g + b + 1)
                            wait(act, y_full, NQUAD * g + QUADS * (b - 1))
                            nc.scalar.activation(v0[:, b % 2, :, 0:HD], m_ps[:, 0:EMB].rearrange("p (h d) -> p h d", h=HEADS),
                                                 ACT.Copy)
                            nc.scalar.activation(v1[:, b % 2, :, 0:HD],
                                                 m_ps[0:K1, EMB:2 * EMB].rearrange("p (h d) -> p h d", h=HEADS),
                                                 ACT.Copy).then_inc(v_set, 1)
                        if s >= 2 and s % 2 == 0:
                            copy_y_hi(g, s // 2 - 1, par)
                    if st["norm2"] is not None:
                        n2 = st["norm2"]
                        if s == 7:
                            act.wait_ge(xhat_set, n2 + 1)
                            wait(act, x_stack_set, 3 * n2)
                            nc.scalar.activation(x_tok[:, :, 0, :], xhat[0:TP, :].rearrange("p (k e) -> p k e", k=NT),
                                                 ACT.Copy).then_inc(x_hi_set, 1)
                        if 0 <= s - XT_SLOT < 3:
                            c = s - XT_SLOT
                            act.wait_ge(xt_full, 3 * n2 + c + 1)
                            wait(act, fc1_full, CHUNKS * n2)
                            nc.scalar.activation(x_stack[:, c, :], m_ps16[:, 0:GT], ACT.Copy).then_inc(x_stack_set, 1)
                    if st["norm1"] is not None:
                        n1 = st["norm1"]
                        if s == UT_SLOT:
                            act.wait_ge(ut_full, n1 + 1)
                            wait(act, h1_full, NPAIR * n1)
                            nc.scalar.activation(u_stack[:, :], m_ps16[:, 0:GT], ACT.Copy).then_inc(u_stack_set, 1)
                        if 0 <= s - H1_SLOT < NPAIR:
                            i = s - H1_SLOT
                            n = min(2, NT - 2 * i) * EMB
                            act.wait_ge(h1_full, NPAIR * n1 + i + 1)
                            wait(act, h2_set, NPAIR * (n1 - 1))
                            nc.scalar.activation(h_tok[0:TP, 1 - par, 2 * i * EMB:2 * i * EMB + n], m_ps[0:TP, 0:n],
                                                 ACT.Copy).then_inc(h_set, 1)
                        if s == PT_SLOT:
                            act.wait_ge(pt_full, n1 + 1)
                            for j in range(2):
                                r = slice(64 * j, 64 * j + 64)
                                last = nc.scalar.activation(p_stack[r, j, :], m_ps16[r, 0:GT], ACT.Copy)
                            last.then_inc(p_stack_set, 1)
                    if st["fc1"] is not None and s >= FC1_SLOT:
                        gf, c = st["fc1"], s - FC1_SLOT
                        m, lo = c % MT, (c // MT) * HALF_T
                        act.wait_ge(fc1_full, CHUNKS * gf + c + 1)
                        wait(act, hid_set, CHUNKS * gf + c - 2)
                        wait(act, fc2_full, NT * gf)
                        src = f_ps[c % 2][:, 0:HALF_T]
                        nc.scalar.activation(gelu32[:, c % 3, :], src, ACT.Gelu, bias=b1[:, m:m + 1], scale=1.0 / WSCALE)
                        nc.scalar.activation(hid[:, 0, m, lo:lo + HALF_T], src, ACT.Gelu, bias=b1[:, m:m + 1],
                                             scale=1.0 / WSCALE).then_inc(gelu_set, 1)

            iterations(act, body)

            act.wait_ge(y_full, NQUAD * NG)
            for i, (ps, k, n0, nn) in enumerate(CT_PARTS):
                act.wait_ge(ct_full, i + 1)
                nc.scalar.activation(cx_t[0:EH, k, n0:n0 + nn, :],
                                     ps[0:EH, 0:nn * 128].rearrange("p (n b) -> p n b", n=nn), ACT.Copy).then_inc(ct_set, 1)
            act.wait_ge(cls_v, CLS_LG)
            nc.scalar.activation(pr[:, :, :], lg[:, :, :], ACT.Exp).then_inc(cls_exp, 1)
            act.wait_ge(fc2_full, NT * NG)
            for a in range(NATOM):
                n = 128 * len(ATOM_TOKENS[a])
                if a >= 2:
                    act.wait_ge(cand_full, CANDS_BEFORE[a - 1])
                for m in range(MT):
                    u = a * MT + m
                    act.wait_ge(ch_full, u + 1)
                    nc.scalar.activation(c_hid[a % 2][:, m, 0:n], f_ps[u % 2][:, 0:n], ACT.Gelu,
                                         bias=b_in[:, u:u + 1]).then_inc(ch_set, 1)

        @block.tensor
        def _(pe):
            def mm(o, lhs_t, rhs, start=True, stop=True):
                return nc.tensor.matmul(o, lhs_t, rhs, start=start, stop=stop)

            pe.wait_ge(const_in, 16 * CONSTS)
            pe.wait_ge(setup_v, 3)
            mm(g_ps[0:64, 0:EMB], spread[:, :], c_raw[:, :])
            mm(s_ps[0][:, 0:64], c_cen[:, 0:128], spread[:, :])
            mm(s_ps[0][0:64, 64:128], c_cen[:, 128:EMB], spread[:, :]).then_inc(setup_p, 1)
            pe.wait_ge(setup_v, 8)

            def head_t(o, col):
                mm(o, wa_raw[:, 0, col:col + HD], cct[:, 0, :], stop=False)
                mm(o, wa_raw[0:64, 1, col:col + HD], cct[0:64, 1, :], start=False, stop=False)
                return mm(o, b_attn[0:1, col:col + HD], bias_row[0:1, :], start=False)

            for h in range(HEADS):
                qb = (s_ps[1], 64 * h) if h < 8 else (k1_ps, 64 * (h - 8))
                kb = (k1_ps, 256 + 64 * h) if h < 4 else (y_ps, 64 * (h - 4))
                head_t(qb[0][0:HD, qb[1]:qb[1] + 64], h * HD)
                head_t(kb[0][0:HD, kb[1]:kb[1] + 64], EMB + h * HD)
            vo = f_ps[0][0:64, 0:EMB]
            mm(vo, cct[:, 0, :], wa_raw[:, 0, 2 * EMB:3 * EMB], stop=False)
            mm(vo, cct[0:64, 1, :], wa_raw[0:64, 1, 2 * EMB:3 * EMB], start=False, stop=False)
            mm(vo, bias_row[0:1, :], b_attn[0:1, 2 * EMB:3 * EMB], start=False).then_inc(setup_p, 1)
            pe.wait_ge(setup_v, 15)
            for h in range(HEADS):
                ab = (g_ps, 64 * h) if h < 8 else (s_ps[0], 64 * (h - 8))
                last = mm(ab[0][0:64, ab[1]:ab[1] + 64], mq_t[:, h, :], mk_t[:, h, :])
            last.then_inc(setup_p, 1)
            pe.wait_ge(ready_v, 1)

            emptied = {"v": (v_set, GI), "h2": (h2_set, NPAIR), "xt": (x_stack_set, 3), "ut": (u_stack_set, 1),
                       "h1": (h_set, NPAIR), "pt": (p_stack_set, 1)}

            def body(t, st, before):
                par = st["par"]
                g = st["attend"]
                uses = shared_uses(st)
                earlier = shared_uses(before)

                def wait_shared(i):
                    if i > 0:
                        _, what, k, stage = uses[i - 1]
                        grp = st[stage]
                    elif earlier:
                        _, what, k, stage = earlier[-1]
                        grp = before[stage]
                    else:
                        return
                    done, per = emptied[what]
                    pe.wait_ge(done, per * grp + k + 1)

                def g_product(s):
                    b, p = divmod(s, PAIRS)
                    wait(pe, g_split, SLOTS * g + s)
                    if s == 0:
                        pe.wait_ge(p_stack_set, g + 1)
                    mm(g_ps[:, 0:TOK], a_stack[:, p * 128:(p + 1) * 128],
                       p_stack[:, 0, b * TOK:(b + 1) * TOK]).then_inc(g_full, 1)

                def scores(s):
                    b = s // PAIRS
                    pe.wait_ge(g_split, SLOTS * g + s + 1)
                    wait(pe, relu0_set, SLOTS * g + s - 1)
                    for j in range(2):
                        mm(s_ps[s % 2][:, j * TOK:(j + 1) * TOK], p_stack[:, j, b * TOK:b * TOK + K0], g_stack[:, s % 2, :])
                    if s % 2 == 0:
                        wait(pe, relu1_set, NQUAD * g + s // 2)
                    for j in range(2):
                        c = (2 * (s % 2) + j) * K1
                        last = mm(k1_ps[0:K1, c:c + K1], p_stack[:, j, b * TOK + K0:(b + 1) * TOK],
                                  g_stack[:, s % 2, K0:TOK])
                    last.then_inc(scores_full, 1)

                def attend_v(gy, q):
                    b, qd = divmod(q, QUADS)
                    pe.wait_ge(relu0_set, SLOTS * gy + 2 * q + 2)
                    pe.wait_ge(relu1_set, NQUAD * gy + q + 1)
                    pe.wait_ge(v_set, GI * gy + b + 1)
                    wait(pe, y_lo_set, NQUAD * gy + q)
                    for j in range(4):
                        w = st0[:, (2 * q + j // 2) % 4, (j % 2) * TOK:(j % 2 + 1) * TOK]
                        mm(y_ps[32 * j:32 * j + 32, 0:TOK], v0[:, b % 2, 4 * qd + j, :], w, stop=False)
                    for j in range(4):
                        last = mm(y_ps[32 * j:32 * j + 32, K0:TOK], v1[:, b % 2, 4 * qd + j, :],
                                  st1[:, q % 2, j * K1:(j + 1) * K1], start=False)
                    last.then_inc(y_full, 1)

                def v_product(b):
                    mm(m_ps[:, 0:EMB], p_stack[:, 0, b * TOK:b * TOK + K0], mv_stack[:, :])
                    mm(m_ps[0:K1, EMB:2 * EMB], p_stack[:, 0, b * TOK + K0:(b + 1) * TOK],
                       mv_stack[:, :]).then_inc(v_full, 1)

                def y_rows(i):
                    pe.wait_ge(y_lo_set, NQUAD * (st["norm2"] + 1))
                    for j, k in enumerate(range(2 * i, min(2 * i + 2, NT))):
                        for qd in range(QUADS):
                            for part in range(2):
                                c = j * EMB + qd * 64
                                last = mm(m_ps[0:TP, c:c + 64], y_t[:, 1 - par, part, qd, k * TP:(k + 1) * TP],
                                          head_sel[:, :], start=part == 0, stop=part == 1)
                    last.then_inc(h2_full, 1)

                def x_columns(c):
                    pe.wait_ge(x_lo_set, st["norm2"] + 1)
                    flat = x_tok[:, :, :, :].rearrange("p k a e -> p k (a e)")
                    for k in range(NT):
                        last = nc.tensor.transpose(m_ps16[:, k * TP:(k + 1) * TP], flat[:, k, c * 128:(c + 1) * 128],
                                                   ident16[0:TP, 0:TP])
                    last.then_inc(xt_full, 1)

                def u_columns():
                    pe.wait_ge(u_tok_set, st["norm1"] + 1)
                    for k in range(NT):
                        last = nc.tensor.transpose(m_ps16[:, k * TP:(k + 1) * TP],
                                                   u_tok[:, k, :, :].rearrange("p a c -> p (a c)"), ident16[0:TP, 0:TP])
                    last.then_inc(ut_full, 1)

                def h_rows(i):
                    pe.wait_ge(u_stack_set, st["norm1"] + 1)
                    for j, k in enumerate(range(2 * i, min(2 * i + 2, NT))):
                        last = mm(m_ps[0:TP, j * EMB:(j + 1) * EMB], u_stack[:, k * TP:(k + 1) * TP], c_stack[:, :])
                    last.then_inc(h1_full, 1)

                def p_columns():
                    pe.wait_ge(p_tok_set, st["norm1"] + 1)
                    for k in range(NT):
                        last = nc.tensor.transpose(m_ps16[:, k * TP:(k + 1) * TP],
                                                   p_tok[:, k, :, :].rearrange("p a c -> p (a c)"), ident16[0:TP, 0:TP])
                    last.then_inc(pt_full, 1)

                def fc1(c):
                    gf = st["fc1"]
                    m, lo = c % MT, (c // MT) * HALF_T
                    pe.wait_ge(x_stack_set, 3 * (gf + 1))
                    if c >= 2:
                        pe.wait_ge(gelu_set, CHUNKS * gf + c - 1)
                    else:
                        wait(pe, o_set, NT * gf)
                    o = f_ps[c % 2][:, 0:HALF_T]
                    parts = [(w1_hi, 0), (w1_lo, 0), (w1_hi, 1), (w1_lo, 1), (w1_hi, 2)]
                    for i, (w, k) in enumerate(parts):
                        last = mm(o, w[:, k, m * 128:(m + 1) * 128], x_stack[:, k, lo:lo + HALF_T], start=i == 0,
                                  stop=i == len(parts) - 1)
                    last.then_inc(fc1_full, 1)

                def fc2(i):
                    gf = st["fc2"]
                    pe.wait_ge(hid_set, CHUNKS * (gf + 1))
                    if i >= 2:
                        pe.wait_ge(o_set, NT * gf + i - 1)
                    o = f_ps[i % 2][0:TP, 0:EMB]
                    mm(o, ones_pad[:, :], b2_stack[:, :], stop=False)
                    for m in range(MT):
                        for part, w in ((0, w2_hi), (0, w2_lo), (1, w2_hi)):
                            last = mm(o, hid[:, part, m, i * TP:(i + 1) * TP], w[:, m, :], start=False,
                                      stop=m == MT - 1 and part == 1)
                    last.then_inc(fc2_full, 1)

                shared = {"v": v_product, "h2": y_rows, "xt": x_columns, "ut": lambda i: u_columns(), "h1": h_rows,
                          "pt": lambda i: p_columns()}
                for s in range(SLOTS):
                    if s == 0 and st["last_av"] is not None:
                        attend_v(st["last_av"], NQUAD - 1)
                    if st["fc2"] is not None and s < NT:
                        fc2(s)
                    if g is not None:
                        if s == 0:
                            g_product(0)
                        if s + 1 < SLOTS and s > 0:
                            g_product(s + 1)
                        if s == 0:
                            g_product(1)
                        scores(s)
                    for i, (slot, what, k, _) in enumerate(uses):
                        if slot == s:
                            wait_shared(i)
                            shared[what](k)
                    if g is not None and s >= 2 and s % 2 == 0:
                        attend_v(g, s // 2 - 1)
                    if st["fc1"] is not None and s >= FC1_SLOT:
                        fc1(s - FC1_SLOT)

            iterations(pe, body)

            pe.wait_ge(cls_in, 32)
            pe.wait_ge(relu0_set, SLOTS * NG)
            pe.wait_ge(o_set, NT * NG)
            for ps, k, n0, nn in CT_PARTS:
                for j in range(nn):
                    last = nc.tensor.transpose(ps[0:EH, j * 128:(j + 1) * 128], cx[:, n0 + j, k * EH:(k + 1) * EH],
                                               ident32[:, :])
                last.then_inc(ct_full, 1)
            pe.wait_ge(ct_set, len(CT_PARTS))
            pe.wait_ge(cls_w_in, 16 * 5)

            def atom_hidden(a):
                toks = ATOM_TOKENS[a]
                n = 128 * len(toks)
                step = toks[1] - toks[0]
                for m in range(MT):
                    u = a * MT + m
                    if u >= 2:
                        pe.wait_ge(ch_set, u - 1)
                    for k in range(2):
                        last = mm(f_ps[u % 2][:, 0:n], a_in[:, k, a * HID + m * 128:a * HID + (m + 1) * 128],
                                  cx_t[0:EH, k, toks[0]:toks[-1] + 1:step, :], start=k == 0, stop=k == 1)
                    last.then_inc(ch_full, 1)

            def atom_candidates(a):
                pe.wait_ge(ch_set, (a + 1) * MT)
                for j, n in enumerate(ATOM_TOKENS[a]):
                    u = CANDS_BEFORE[a] + j
                    r = 0 if a < 3 else 1
                    if u >= 2:
                        pe.wait_ge(cand_tmp, u - 1)
                    for m in range(MT):
                        last = mm(s_ps[u % 2][:, 0:EMB], c_hid[a % 2][:, m, j * 128:(j + 1) * 128],
                                  a_out[:, m, DST[n][r] * EMB:(DST[n][r] + 1) * EMB], start=m == 0, stop=m == MT - 1)
                    last.then_inc(cand_full, 1)

            atom_hidden(0)
            for a in range(NATOM):
                if a + 1 < NATOM:
                    atom_hidden(a + 1)
                atom_candidates(a)

        @block.vector
        def _(dve):
            count = [0]

            def step(ins):
                count[0] += 1
                ins.then_inc(setup_v, 1)
                dve.wait_ge(setup_v, count[0])

            v = nc.vector
            dve.wait_ge(const_in, 16 * CONSTS)
            step(v.tensor_reduce(c_sum[:, 0:1], c_raw[:, :], AX.X, ALU.add))
            step(v.tensor_scalar(c_sum[:, 1:2], c_sum[:, 0:1], -1.0 / EMB, None, ALU.mult))
            step(v.tensor_scalar(c_cen[:, :], c_raw[:, :], c_sum[:, 1:2], None, ALU.add))
            dve.wait_ge(setup_p, 1)

            def split_rows(dst, src, tmp):
                step(v.tensor_copy(tmp, src))
                step(v.tensor_copy(dst[0:32, :], src[0:32, :]))
                step(v.tensor_tensor(dst[32:64, :], src[32:64, :], tmp[32:64, :], ALU.subtract))

            split_rows(c_stack[:, :], g_ps[0:64, 0:EMB], setup16[:, 0:EMB])
            step(v.tensor_copy(cct[:, 0, :], s_ps[0][:, 0:64]))
            step(v.tensor_copy(cct[0:64, 1, :], s_ps[0][0:64, 64:128]))
            dve.wait_ge(setup_p, 2)

            def heads_view(ps, c, n):
                return ps[0:HD, c:c + 64 * n].rearrange("p (h c) -> p h c", h=n)

            step(v.tensor_scalar(mq_t[:, 0:8, :], heads_view(s_ps[1], 0, 8), HD ** -0.5, None, ALU.mult))
            step(v.tensor_scalar(mq_t[:, 8:12, :], heads_view(k1_ps, 0, 4), HD ** -0.5, None, ALU.mult))
            step(v.tensor_copy(mk_t[:, 0:4, :], heads_view(k1_ps, 256, 4)))
            step(v.tensor_copy(mk_t[:, 4:12, :], heads_view(y_ps, 0, 8)))
            split_rows(mv_stack[:, :], f_ps[0][0:64, 0:EMB], setup16[:, 0:EMB])
            dve.wait_ge(setup_p, 3)
            split_rows(a_stack[:, 0:512], g_ps[0:64, :], setup16[:, 0:512])
            split_rows(a_stack[:, 512:768], s_ps[0][0:64, 0:256], setup16[:, 512:768])
            dve.wait_ge(wts_in, 16 * WEIGHTS)
            step(v.tensor_scalar(w1_hi[:, :, :], w1_raw[:, :, :], WSCALE, None, ALU.mult))
            step(v.scalar_tensor_tensor(w1_lo[:, 0, :], w1_raw[:, 0, :], WSCALE, w1_hi[:, 0, :], ALU.mult, ALU.subtract))
            step(v.scalar_tensor_tensor(w1_lo[0:64, 1, :], w1_raw[0:64, 1, :], WSCALE, w1_hi[0:64, 1, :],
                                        ALU.mult, ALU.subtract))
            step(v.memset(w1_lo[64:128, 1, :], 0.0))
            step(v.tensor_scalar(w2_hi[:, :, :], w2_raw[:, :, :], WSCALE, None, ALU.mult))
            step(v.scalar_tensor_tensor(w2_lo[:, :, :], w2_raw[:, :, :], WSCALE, w2_hi[:, :, :], ALU.mult, ALU.subtract))
            step(v.memset(b2_stack[:, :], 0.0))
            step(v.tensor_scalar(b2_stack[0:1, :], b2_raw[0:1, :], WSCALE, None, ALU.mult))
            step(v.tensor_scalar(b2_tmp[32:33, :], b2_raw[32:33, :], WSCALE, None, ALU.mult))
            step(v.scalar_tensor_tensor(b2_stack[32:33, :], b2_raw[32:33, :], WSCALE, b2_tmp[32:33, :],
                                        ALU.mult, ALU.subtract))
            step(v.memset(u_tok[:, :, :, :], 0.0))
            for stack in (c_stack, a_stack, mv_stack, p_stack[:, 0, :]):
                step(v.memset(stack[64:128, :], 0.0))
            step(v.memset(p_stack[0:64, 1, :], 0.0))
            step(v.memset(p_tok[:, :, :, :], 0.0))
            step(v.memset(p_tok[:, :, 0:8:2, NCH:NCH + 1], 1.0))
            step(v.memset(v0[:, :, :, :], 0.0))
            step(v.memset(v1[:, :, :, :], 0.0))
            step(v.memset(half_c[:, :], 0.5))
            step(v.memset(minus_half[:, :], -0.5))
            v.memset(xhat[:, 0:1], 0.0).then_inc(ready_v, 1)
            dve.wait_ge(ready_v, 1)

            def body(t, st, before):
                par = st["par"]
                g = st["attend"]

                def split_g(s):
                    dve.wait_ge(g_hi_set, SLOTS * g + s + 1)
                    wait(dve, scores_full, SLOTS * g + s - 1)
                    v.scalar_tensor_tensor(g_stack[:, s % 2, :], g_hi[:, s % 2, :], neg_lo[:, 0:1], g_ps[:, 0:TOK],
                                           ALU.mult, ALU.add).then_inc(g_split, 1)

                def relu_k0(s):
                    dve.wait_ge(scores_full, SLOTS * g + s + 1)
                    wait(dve, y_full, NQUAD * g + s // 2 - 1)
                    v.scalar_tensor_tensor(st0[:, s % 4, :], s_ps[s % 2][:, 0:2 * TOK], 0.0, mask_k0[:, :],
                                           ALU.max, ALU.mult).then_inc(relu0_set, 1)

                def relu_k1(q):
                    wait(dve, y_full, NQUAD * g + q - 1)
                    v.scalar_tensor_tensor(st1[:, q % 2, :], k1_ps[0:K1, 0:4 * K1], 0.0, mask_k1[:, :],
                                           ALU.max, ALU.mult).then_inc(relu1_set, 1)

                def y_low(gy, q, gpar):
                    dve.wait_ge(y_hi_set, NQUAD * gy + q + 1)
                    b = q // QUADS
                    c = slice(b * TOK, (b + 1) * TOK)
                    v.tensor_tensor(y_t[:, gpar, 1, q % QUADS, c], y_ps[:, 0:TOK], y_t[:, gpar, 0, q % QUADS, c],
                                    ALU.subtract).then_inc(y_lo_set, 1)

                def window_sums(gp, hk, gpar):
                    dve.wait_ge(x_halved, NHALF * gp + hk + 1)
                    w = x_ring[:, hk % RING, :].rearrange("p (c n) -> p c n", c=HCH)
                    c = (hk % 2) * HCH
                    v.tensor_reduce(pooled[:, gpar, hk // 2, c:c + HCH], w[:, :, 0:PIX // 2], AX.X,
                                    ALU.add).then_inc(x_pooled, 1)

                def variance(bn, tmp, var, part_set, sq_set, gn):
                    v.tensor_tensor(tmp[:, 0, :], bn[:, :, 1], bn[:, :, 4], ALU.subtract)
                    v.scalar_tensor_tensor(tmp[:, 1, :], bn[:, :, 2], EMB * EPS, bn[:, :, 5], ALU.add,
                                           ALU.add).then_inc(part_set, 1)
                    dve.wait_ge(part_set, gn + 1)
                    v.scalar_tensor_tensor(tmp[:, 2, :], tmp[:, 0, :], 0.25, tmp[:, 0, :], ALU.mult,
                                           ALU.mult).then_inc(sq_set, 1)
                    dve.wait_ge(sq_set, gn + 1)
                    return v.scalar_tensor_tensor(var[:, :], tmp[:, 1, :], 1.0 / EMB, tmp[:, 2, :], ALU.mult, ALU.add)

                def residual(i):
                    n2 = st["norm2"]
                    n = min(2, NT - 2 * i)
                    c = slice(2 * i * EMB, (2 * i + n) * EMB)
                    dve.wait_ge(h2_full, NPAIR * n2 + i + 1)
                    if i == 0:
                        dve.wait_ge(h_set, NPAIR * (n2 + 1))
                        wait(dve, cls_out, 32 * GI * (n2 - 1))
                        wait(dve, o_set, NT * (n2 - 1))
                    v.tensor_tensor(h2_tok[0:TP, 1 - par, c], m_ps[0:TP, 0:n * EMB], h_tok[0:TP, 1 - par, c],
                                    ALU.add).then_inc(h2_set, 1)
                    dve.wait_ge(h2_set, NPAIR * n2 + i + 1)
                    for k in range(2 * i, 2 * i + n):
                        last = v.bn_stats(bn2[:, k, :], h2_tok[0:TP, 1 - par, k * EMB:(k + 1) * EMB])
                    last.then_inc(bn2_set, 1)

                for s in range(SLOTS):
                    if s == 0 and st["last_av"] is not None:
                        y_low(st["last_av"], NQUAD - 1, 1 - par)
                    if g is not None:
                        if s == 0:
                            split_g(0)
                        if s + 1 < SLOTS:
                            split_g(s + 1)
                        relu_k0(s)
                        if s % 2 == 1:
                            relu_k1(s // 2)
                        elif s >= 2:
                            y_low(g, s // 2 - 1, par)
                    if st["fc2"] is not None and s < NT:
                        gf = st["fc2"]
                        dve.wait_ge(fc2_full, NT * gf + s + 1)
                        if s == 0:
                            wait(dve, out_done, 16 * gf)
                        c = slice(s * EMB, (s + 1) * EMB)
                        v.scalar_tensor_tensor(o_tok[0:TP, c], f_ps[s % 2][0:TP, 0:EMB], 1.0 / WSCALE,
                                               h2_tok[0:TP, par, c], ALU.mult, ALU.add).then_inc(o_set, 1)
                    if st["norm2"] is not None:
                        n2 = st["norm2"]
                        if 0 <= s - H2_SLOT < NPAIR:
                            residual(s - H2_SLOT)
                        if s == 5:
                            dve.wait_ge(bn2_set, NPAIR * (n2 + 1))
                            v.tensor_tensor(sum2[:, :], bn2[:, :, 1], bn2[:, :, 4], ALU.add)
                            variance(bn2, st2s, var2, part2_set, sq2_set, n2).then_inc(var2_set, 1)
                            v.tensor_scalar(mean2[:, :], sum2[:, :], 0.5, None, ALU.mult).then_inc(mean2_set, 1)
                        if s == 6:
                            dve.wait_ge(rstd2_set, n2 + 1)
                            dve.wait_ge(mean2_set, n2 + 1)
                            wait(dve, cls_out, 32 * GI * n2)
                            wait(dve, x_lo_set, n2)
                            for k in range(NT):
                                c = slice(k * EMB, (k + 1) * EMB)
                                last = v.tensor_scalar(xhat[0:TP, c], h2_tok[0:TP, 1 - par, c], mean2[:, k:k + 1],
                                                       rstd2[:, k:k + 1], ALU.subtract, ALU.mult)
                            last.then_inc(xhat_set, 1)
                    if st["pool_cur"] is not None and s in POOL_CUR:
                        window_sums(st["pool_cur"], POOL_CUR[s], 1 - par)
                    if st["pool_next"] is not None and s in POOL_NEXT:
                        window_sums(st["pool_next"], POOL_NEXT[s], par)
                    if st["norm1"] is not None:
                        n1 = st["norm1"]
                        if s == 11:
                            sums = pooled[:, 1 - par, :, :].unsqueeze(2).broadcast_to([TP, NT, 2, NCH])
                            dve.wait_ge(x_pooled, NHALF * (n1 + 1))
                            wait(dve, ut_full, n1)
                            v.tensor_copy(u_tok[:, :, 0:4:2, 0:NCH], sums).then_inc(u_hi_set, 1)
                            dve.wait_ge(u_hi_set, n1 + 1)
                            v.tensor_tensor(u_tok[:, :, 1:4:2, 0:NCH], sums,
                                            u_tok[:, :, 0:1, 0:NCH].broadcast_to([TP, NT, 2, NCH]),
                                            ALU.subtract).then_inc(u_tok_set, 1)
                        if 0 <= s - H1_SLOT - 1 < NPAIR:
                            i = s - H1_SLOT - 1
                            dve.wait_ge(h_set, NPAIR * n1 + i + 1)
                            for k in range(2 * i, min(2 * i + 2, NT)):
                                last = v.bn_stats(bn1[:, k, :], h_tok[0:TP, 1 - par, k * EMB:(k + 1) * EMB])
                            last.then_inc(bn1_set, 1)
                        if s == 19:
                            dve.wait_ge(bn1_set, NPAIR * (n1 + 1))
                            variance(bn1, st1s, var1, part1_set, sq1_set, n1).then_inc(var1_set, 1)
                        if s == 21:
                            dve.wait_ge(rstd1_set, n1 + 1)
                            v.tensor_tensor(pn[:, :, :], pooled[:, 1 - par, :, :],
                                            rstd1[:, :].unsqueeze(2).broadcast_to([TP, NT, NCH]),
                                            ALU.mult).then_inc(pn_set, 1)
                            p4 = pn[:, :, :].unsqueeze(2).broadcast_to([TP, NT, 4, NCH])
                            dve.wait_ge(pn_set, n1 + 1)
                            wait(dve, pt_full, n1)
                            v.tensor_copy(p_tok[:, :, 0:8:2, 0:NCH], p4).then_inc(p_hi_set, 1)
                            dve.wait_ge(p_hi_set, n1 + 1)
                            v.tensor_tensor(p_tok[:, :, 1:8:2, 0:NCH], p4,
                                            p_tok[:, :, 0:1, 0:NCH].broadcast_to([TP, NT, 4, NCH]),
                                            ALU.subtract).then_inc(p_tok_set, 1)

            iterations(dve, body)

            done = [0]

            def link(ins):
                done[0] += 1
                ins.then_inc(cls_v, 1)
                dve.wait_ge(cls_v, done[0])

            dve.wait_ge(cls_in, 32)
            dve.wait_ge(cls_w_in, 16 * 5)
            dve.wait_ge(h2_full, NPAIR * NG)
            link(v.tensor_tensor(gate_tmp[:, 0:NCLS, :], cx, cx, ALU.mult))
            link(v.tensor_reduce(ss[:, 0:NCLS], gate_tmp[:, 0:NCLS, :], AX.X, ALU.add))
            link(v.tensor_tensor(gate_tmp, gate_w, gate_w, ALU.mult))
            link(v.tensor_reduce(ss[:, NCLS:3 * NCLS], gate_tmp, AX.X, ALU.add))
            assert done[0] == CLS_SS
            by_route = gate_tmp.rearrange("p (n r) e -> p n r e", r=2)
            link(v.tensor_tensor(by_route, cx.unsqueeze(2).broadcast_to([128, NCLS, 2, EMB]),
                                 gate_w.rearrange("p (n r) e -> p n r e", r=2), ALU.mult))
            link(v.tensor_reduce(lg[:, :, :].rearrange("p n r -> p (n r)"), gate_tmp, AX.X, ALU.add))
            dve.wait_ge(cls_pow, 1)
            link(v.tensor_scalar(nrm[:, :], nrm[:, :], 1e-12, None, ALU.max))
            link(v.reciprocal(nrm[:, :], nrm[:, :]))
            flat = lg[:, :, :].rearrange("p n r -> p (n r)")
            link(v.tensor_tensor(flat, flat, nrm[:, NCLS:3 * NCLS], ALU.mult))
            link(v.tensor_tensor(lg[:, :, :], lg[:, :, :], nrm[:, 0:NCLS].unsqueeze(2).broadcast_to([128, NCLS, 2]), ALU.mult))
            link(v.tensor_tensor(flat, flat, bal[:, :], ALU.add))
            link(v.tensor_tensor(gs[:, 0, :], lg[:, :, 0], lg[:, :, 1], ALU.max))
            link(v.tensor_tensor(lg[:, :, :], lg[:, :, :], gs[:, 0, :].unsqueeze(2).broadcast_to([128, NCLS, 2]), ALU.subtract))
            assert done[0] == CLS_LG
            dve.wait_ge(cls_exp, 1)
            link(v.tensor_tensor(gs[:, 1, :], pr[:, :, 0], pr[:, :, 1], ALU.add))
            link(v.reciprocal(gs[:, 2, :], gs[:, 1, :]))
            link(v.tensor_tensor(pr[:, :, :], pr[:, :, :], gs[:, 2, :].unsqueeze(2).broadcast_to([128, NCLS, 2]), ALU.mult))
            link(v.tensor_tensor(gs[:, 3, :], pr[:, :, 1], pr[:, :, 0], ALU.is_gt))
            link(v.tensor_scalar(gs[:, 4, :], gs[:, 3, :], -1.0, 1.0, ALU.mult, ALU.add))
            link(v.tensor_tensor(wgt[:, :, 1], pr[:, :, 1], gs[:, 3, :], ALU.mult))
            link(v.tensor_tensor(wgt[:, :, 0], pr[:, :, 0], gs[:, 4, :], ALU.mult))
            dve.wait_ge(out_done, 16 * NG)
            dve.wait_ge(x_lo_set, NG)
            dve.wait_ge(cls_out, 32 * GI * NG)
            for a in range(NATOM):
                r = 0 if a < 3 else 1
                for j, n in enumerate(ATOM_TOKENS[a]):
                    u = CANDS_BEFORE[a] + j
                    dve.wait_ge(cand_full, u + 1)
                    wait(dve, cand_set, u)
                    v.tensor_tensor(c_tmp[:, u % 2, :], s_ps[u % 2][:, 0:EMB], b_out[:, DST[n][r], :],
                                    ALU.add).then_inc(cand_tmp, 1)
                    dve.wait_ge(cand_tmp, u + 1)
                    base = ch[:, n, :] if r == 0 else c_acc[:, n, :]
                    v.scalar_tensor_tensor(c_acc[:, n, :], c_tmp[:, u % 2, :], wgt[:, n, r:r + 1], base,
                                           ALU.mult, ALU.add).then_inc(cand_set, 1)


def kernel(x, L0_tok_channel_weights, L0_attn_W_attn, L0_attn_b_attn, L0_ffn_fc1_w, L0_ffn_fc1_b, L0_ffn_fc2_w,
           L0_ffn_fc2_b, L0_ffn_gate_pair, L0_ffn_atom_in_w, L0_ffn_atom_in_b, L0_ffn_atom_out_w, L0_ffn_atom_out_b,
           L0_ffn_balance_bias):
    import concourse.bacc as bacc
    from concourse.bass_utils import run_bass_kernel_spmd

    def lay(a):
        return np.ascontiguousarray(a)

    f = np.float32
    rows = np.arange(128)
    head_sel = np.zeros((128, 64), np.float16)
    for j in range(4):
        for k in range(HD):
            head_sel[32 * j + k, HD * j + k] = 1
    causal = (np.arange(TOK)[None, :] >= rows[:, None]).astype(f)
    causal1 = (np.arange(K1)[None, :] >= np.arange(K1)[:, None]).astype(f)
    spread = np.zeros((NCH, 64), f)
    bias_row = np.zeros((1, 64), f)
    for part in range(4):
        for c in range(NCH):
            spread[c, 16 * part + c] = 1
        bias_row[0, 16 * part + NCH] = 1
    ones_pad = np.zeros((128, TP), np.float16)
    ones_pad[0] = ones_pad[32] = 1
    arrays = {
        "ident16": np.eye(128, dtype=np.float16), "ident32": np.eye(128, dtype=f), "head_sel": head_sel,
        "mask_k0": np.concatenate([causal, causal], 1), "mask_k1": np.concatenate([causal1] * 4, 1),
        "neg_lo": -((rows // 32) % 2).astype(f)[:, None], "spread": spread, "bias_row": bias_row, "ones_pad": ones_pad,
        "x": lay(np.asarray(x).reshape(NIMG, NCH, SIDE, PATCH, SIDE, PATCH).transpose(0, 2, 4, 1, 3, 5)).reshape(
            NIMG * TOK, ROW),
        "cw": lay(L0_tok_channel_weights),
        "wa_t": lay(np.asarray(L0_attn_W_attn).T), "b_attn": lay(np.asarray(L0_attn_b_attn).reshape(1, 3 * EMB)),
        "w1_t": lay(np.asarray(L0_ffn_fc1_w).T), "w2_t": lay(np.asarray(L0_ffn_fc2_w).T),
        "b1": lay(np.asarray(L0_ffn_fc1_b).reshape(MT, 128).T), "b2": lay(np.asarray(L0_ffn_fc2_b).reshape(1, EMB)),
        "gate": lay(np.asarray(L0_ffn_gate_pair).reshape(-1)),
        "a_in_t": lay(np.asarray(L0_ffn_atom_in_w).reshape(NATOM * HID, EMB).T),
        "b_in": lay(np.asarray(L0_ffn_atom_in_b).reshape(NATOM * MT, 128).T),
        "a_out_t": lay(np.asarray(L0_ffn_atom_out_w).transpose(2, 0, 1)).reshape(HID, NATOM * EMB),
        "b_out": lay(np.asarray(L0_ffn_atom_out_b).reshape(-1)),
        "bal": lay(np.asarray(L0_ffn_balance_bias).reshape(-1)),
    }
    nc = bacc.Bacc("TRN2", target_bir_lowering=False, num_devices=1)
    d = {n: nc.dram_tensor("in_" + n, a.shape, mybir.dt.from_np(a.dtype), kind="ExternalInput").ap() for n, a in arrays.items()}
    out = nc.dram_tensor("out", (NIMG * TOK, EMB), F32, kind="ExternalOutput").ap()
    cls_x = nc.dram_tensor("cls_x", (NIMG * NCLS, EMB), F32, kind="Internal").ap()
    cls_h = nc.dram_tensor("cls_h", (NIMG * NCLS, EMB), F32, kind="Internal").ap()
    vit_tower_kernel(nc, d, out, cls_x, cls_h)
    r = run_bass_kernel_spmd(nc, [{"in_" + n: a for n, a in arrays.items()}], core_ids=[0])
    return r.results[0]["out"].reshape(NIMG, TOK, EMB)
```

```python
from contextlib import ExitStack

import numpy as np

import concourse.bass as bass
from concourse import mybir

F32 = mybir.dt.float32
F16 = mybir.dt.float16
BF16 = mybir.dt.bfloat16
ACT = mybir.ActivationFunctionType
ALU = mybir.AluOpType
AX = mybir.AxisListType

NIMG, NCH, SIDE, PATCH = 128, 12, 14, 16
TOK = SIDE * SIDE
PIX = PATCH * PATCH
EMB = 192
HEADS, HD = 12, 16
HID = 768
NCLS, NATOM = 6, 5
EPS = 1e-5

GI = 4
GT = GI * TOK
TP = 112
NT = GT // TP
NG = NIMG // GI
NHALF = 2 * NT
HCH = NCH // 2
RING = 7
ROW = NCH * PIX
K0, K1 = 128, TOK - 128
PAIRS = HEADS // 2
QUADS = HEADS // 4
SLOTS = GI * PAIRS
NQUAD = GI * QUADS
MT = HID // 128
EH = EMB // 2
HALF_T = GT // 2
CHUNKS = 2 * MT
WSCALE = 64.0

POOL_CUR = {0: 7, 1: 8, 3: 9, 4: 10, 5: 11, 6: 12, 7: 13}
POOL_NEXT = {10: 0, 12: 1, 14: 2, 16: 3, 18: 4, 20: 5, 22: 6}
SUM_CUR = {s + 1: hk for s, hk in POOL_CUR.items()}
SUM_NEXT = {s + 1: hk for s, hk in POOL_NEXT.items()}
NPAIR = (NT + 1) // 2
H2_SLOT = 1
STAT2_SLOT, XHAT_SLOT, X_HI_SLOT, X_LO_SLOT = 5, 7, 7, 8
XT_SLOTS = (9, 10, 11)
U_SLOT, UT_SLOT, H1_SLOT = 9, 10, 12
STAT1_SLOT, PN_SLOT, PT_SLOT = 17, 19, 20
FC2_SLOTS = (1, 3, 4, 6, 7, 9, 11)
FC1_SLOT = 12
AHEAD = 2
ACT_RELU = (2, 4, 6, 8, 10)
NR_A, NR_V = len(ACT_RELU), SLOTS - len(ACT_RELU)
BIG = 2.0 ** 60

SRC = [[n // 2, 3 + n % 2] for n in range(NCLS)]
DST = [[3 + n % 2, n // 2] for n in range(NCLS)]


def stages(t, python_t):
    def there(d):
        return 0 <= python_t + d < NG
    return {
        "pool_next": t + 2 if there(2) else None,
        "pool_cur": t + 1 if there(1) else None,
        "norm1": t + 1 if there(1) else None,
        "attend": t if there(0) else None,
        "last_av": t - 1 if there(-1) else None,
        "norm2": t - 1 if there(-1) else None,
        "fc1": t - 1 if there(-1) else None,
        "fc2": t - 2 if there(-2) else None,
        "par": python_t % 2,
    }


ATOM_TOKENS = [[0, 1], [2, 3], [4, 5], [0, 2, 4], [1, 3, 5]]
CANDS_BEFORE = [0, 2, 4, 6, 9, 12]
CLS_SS, CLS_LG = 4, 13


def shared_uses(st):
    uses = []
    for s in range(SLOTS):
        if st["attend"] is not None and s % PAIRS == 0:
            uses.append((s, "v", s // PAIRS, "attend"))
        if st["norm2"] is not None and 0 <= s - H2_SLOT < NPAIR:
            uses.append((s, "h2", s - H2_SLOT, "norm2"))
        if st["norm2"] is not None and s in XT_SLOTS:
            uses.append((s, "xt", XT_SLOTS.index(s), "norm2"))
        if st["norm1"] is not None and s == UT_SLOT:
            uses.append((s, "ut", 0, "norm1"))
        if st["norm1"] is not None and 0 <= s - H1_SLOT < NPAIR:
            uses.append((s, "h1", s - H1_SLOT, "norm1"))
        if st["norm1"] is not None and s == PT_SLOT:
            uses.append((s, "pt", 0, "norm1"))
    return uses


FIRST_T, LAST_T = -2, NG + 1
LOOP_T0, LOOP_T1 = 2, NG - 2


def iterations(eng, body):
    for t in range(FIRST_T, LOOP_T0):
        body(t, stages(t, t), stages(t - 1, t - 1))
    with eng.Fori(0, (LOOP_T1 - LOOP_T0) // 2) as turn:
        for half in range(2):
            t = turn * 2 + LOOP_T0
            body(t + half, stages(t + half, LOOP_T0 + half), stages(t + (half - 1), LOOP_T0 + half - 1))
    for t in range(LOOP_T1, LAST_T + 1):
        body(t, stages(t, t), stages(t - 1, t - 1))


def by_act(n):
    return sum(s < n for s in ACT_RELU)


def gelu_chunks(st, s):
    if s == 0:
        return None if st["fc2"] is None else (st["fc2"], CHUNKS - 1)
    if st["fc1"] is not None and s > FC1_SLOT:
        return st["fc1"], s - 1 - FC1_SLOT
    return None


def wait(eng, sem, value):
    if not (isinstance(value, int) and value <= 0):
        eng.wait_ge(sem, value)


def vit_tower_kernel(nc, d, out, cls_x, cls_h):
    with ExitStack() as ctx:
        def sb(name, shape, dt):
            return ctx.enter_context(nc.sbuf_tensor(name, shape, dt))

        def bank(name):
            return ctx.enter_context(nc.psum_tensor(name, [128, 512], F32))

        def sem(name):
            return ctx.enter_context(nc.semaphore(name))

        g_ps = bank("g_ps")
        s_ps = [bank("s_ps0"), bank("s_ps1")]
        k1_ps = bank("k1_ps")
        y_ps = bank("y_ps")
        f_ps = [bank("f_ps0"), bank("f_ps1")]
        m_ps = bank("m_ps")
        m_ps16 = m_ps[:, :].bitcast(F16)

        ident16 = sb("ident16", [128, 128], F16)
        ident32 = sb("ident32", [128, 128], F32)
        head_sel = sb("head_sel", [128, 64], F16)
        mask_k0 = sb("mask_k0", [128, 2 * TOK], F32)
        mask_big = sb("mask_big", [128, 128], BF16)
        ident_big = sb("ident_big", [128, 128], BF16)
        neg_lo = sb("neg_lo", [128, 1], F32)
        spread = sb("spread", [NCH, 64], F32)
        bias_row = sb("bias_row", [1, 64], F32)
        ones_pad = sb("ones_pad", [128, TP], F16)
        minus_half = sb("minus_half", [128, NT], F32)

        c_raw = sb("c_raw", [NCH, EMB], F32)
        c_cen = sb("c_cen", [NCH, EMB], F32)
        c_sum = sb("c_sum", [NCH, 2], F32)
        c_stack = sb("c_stack", [128, EMB], F16)
        cct = sb("cct", [128, 2, 64], F32)
        b_attn = sb("b_attn", [1, 3 * EMB], F32)
        mq_t = sb("mq_t", [HD, HEADS, 64], F32)
        mk_t = sb("mk_t", [HD, HEADS, 64], F32)
        a_stack = sb("a_stack", [128, HEADS * 64], F16)
        mv_stack = sb("mv_stack", [128, EMB], F16)
        setup16 = sb("setup16", [64, HEADS * 64], F16)
        w1_hi = sb("w1_hi", [128, 3, HID], F16)
        w1_lo = sb("w1_lo", [128, 2, HID], F16)
        w2_hi = sb("w2_hi", [128, MT, EMB], F16)
        w2_lo = sb("w2_lo", [128, MT, EMB], F16)
        b1 = sb("b1", [128, MT], F32)
        b2_raw = sb("b2_raw", [64, EMB], F32)
        b2_stack = sb("b2_stack", [128, EMB], F16)
        b2_tmp = sb("b2_tmp", [64, EMB], F16)

        x_ring = sb("x_ring", [128, RING, HCH * PIX], F32)
        pooled = sb("pooled", [TP, 2, NT, NCH], F32)
        u_tok = sb("u_tok", [TP, NT, 8, 16], F16)
        u_stack = sb("u_stack", [128, GT], F16)
        h_tok = sb("h_tok", [128, 2, NT * EMB], F32)
        bn1 = sb("bn1", [TP, NT, 6], F32)
        st1s = sb("st1s", [TP, 3, NT], F32)
        var1 = sb("var1", [TP, NT], F32)
        rstd1 = sb("rstd1", [TP, NT], F32)
        pn = sb("pn", [TP, NT, NCH], F32)
        p_tok = sb("p_tok", [TP, NT, 8, 16], F16)
        p_stack = sb("p_stack", [128, 2, 2, GT], F16)
        g_hi = sb("g_hi", [128, 2, TOK], F16)
        g_stack = sb("g_stack", [128, 3, TOK], F16)
        st0 = sb("st0", [128, 4, 2 * TOK], F32)
        st1 = sb("st1", [K1, 2, 4 * K1], F32)
        v0 = sb("v0", [128, 2, HEADS, 32], F32)
        v1 = sb("v1", [K1, 2, HEADS, 32], F32)
        y_t = sb("y_t", [128, 2, 2, QUADS, GT], F16)
        h2_tok = sb("h2_tok", [128, 2, NT * EMB], F32)
        bn2 = sb("bn2", [TP, NT, 6], F32)
        st2s = sb("st2s", [TP, 3, NT], F32)
        sum2 = sb("sum2", [TP, NT], F32)
        mean2 = sb("mean2", [TP, NT], F32)
        var2 = sb("var2", [TP, NT], F32)
        rstd2 = sb("rstd2", [TP, NT], F32)
        xhat = sb("xhat", [128, NT * EMB], F32)
        x_tok = sb("x_tok", [TP, NT, 2, EMB], F16)
        x_stack = sb("x_stack", [128, 3, GT], F16)
        gelu32 = sb("gelu32", [128, 3, HALF_T], F32)
        hid = sb("hid", [128, 2, MT, GT], F16)
        o_tok = sb("o_tok", [128, NT * EMB], F32)

        hid32 = hid[:, :, :, :].rearrange("p a m t -> p (a m t)").bitcast(F32)
        w1_raw = hid32[:, 0:3 * HID].rearrange("p (k n) -> p k n", k=3)
        w2_raw = hid32[:, 3 * HID:3 * HID + MT * EMB].rearrange("p (m n) -> p m n", m=MT)
        wa_raw = hid32[:, 3 * HID + MT * EMB:3 * HID + MT * EMB + 2 * 3 * EMB].rearrange("p (k n) -> p k n", k=2)

        x_flat = x_ring[:, :, :].rearrange("p r n -> p (r n)")
        a_in = x_flat[0:EH, 0:2 * NATOM * HID].rearrange("p (k n) -> p k n", k=2)
        a_out_late = x_flat[:, 2 * NATOM * HID:2 * NATOM * HID + MT // 2 * NATOM * EMB].rearrange("p (m n) -> p m n", m=MT // 2)
        a_out_early = sb("a_out_early", [128, MT // 2, NATOM * EMB], F32)
        cx = h_tok[:, 0, 0:NCLS * EMB].rearrange("p (n e) -> p n e", n=NCLS)
        ch = h_tok[:, 1, 0:NCLS * EMB].rearrange("p (n e) -> p n e", n=NCLS)
        y32 = y_t[:, :, :, :, :].rearrange("p a b q t -> p (a b q t)").bitcast(F32)
        gate_w = y32[:, 0:2 * NCLS * EMB].rearrange("p (n e) -> p n e", n=2 * NCLS)
        gate_tmp = y32[:, 2 * NCLS * EMB:4 * NCLS * EMB].rearrange("p (n e) -> p n e", n=2 * NCLS)
        b_out = h2_tok[:, 0, 0:NATOM * EMB].rearrange("p (a e) -> p a e", a=NATOM)
        cx_t = st0[:, :, :].rearrange("p a b -> p (a b)")[:, 0:2 * NCLS * 128].rearrange("p (k n b) -> p k n b", k=2, n=NCLS)
        c_hid = [hid32[:, i * MT * 3 * 128:(i + 1) * MT * 3 * 128].rearrange("p (m n) -> p m n", m=MT) for i in range(2)]
        c_acc = o_tok[:, 0:NCLS * EMB].rearrange("p (n e) -> p n e", n=NCLS)
        c_tmp = xhat[:, 0:2 * EMB].rearrange("p (n e) -> p n e", n=2)
        b_in = sb("b_in", [128, NATOM * MT], F32)
        bal = sb("bal", [128, 2 * NCLS], F32)
        ss = sb("ss", [128, 3 * NCLS], F32)
        nrm = sb("nrm", [128, 3 * NCLS], F32)
        half_c = sb("half_c", [128, 3 * NCLS], F32)
        lg = sb("lg", [128, NCLS, 2], F32)
        pr = sb("pr", [128, NCLS, 2], F32)
        gs = sb("gs", [128, 6, NCLS], F32)
        wgt = sb("wgt", [128, NCLS, 2], F32)

        const_in = sem("const_in")
        wts_in = sem("wts_in")
        const_set = sem("const_set")
        setup_v = sem("setup_v")
        setup_p = sem("setup_p")
        ready_v = sem("ready_v")
        x_in = [sem(f"x_in{i}") for i in range(RING)]
        x_halved = sem("x_halved")
        x_pooled = sem("x_pooled")
        v_full = sem("v_full")
        h2_full = sem("h2_full")
        xt_full = sem("xt_full")
        ut_full = sem("ut_full")
        h1_full = sem("h1_full")
        pt_full = sem("pt_full")
        u_hi_set = sem("u_hi_set")
        u_tok_set = sem("u_tok_set")
        u_stack_set = sem("u_stack_set")
        h_set = sem("h_set")
        bn1_set = sem("bn1_set")
        part1_set = sem("part1_set")
        sq1_set = sem("sq1_set")
        sq2_set = sem("sq2_set")
        var1_set = sem("var1_set")
        rstd1_set = sem("rstd1_set")
        pn_set = sem("pn_set")
        p_hi_set = sem("p_hi_set")
        p_tok_set = sem("p_tok_set")
        p_stack_set = sem("p_stack_set")
        g_full = sem("g_full")
        g_hi_set = sem("g_hi_set")
        g_split = sem("g_split")
        scores_full = sem("scores_full")
        k1_full = sem("k1_full")
        relu0_v = sem("relu0_v")
        relu0_a = sem("relu0_a")
        relu1_set = sem("relu1_set")
        v_set = sem("v_set")
        y_full = sem("y_full")
        y_hi_set = sem("y_hi_set")
        y_lo_set = sem("y_lo_set")
        h2_set = sem("h2_set")
        bn2_set = sem("bn2_set")
        part2_set = sem("part2_set")
        var2_set = sem("var2_set")
        mean2_set = sem("mean2_set")
        rstd2_set = sem("rstd2_set")
        xhat_set = sem("xhat_set")
        x_hi_set = sem("x_hi_set")
        x_lo_set = sem("x_lo_set")
        x_stack_set = sem("x_stack_set")
        fc1_full = sem("fc1_full")
        gelu_set = sem("gelu_set")
        hid_set = sem("hid_set")
        fc2_full = sem("fc2_full")
        o_set = sem("o_set")
        out_done = sem("out_done")
        cls_out = sem("cls_out")
        cls_w_in = sem("cls_w_in")
        cls_in = sem("cls_in")
        cls_v = sem("cls_v")
        cls_pow = sem("cls_pow")
        cls_exp = sem("cls_exp")
        ct_full = sem("ct_full")
        ct_set = sem("ct_set")
        ch_full = sem("ch_full")
        ch_set = sem("ch_set")
        cand_full = sem("cand_full")
        cand_tmp = sem("cand_tmp")
        cand_set = sem("cand_set")
        cls_done = sem("cls_done")

        CT_PARTS = [(s_ps[0], 0, 0, 4), (s_ps[1], 0, 4, 2), (f_ps[0], 1, 0, 4), (f_ps[1], 1, 4, 2)]
        CONSTS = 11
        WEIGHTS = 11

        def ring_reuse(g, hk):
            return NHALF * g + (hk - RING) + 1

        block = ctx.enter_context(nc.Block())

        @block.sync
        def _(sp):
            for dst, src in ((c_raw[:, :], d["cw"]), (spread[:, :], d["spread"]), (bias_row[:, :], d["bias_row"]),
                             (b_attn[:, :], d["b_attn"]), (wa_raw[:, 0, :], d["wa_t"][0:128, :]),
                             (wa_raw[0:64, 1, :], d["wa_t"][128:EMB, :]), (ident16[:, :], d["ident16"]),
                             (ident32[:, :], d["ident32"]), (head_sel[:, :], d["head_sel"]),
                             (mask_k0[:, :], d["mask_k0"]),
                             (neg_lo[:, :], d["neg_lo"])):
                sp.dma_start(dst, src).then_inc(const_in, 16)

            def load_x(g, hk):
                wait(sp, x_pooled, ring_reuse(g, hk))
                src = d["x"][bass.ds(g * GT + (hk // 2) * TP, TP), (hk % 2) * HCH * PIX:(hk % 2 + 1) * HCH * PIX]
                sp.dma_start(x_ring[0:TP, hk % RING, :], src).then_inc(x_in[hk % RING], 16)

            for hk in range(3):
                load_x(0, hk)
            for dst, src in ((w1_raw[:, 0, :], d["w1_t"][0:128, :]), (w1_raw[0:64, 1, :], d["w1_t"][128:EMB, :]),
                             (w1_raw[64:128, 1, :], d["w1_t"][0:64, :]), (w1_raw[:, 2, :], d["w1_t"][64:EMB, :]),
                             (w2_raw[:, :, :], d["w2_t"].rearrange("(m p) n -> p m n", p=128)),
                             (b1[:, :], d["b1"]), (b2_raw[0:1, :], d["b2"]), (b2_raw[32:33, :], d["b2"]),
                             (ones_pad[:, :], d["ones_pad"]),
                             (a_out_early[:, :, :], d["a_out_t"][0:HID // 2, :].rearrange("(m p) n -> p m n", p=128)),
                             (b_in[:, :], d["b_in"])):
                sp.dma_start(dst, src).then_inc(wts_in, 16)
            for hk in range(3, RING):
                load_x(0, hk)

            def body(t, st, before):
                par = st["par"]
                for s in range(SLOTS):
                    for stage, table in (("pool_cur", SUM_CUR), ("pool_next", SUM_NEXT)):
                        if st[stage] is not None and s in table:
                            g, hk = st[stage], table[s]
                            if hk + RING < NHALF:
                                load_x(g, hk + RING)
                            elif stage == "pool_next" or st["pool_next"] is not None:
                                load_x(g + 1, hk + RING - NHALF)
                    if s == FC2_SLOTS[-1] + 1 and st["fc2"] is not None:
                        g = st["fc2"]
                        sp.wait_ge(o_set, NT * g + NT)
                        sp.dma_start(out[bass.ds(g * GT, GT), :].rearrange("(k p) e -> p k e", p=TP),
                                     o_tok[0:TP, :].rearrange("p (k e) -> p k e", k=NT)).then_inc(out_done, 16)
                    if s == XHAT_SLOT + 1 and st["norm2"] is not None:
                        g = st["norm2"]
                        sp.wait_ge(xhat_set, g + 1)
                        for b in range(GI):
                            k, r = divmod(b * TOK, TP)
                            for buf, dst in ((xhat[:, :], cls_x), (h2_tok[:, (par + 1) % 2, :], cls_h)):
                                sp.dma_start(dst[bass.ds((g * GI + b) * NCLS, NCLS), :],
                                             buf[r:r + NCLS, k * EMB:(k + 1) * EMB]).then_inc(cls_out, 16)

            iterations(sp, body)

            sp.wait_ge(x_pooled, NHALF * NG)
            sp.dma_start(a_in[:, 0, :], d["a_in_t"][0:EH, :]).then_inc(cls_w_in, 16)
            sp.dma_start(a_in[:, 1, :], d["a_in_t"][EH:EMB, :]).then_inc(cls_w_in, 16)
            sp.dma_start(a_out_late, d["a_out_t"][HID // 2:HID, :].rearrange("(m p) n -> p m n", p=128)).then_inc(cls_w_in, 16)
            sp.wait_ge(h2_set, NPAIR * NG)
            sp.dma_start(gate_w, d["gate"].partition_broadcast(128).rearrange("p (n e) -> p n e", e=EMB)).then_inc(cls_w_in, 16)
            sp.dma_start(bal[:, :], d["bal"].partition_broadcast(128)).then_inc(cls_w_in, 16)
            sp.wait_ge(cls_out, 16 * 2 * GI * NG)
            sp.dma_start(cx, cls_x.rearrange("(b n) e -> b n e", n=NCLS)).then_inc(cls_in, 16)
            sp.dma_start(ch, cls_h.rearrange("(b n) e -> b n e", n=NCLS)).then_inc(cls_in, 16)
            sp.wait_ge(o_set, NT * NG)
            sp.dma_start(b_out, d["b_out"].partition_broadcast(128).rearrange("p (a e) -> p a e", e=EMB)).then_inc(cls_w_in, 16)
            sp.wait_ge(out_done, 16 * NG)
            sp.wait_ge(cand_set, 2 * NCLS)
            sp.dma_start(out.rearrange("(b t) e -> b t e", t=TOK)[:, 0:NCLS, :], c_acc).then_inc(cls_done, 16)
            sp.wait_ge(cls_done, 16)


        @block.gpsimd
        def _(pool):
            pool.wait_ge(ready_v, 1)

            def halve(g, hk):
                pool.wait_ge(x_in[hk % RING], 16 * (g * (NHALF // RING) + hk // RING + 1))
                w = x_ring[0:TP, hk % RING, :].rearrange("p (c n) -> p c n", c=HCH)
                nc.gpsimd.tensor_tensor(w[:, :, 0:PIX // 2], w[:, :, 0:PIX // 2], w[:, :, PIX // 2:PIX],
                                        ALU.add).then_inc(x_halved, 1)

            def body(t, st, before):
                for s in range(SLOTS):
                    if st["pool_cur"] is not None and s in POOL_CUR:
                        halve(st["pool_cur"], POOL_CUR[s])
                    if st["pool_next"] is not None and s in POOL_NEXT:
                        halve(st["pool_next"], POOL_NEXT[s])
                    if st["norm2"] is not None and s == STAT2_SLOT + 1:
                        g = st["norm2"]
                        pool.wait_ge(var2_set, g + 1)
                        nc.gpsimd.tensor_tensor(rstd2[:, :], var2[:, :], minus_half[0:TP, :],
                                                ALU.pow).then_inc(rstd2_set, 1)
                    if st["norm2"] is not None and s == X_LO_SLOT:
                        g = st["norm2"]
                        pool.wait_ge(x_hi_set, g + 1)
                        nc.gpsimd.tensor_tensor(x_tok[:, :, 1, :], xhat[0:TP, :].rearrange("p (k e) -> p k e", k=NT),
                                                x_tok[:, :, 0, :], ALU.subtract).then_inc(x_lo_set, 1)
                    if st["norm1"] is not None and s == STAT1_SLOT + 1:
                        g = st["norm1"]
                        pool.wait_ge(var1_set, g + 1)
                        nc.gpsimd.tensor_tensor(rstd1[:, :], var1[:, :], minus_half[0:TP, :],
                                                ALU.pow).then_inc(rstd1_set, 1)
                    if gelu_chunks(st, s) is not None:
                        g, c = gelu_chunks(st, s)
                        m, lo = c % MT, (c // MT) * HALF_T
                        pool.wait_ge(gelu_set, CHUNKS * g + c + 1)
                        nc.gpsimd.tensor_tensor(hid[:, 1, m, lo:lo + HALF_T], gelu32[:, c % 3, :],
                                                hid[:, 0, m, lo:lo + HALF_T], ALU.subtract).then_inc(hid_set, 1)

            iterations(pool, body)
            pool.wait_ge(cls_v, CLS_SS)
            nc.gpsimd.tensor_tensor(nrm[:, :], ss[:, :], half_c[:, :], ALU.pow).then_inc(cls_pow, 1)

        @block.scalar
        def _(act):
            act.wait_ge(ready_v, 1)

            def body(t, st, before):
                par = st["par"]
                g = st["attend"]

                def copy_g_hi(gg, n):
                    act.wait_ge(g_full, SLOTS * gg + n + 1)
                    wait(act, g_split, SLOTS * gg + n - 1)
                    nc.scalar.activation(g_hi[:, n % 2, :], g_ps[:, 0:TOK], ACT.Copy).then_inc(g_hi_set, 1)

                def copy_y_hi(gy, q, gpar):
                    act.wait_ge(y_full, NQUAD * gy + q + 1)
                    wait(act, h2_set, NPAIR * (gy - 1))
                    b = q // QUADS
                    nc.scalar.activation(y_t[:, gpar, 0, q % QUADS, b * TOK:(b + 1) * TOK], y_ps[:, 0:TOK],
                                         ACT.Copy).then_inc(y_hi_set, 1)

                def gelu(gf, c):
                    m, lo = c % MT, (c // MT) * HALF_T
                    act.wait_ge(fc1_full, CHUNKS * gf + c + 1)
                    wait(act, hid_set, CHUNKS * gf + c - 2)
                    wait(act, fc2_full, NT * gf)
                    src = f_ps[(c + 1) % 2][:, 0:HALF_T]
                    nc.scalar.activation(gelu32[:, c % 3, :], src, ACT.Gelu, bias=b1[:, m:m + 1], scale=1.0 / WSCALE)
                    nc.scalar.activation(hid[:, 0, m, lo:lo + HALF_T], src, ACT.Gelu, bias=b1[:, m:m + 1],
                                         scale=1.0 / WSCALE).then_inc(gelu_set, 1)

                for s in range(SLOTS):
                    ahead = st["attend"] if s + AHEAD < SLOTS else st["norm1"]
                    if ahead is not None:
                        copy_g_hi(ahead, (s + AHEAD) % SLOTS)
                    if gelu_chunks(st, s) is not None:
                        gelu(*gelu_chunks(st, s))
                    if g is not None:
                        if s in ACT_RELU:
                            act.wait_ge(scores_full, SLOTS * g + s + 1)
                            wait(act, y_full, NQUAD * g + s // 2 - 1)
                            nc.scalar.activation(st0[:, s % 4, :], s_ps[s % 2][:, 0:2 * TOK],
                                                 ACT.Relu).then_inc(relu0_a, 1)
                        if s % 2 == 1:
                            q = s // 2
                            act.wait_ge(k1_full, SLOTS * g + s + 1)
                            wait(act, y_full, NQUAD * g + q - 1)
                            nc.scalar.activation(st1[:, q % 2, :], k1_ps[0:K1, 0:4 * K1],
                                                 ACT.Relu).then_inc(relu1_set, 1)
                        if s >= 3 and s % 2 == 1:
                            copy_y_hi(g, s // 2 - 1, par)
                    if s == 0 and st["last_av"] is not None:
                        copy_y_hi(st["last_av"], NQUAD - 1, 1 - par)
                    if g is not None and s % PAIRS == 0:
                        b = s // PAIRS
                        act.wait_ge(v_full, GI * g + b + 1)
                        wait(act, y_full, NQUAD * g + QUADS * (b - 1))
                        nc.scalar.activation(v0[:, b % 2, :, 0:HD], m_ps[:, 0:EMB].rearrange("p (h d) -> p h d", h=HEADS),
                                             ACT.Copy)
                        nc.scalar.activation(v1[:, b % 2, :, 0:HD],
                                             m_ps[0:K1, EMB:2 * EMB].rearrange("p (h d) -> p h d", h=HEADS),
                                             ACT.Copy).then_inc(v_set, 1)
                    if st["norm2"] is not None:
                        n2 = st["norm2"]
                        if s == X_HI_SLOT:
                            act.wait_ge(xhat_set, n2 + 1)
                            wait(act, x_stack_set, 3 * n2)
                            nc.scalar.activation(x_tok[:, :, 0, :], xhat[0:TP, :].rearrange("p (k e) -> p k e", k=NT),
                                                 ACT.Copy).then_inc(x_hi_set, 1)
                        if s in XT_SLOTS:
                            c = XT_SLOTS.index(s)
                            act.wait_ge(xt_full, 3 * n2 + c + 1)
                            wait(act, fc1_full, CHUNKS * n2)
                            nc.scalar.activation(x_stack[:, c, :], m_ps16[:, 0:GT], ACT.Copy).then_inc(x_stack_set, 1)
                    if st["norm1"] is not None:
                        n1 = st["norm1"]
                        if s == UT_SLOT:
                            act.wait_ge(ut_full, n1 + 1)
                            wait(act, h1_full, NPAIR * n1)
                            nc.scalar.activation(u_stack[:, :], m_ps16[:, 0:GT], ACT.Copy).then_inc(u_stack_set, 1)
                        if 0 <= s - H1_SLOT < NPAIR:
                            i = s - H1_SLOT
                            n = min(2, NT - 2 * i) * EMB
                            act.wait_ge(h1_full, NPAIR * n1 + i + 1)
                            wait(act, h2_set, NPAIR * (n1 - 1))
                            nc.scalar.activation(h_tok[0:TP, 1 - par, 2 * i * EMB:2 * i * EMB + n], m_ps[0:TP, 0:n],
                                                 ACT.Copy).then_inc(h_set, 1)
                        if s == PT_SLOT:
                            act.wait_ge(pt_full, n1 + 1)
                            for j in range(2):
                                r = slice(64 * j, 64 * j + 64)
                                last = nc.scalar.activation(p_stack[r, 1 - par, j, :], m_ps16[r, 0:GT], ACT.Copy)
                            last.then_inc(p_stack_set, 1)

            iterations(act, body)

            act.wait_ge(y_full, NQUAD * NG)
            for i, (ps, k, n0, nn) in enumerate(CT_PARTS):
                act.wait_ge(ct_full, i + 1)
                nc.scalar.activation(cx_t[0:EH, k, n0:n0 + nn, :],
                                     ps[0:EH, 0:nn * 128].rearrange("p (n b) -> p n b", n=nn), ACT.Copy).then_inc(ct_set, 1)
            act.wait_ge(cls_v, CLS_LG)
            nc.scalar.activation(pr[:, :, :], lg[:, :, :], ACT.Exp).then_inc(cls_exp, 1)
            act.wait_ge(fc2_full, NT * NG)
            for a in range(NATOM):
                n = 128 * len(ATOM_TOKENS[a])
                if a >= 2:
                    act.wait_ge(cand_full, CANDS_BEFORE[a - 1])
                for m in range(MT):
                    u = a * MT + m
                    act.wait_ge(ch_full, u + 1)
                    nc.scalar.activation(c_hid[a % 2][:, m, 0:n], f_ps[u % 2][:, 0:n], ACT.Gelu,
                                         bias=b_in[:, u:u + 1]).then_inc(ch_set, 1)

        @block.tensor
        def _(pe):
            def mm(o, lhs_t, rhs, start=True, stop=True):
                return nc.tensor.matmul(o, lhs_t, rhs, start=start, stop=stop)

            pe.wait_ge(const_in, 16 * CONSTS)
            pe.wait_ge(setup_v, 3)
            mm(g_ps[0:64, 0:EMB], spread[:, :], c_raw[:, :])
            mm(s_ps[0][:, 0:64], c_cen[:, 0:128], spread[:, :])
            mm(s_ps[0][0:64, 64:128], c_cen[:, 128:EMB], spread[:, :]).then_inc(setup_p, 1)
            pe.wait_ge(setup_v, 8)

            def head_t(o, col):
                mm(o, wa_raw[:, 0, col:col + HD], cct[:, 0, :], stop=False)
                mm(o, wa_raw[0:64, 1, col:col + HD], cct[0:64, 1, :], start=False, stop=False)
                return mm(o, b_attn[0:1, col:col + HD], bias_row[0:1, :], start=False)

            for h in range(HEADS):
                qb = (s_ps[1], 64 * h) if h < 8 else (k1_ps, 64 * (h - 8))
                kb = (k1_ps, 256 + 64 * h) if h < 4 else (y_ps, 64 * (h - 4))
                head_t(qb[0][0:HD, qb[1]:qb[1] + 64], h * HD)
                head_t(kb[0][0:HD, kb[1]:kb[1] + 64], EMB + h * HD)
            vo = f_ps[0][0:64, 0:EMB]
            mm(vo, cct[:, 0, :], wa_raw[:, 0, 2 * EMB:3 * EMB], stop=False)
            mm(vo, cct[0:64, 1, :], wa_raw[0:64, 1, 2 * EMB:3 * EMB], start=False, stop=False)
            mm(vo, bias_row[0:1, :], b_attn[0:1, 2 * EMB:3 * EMB], start=False).then_inc(setup_p, 1)
            pe.wait_ge(setup_v, 15)
            for h in range(HEADS):
                ab = (g_ps, 64 * h) if h < 8 else (s_ps[0], 64 * (h - 8))
                last = mm(ab[0][0:64, ab[1]:ab[1] + 64], mq_t[:, h, :], mk_t[:, h, :])
            last.then_inc(setup_p, 1)
            pe.wait_ge(ready_v, 1)

            emptied = {"v": (v_set, GI), "h2": (h2_set, NPAIR), "xt": (x_stack_set, 3), "ut": (u_stack_set, 1),
                       "h1": (h_set, NPAIR), "pt": (p_stack_set, 1)}

            def body(t, st, before):
                par = st["par"]
                g = st["attend"]
                uses = shared_uses(st)
                earlier = shared_uses(before)

                def wait_shared(i):
                    if i > 0:
                        _, what, k, stage = uses[i - 1]
                        grp = st[stage]
                    elif earlier:
                        _, what, k, stage = earlier[-1]
                        grp = before[stage]
                    else:
                        return
                    done, per = emptied[what]
                    pe.wait_ge(done, per * grp + k + 1)

                def g_product(gg, n, gpar):
                    b, p = divmod(n, PAIRS)
                    wait(pe, g_split, SLOTS * gg + n)
                    if n == 0:
                        pe.wait_ge(p_stack_set, gg + 1)
                    mm(g_ps[:, 0:TOK], a_stack[:, p * 128:(p + 1) * 128],
                       p_stack[:, gpar, 0, b * TOK:(b + 1) * TOK]).then_inc(g_full, 1)

                def scores_k0(s):
                    b = s // PAIRS
                    pe.wait_ge(g_split, SLOTS * g + s + 1)
                    if s < 2:
                        wait(pe, relu0_v, NR_V * (g - 1) + SLOTS + s - 1 - by_act(SLOTS + s - 1))
                    elif s - 2 in ACT_RELU:
                        pe.wait_ge(relu0_a, NR_A * g + by_act(s - 1))
                    else:
                        pe.wait_ge(relu0_v, NR_V * g + s - 1 - by_act(s - 1))
                    masked = s in ACT_RELU
                    for j in range(2):
                        c = j * TOK
                        if masked:
                            mm(s_ps[s % 2][:, c:c + K0], ident_big[:, :], mask_big[:, :], stop=False)
                            mm(s_ps[s % 2][:, c:c + K0], p_stack[:, par, j, b * TOK:b * TOK + K0],
                               g_stack[:, s % 3, 0:K0], start=False)
                            last = mm(s_ps[s % 2][:, c + K0:c + TOK], p_stack[:, par, j, b * TOK:b * TOK + K0],
                                      g_stack[:, s % 3, K0:TOK])
                        else:
                            last = mm(s_ps[s % 2][:, c:c + TOK], p_stack[:, par, j, b * TOK:b * TOK + K0],
                                      g_stack[:, s % 3, :])
                    last.then_inc(scores_full, 1)

                def scores_k1(s):
                    b, q = s // PAIRS, s // 2
                    if s % 2 == 0:
                        wait(pe, relu1_set, NQUAD * g + q)
                    for j in range(2):
                        c = (2 * (s % 2) + j) * K1
                        mm(k1_ps[0:K1, c:c + K1], ident_big[0:K1, 0:K1], mask_big[0:K1, 0:K1], stop=False)
                        last = mm(k1_ps[0:K1, c:c + K1], p_stack[:, par, j, b * TOK + K0:(b + 1) * TOK],
                                  g_stack[:, s % 3, K0:TOK], start=False)
                    last.then_inc(k1_full, 1)

                def attend_v(gy, q):
                    b, qd = divmod(q, QUADS)
                    pe.wait_ge(relu0_v, NR_V * gy + 2 * q + 2 - by_act(2 * q + 2))
                    wait(pe, relu0_a, NR_A * gy + by_act(2 * q + 2))
                    pe.wait_ge(relu1_set, NQUAD * gy + q + 1)
                    pe.wait_ge(v_set, GI * gy + b + 1)
                    wait(pe, y_lo_set, NQUAD * gy + q)
                    for j in range(4):
                        w = st0[:, (2 * q + j // 2) % 4, (j % 2) * TOK:(j % 2 + 1) * TOK]
                        mm(y_ps[32 * j:32 * j + 32, 0:TOK], v0[:, b % 2, 4 * qd + j, :], w, stop=False)
                    for j in range(4):
                        last = mm(y_ps[32 * j:32 * j + 32, K0:TOK], v1[:, b % 2, 4 * qd + j, :],
                                  st1[:, q % 2, j * K1:(j + 1) * K1], start=False)
                    last.then_inc(y_full, 1)

                def v_product(b):
                    mm(m_ps[:, 0:EMB], p_stack[:, par, 0, b * TOK:b * TOK + K0], mv_stack[:, :])
                    mm(m_ps[0:K1, EMB:2 * EMB], p_stack[:, par, 0, b * TOK + K0:(b + 1) * TOK],
                       mv_stack[:, :]).then_inc(v_full, 1)

                def y_rows(i):
                    pe.wait_ge(y_lo_set, NQUAD * (st["norm2"] + 1))
                    for j, k in enumerate(range(2 * i, min(2 * i + 2, NT))):
                        for qd in range(QUADS):
                            for part in range(2):
                                c = j * EMB + qd * 64
                                last = mm(m_ps[0:TP, c:c + 64], y_t[:, 1 - par, part, qd, k * TP:(k + 1) * TP],
                                          head_sel[:, :], start=part == 0, stop=part == 1)
                    last.then_inc(h2_full, 1)

                def x_columns(c):
                    pe.wait_ge(x_lo_set if c > 0 else x_hi_set, st["norm2"] + 1)
                    flat = x_tok[:, :, :, :].rearrange("p k a e -> p k (a e)")
                    for k in range(NT):
                        last = nc.tensor.transpose(m_ps16[:, k * TP:(k + 1) * TP], flat[:, k, c * 128:(c + 1) * 128],
                                                   ident16[0:TP, 0:TP])
                    last.then_inc(xt_full, 1)

                def u_columns():
                    pe.wait_ge(u_tok_set, st["norm1"] + 1)
                    for k in range(NT):
                        last = nc.tensor.transpose(m_ps16[:, k * TP:(k + 1) * TP],
                                                   u_tok[:, k, :, :].rearrange("p a c -> p (a c)"), ident16[0:TP, 0:TP])
                    last.then_inc(ut_full, 1)

                def h_rows(i):
                    pe.wait_ge(u_stack_set, st["norm1"] + 1)
                    for j, k in enumerate(range(2 * i, min(2 * i + 2, NT))):
                        last = mm(m_ps[0:TP, j * EMB:(j + 1) * EMB], u_stack[:, k * TP:(k + 1) * TP], c_stack[:, :])
                    last.then_inc(h1_full, 1)

                def p_columns():
                    pe.wait_ge(p_tok_set, st["norm1"] + 1)
                    for k in range(NT):
                        last = nc.tensor.transpose(m_ps16[:, k * TP:(k + 1) * TP],
                                                   p_tok[:, k, :, :].rearrange("p a c -> p (a c)"), ident16[0:TP, 0:TP])
                    last.then_inc(pt_full, 1)

                def fc1(c):
                    gf = st["fc1"]
                    m, lo = c % MT, (c // MT) * HALF_T
                    pe.wait_ge(x_stack_set, 3 * (gf + 1))
                    if c >= 2:
                        pe.wait_ge(gelu_set, CHUNKS * gf + c - 1)
                    else:
                        wait(pe, o_set, NT * gf - 1 + c)
                    o = f_ps[(c + 1) % 2][:, 0:HALF_T]
                    parts = [(w1_hi, 0), (w1_lo, 0), (w1_hi, 1), (w1_lo, 1), (w1_hi, 2)]
                    for i, (w, k) in enumerate(parts):
                        last = mm(o, w[:, k, m * 128:(m + 1) * 128], x_stack[:, k, lo:lo + HALF_T], start=i == 0,
                                  stop=i == len(parts) - 1)
                    last.then_inc(fc1_full, 1)

                def fc2(i):
                    gf = st["fc2"]
                    pe.wait_ge(hid_set, CHUNKS * (gf + 1))
                    if i >= 2:
                        pe.wait_ge(o_set, NT * gf + i - 1)
                    o = f_ps[i % 2][0:TP, 0:EMB]
                    mm(o, ones_pad[:, :], b2_stack[:, :], stop=False)
                    for m in range(MT):
                        for part, w in ((0, w2_hi), (0, w2_lo), (1, w2_hi)):
                            last = mm(o, hid[:, part, m, i * TP:(i + 1) * TP], w[:, m, :], start=False,
                                      stop=m == MT - 1 and part == 1)
                    last.then_inc(fc2_full, 1)

                shared = {"v": v_product, "h2": y_rows, "xt": x_columns, "ut": lambda i: u_columns(), "h1": h_rows,
                          "pt": lambda i: p_columns()}
                for s in range(SLOTS):
                    ahead = st["attend"] if s + AHEAD < SLOTS else st["norm1"]
                    if ahead is not None:
                        g_product(ahead, (s + AHEAD) % SLOTS, par if s + AHEAD < SLOTS else 1 - par)
                    if g is not None:
                        scores_k0(s)
                        if s >= 3 and s % 2 == 1:
                            attend_v(g, s // 2 - 1)
                        scores_k1(s)
                    if s == 0 and st["last_av"] is not None:
                        attend_v(st["last_av"], NQUAD - 1)
                    if st["fc2"] is not None and s in FC2_SLOTS:
                        fc2(FC2_SLOTS.index(s))
                    for i, (slot, what, k, _) in enumerate(uses):
                        if slot == s:
                            wait_shared(i)
                            shared[what](k)
                    if st["fc1"] is not None and s >= FC1_SLOT:
                        fc1(s - FC1_SLOT)

            iterations(pe, body)

            pe.wait_ge(cls_in, 32)
            pe.wait_ge(relu0_v, NR_V * NG)
            pe.wait_ge(o_set, NT * NG)
            for ps, k, n0, nn in CT_PARTS:
                for j in range(nn):
                    last = nc.tensor.transpose(ps[0:EH, j * 128:(j + 1) * 128], cx[:, n0 + j, k * EH:(k + 1) * EH],
                                               ident32[:, :])
                last.then_inc(ct_full, 1)
            pe.wait_ge(ct_set, len(CT_PARTS))
            pe.wait_ge(cls_w_in, 16 * 6)

            def atom_hidden(a):
                toks = ATOM_TOKENS[a]
                n = 128 * len(toks)
                step = toks[1] - toks[0]
                for m in range(MT):
                    u = a * MT + m
                    if u >= 2:
                        pe.wait_ge(ch_set, u - 1)
                    for k in range(2):
                        last = mm(f_ps[u % 2][:, 0:n], a_in[:, k, a * HID + m * 128:a * HID + (m + 1) * 128],
                                  cx_t[0:EH, k, toks[0]:toks[-1] + 1:step, :], start=k == 0, stop=k == 1)
                    last.then_inc(ch_full, 1)

            def atom_candidates(a):
                pe.wait_ge(ch_set, (a + 1) * MT)
                for j, n in enumerate(ATOM_TOKENS[a]):
                    u = CANDS_BEFORE[a] + j
                    r = 0 if a < 3 else 1
                    if u >= 2:
                        pe.wait_ge(cand_tmp, u - 1)
                    for m in range(MT):
                        w = a_out_early[:, m, :] if m < MT // 2 else a_out_late[:, m - MT // 2, :]
                        last = mm(s_ps[u % 2][:, 0:EMB], c_hid[a % 2][:, m, j * 128:(j + 1) * 128],
                                  w[:, DST[n][r] * EMB:(DST[n][r] + 1) * EMB], start=m == 0, stop=m == MT - 1)
                    last.then_inc(cand_full, 1)

            atom_hidden(0)
            for a in range(NATOM):
                if a + 1 < NATOM:
                    atom_hidden(a + 1)
                atom_candidates(a)

        @block.vector
        def _(dve):
            count = [0]

            def step(ins):
                count[0] += 1
                ins.then_inc(setup_v, 1)
                dve.wait_ge(setup_v, count[0])

            v = nc.vector
            dve.wait_ge(const_in, 16 * CONSTS)
            step(v.tensor_reduce(c_sum[:, 0:1], c_raw[:, :], AX.X, ALU.add))
            step(v.tensor_scalar(c_sum[:, 1:2], c_sum[:, 0:1], -1.0 / EMB, None, ALU.mult))
            step(v.tensor_scalar(c_cen[:, :], c_raw[:, :], c_sum[:, 1:2], None, ALU.add))
            dve.wait_ge(setup_p, 1)

            def split_rows(dst, src, tmp):
                step(v.tensor_copy(tmp, src))
                step(v.tensor_copy(dst[0:32, :], src[0:32, :]))
                step(v.tensor_tensor(dst[32:64, :], src[32:64, :], tmp[32:64, :], ALU.subtract))

            split_rows(c_stack[:, :], g_ps[0:64, 0:EMB], setup16[:, 0:EMB])
            step(v.tensor_copy(cct[:, 0, :], s_ps[0][:, 0:64]))
            step(v.tensor_copy(cct[0:64, 1, :], s_ps[0][0:64, 64:128]))
            dve.wait_ge(setup_p, 2)

            def heads_view(ps, c, n):
                return ps[0:HD, c:c + 64 * n].rearrange("p (h c) -> p h c", h=n)

            step(v.tensor_scalar(mq_t[:, 0:8, :], heads_view(s_ps[1], 0, 8), HD ** -0.5, None, ALU.mult))
            step(v.tensor_scalar(mq_t[:, 8:12, :], heads_view(k1_ps, 0, 4), HD ** -0.5, None, ALU.mult))
            step(v.tensor_copy(mk_t[:, 0:4, :], heads_view(k1_ps, 256, 4)))
            step(v.tensor_copy(mk_t[:, 4:12, :], heads_view(y_ps, 0, 8)))
            split_rows(mv_stack[:, :], f_ps[0][0:64, 0:EMB], setup16[:, 0:EMB])
            dve.wait_ge(setup_p, 3)
            split_rows(a_stack[:, 0:512], g_ps[0:64, :], setup16[:, 0:512])
            split_rows(a_stack[:, 512:768], s_ps[0][0:64, 0:256], setup16[:, 512:768])
            dve.wait_ge(wts_in, 16 * WEIGHTS)
            step(v.tensor_scalar(w1_hi[:, :, :], w1_raw[:, :, :], WSCALE, None, ALU.mult))
            step(v.scalar_tensor_tensor(w1_lo[:, 0, :], w1_raw[:, 0, :], WSCALE, w1_hi[:, 0, :], ALU.mult, ALU.subtract))
            step(v.scalar_tensor_tensor(w1_lo[0:64, 1, :], w1_raw[0:64, 1, :], WSCALE, w1_hi[0:64, 1, :],
                                        ALU.mult, ALU.subtract))
            step(v.memset(w1_lo[64:128, 1, :], 0.0))
            step(v.tensor_scalar(w2_hi[:, :, :], w2_raw[:, :, :], WSCALE, None, ALU.mult))
            step(v.scalar_tensor_tensor(w2_lo[:, :, :], w2_raw[:, :, :], WSCALE, w2_hi[:, :, :], ALU.mult, ALU.subtract))
            step(v.memset(b2_stack[:, :], 0.0))
            step(v.tensor_scalar(b2_stack[0:1, :], b2_raw[0:1, :], WSCALE, None, ALU.mult))
            step(v.tensor_scalar(b2_tmp[32:33, :], b2_raw[32:33, :], WSCALE, None, ALU.mult))
            step(v.scalar_tensor_tensor(b2_stack[32:33, :], b2_raw[32:33, :], WSCALE, b2_tmp[32:33, :],
                                        ALU.mult, ALU.subtract))
            step(v.memset(u_tok[:, :, :, :], 0.0))
            for stack in (c_stack, a_stack, mv_stack):
                step(v.memset(stack[64:128, :], 0.0))
            step(v.memset(p_stack[64:128, :, 0, :], 0.0))
            step(v.tensor_scalar(mask_big[:, :], mask_k0[:, 0:128], -1.0, BIG, ALU.add, ALU.mult))
            step(v.tensor_scalar(ident_big[:, :], ident32[:, :], BIG, None, ALU.mult))
            step(v.memset(p_stack[0:64, :, 1, :], 0.0))
            step(v.memset(p_tok[:, :, :, :], 0.0))
            step(v.memset(p_tok[:, :, 0:8:2, NCH:NCH + 1], 1.0))
            step(v.memset(v0[:, :, :, :], 0.0))
            step(v.memset(v1[:, :, :, :], 0.0))
            step(v.memset(half_c[:, :], 0.5))
            step(v.memset(minus_half[:, :], -0.5))
            v.memset(xhat[:, 0:1], 0.0).then_inc(ready_v, 1)
            dve.wait_ge(ready_v, 1)

            def body(t, st, before):
                par = st["par"]
                g = st["attend"]

                def split_g(gg, n):
                    dve.wait_ge(g_hi_set, SLOTS * gg + n + 1)
                    wait(dve, k1_full, SLOTS * gg + n - 2)
                    v.scalar_tensor_tensor(g_stack[:, n % 3, :], g_hi[:, n % 2, :], neg_lo[:, 0:1], g_ps[:, 0:TOK],
                                           ALU.mult, ALU.add).then_inc(g_split, 1)

                def relu_k0(s):
                    dve.wait_ge(scores_full, SLOTS * g + s + 1)
                    wait(dve, y_full, NQUAD * g + s // 2 - 1)
                    v.scalar_tensor_tensor(st0[:, s % 4, :], s_ps[s % 2][:, 0:2 * TOK], 0.0, mask_k0[:, :],
                                           ALU.max, ALU.mult).then_inc(relu0_v, 1)

                def y_low(gy, q, gpar):
                    dve.wait_ge(y_hi_set, NQUAD * gy + q + 1)
                    b = q // QUADS
                    c = slice(b * TOK, (b + 1) * TOK)
                    v.tensor_tensor(y_t[:, gpar, 1, q % QUADS, c], y_ps[:, 0:TOK], y_t[:, gpar, 0, q % QUADS, c],
                                    ALU.subtract).then_inc(y_lo_set, 1)

                def window_sums(gp, hk, gpar):
                    dve.wait_ge(x_halved, NHALF * gp + hk + 1)
                    w = x_ring[0:TP, hk % RING, :].rearrange("p (c n) -> p c n", c=HCH)
                    c = (hk % 2) * HCH
                    v.tensor_reduce(pooled[:, gpar, hk // 2, c:c + HCH], w[:, :, 0:PIX // 2], AX.X,
                                    ALU.add).then_inc(x_pooled, 1)

                def variance(bn, tmp, var, part_set, sq_set, gn):
                    v.tensor_tensor(tmp[:, 0, :], bn[:, :, 1], bn[:, :, 4], ALU.subtract)
                    v.scalar_tensor_tensor(tmp[:, 1, :], bn[:, :, 2], EMB * EPS, bn[:, :, 5], ALU.add,
                                           ALU.add).then_inc(part_set, 1)
                    dve.wait_ge(part_set, gn + 1)
                    v.scalar_tensor_tensor(tmp[:, 2, :], tmp[:, 0, :], 0.25, tmp[:, 0, :], ALU.mult,
                                           ALU.mult).then_inc(sq_set, 1)
                    dve.wait_ge(sq_set, gn + 1)
                    return v.scalar_tensor_tensor(var[:, :], tmp[:, 1, :], 1.0 / EMB, tmp[:, 2, :], ALU.mult, ALU.add)

                def residual(i):
                    n2 = st["norm2"]
                    n = min(2, NT - 2 * i)
                    c = slice(2 * i * EMB, (2 * i + n) * EMB)
                    dve.wait_ge(h2_full, NPAIR * n2 + i + 1)
                    if i == 0:
                        dve.wait_ge(h_set, NPAIR * (n2 + 1))
                        wait(dve, cls_out, 32 * GI * (n2 - 1))
                        wait(dve, o_set, NT * (n2 - 1))
                    v.tensor_tensor(h2_tok[0:TP, 1 - par, c], m_ps[0:TP, 0:n * EMB], h_tok[0:TP, 1 - par, c],
                                    ALU.add).then_inc(h2_set, 1)
                    dve.wait_ge(h2_set, NPAIR * n2 + i + 1)
                    for k in range(2 * i, 2 * i + n):
                        last = v.bn_stats(bn2[:, k, :], h2_tok[0:TP, 1 - par, k * EMB:(k + 1) * EMB])
                    last.then_inc(bn2_set, 1)

                for s in range(SLOTS):
                    if s == 0 and st["last_av"] is not None:
                        y_low(st["last_av"], NQUAD - 2, 1 - par)
                    if s == 1 and st["last_av"] is not None:
                        y_low(st["last_av"], NQUAD - 1, 1 - par)
                    if g is not None and s >= 4 and s % 2 == 0:
                        y_low(g, s // 2 - 2, par)
                    if g is not None and s not in ACT_RELU:
                        relu_k0(s)
                    ahead = st["attend"] if s + AHEAD < SLOTS else st["norm1"]
                    if ahead is not None:
                        split_g(ahead, (s + AHEAD) % SLOTS)
                    if st["fc2"] is not None and s - 1 in FC2_SLOTS:
                        gf, i = st["fc2"], FC2_SLOTS.index(s - 1)
                        dve.wait_ge(fc2_full, NT * gf + i + 1)
                        if i == 0:
                            wait(dve, out_done, 16 * gf)
                        c = slice(i * EMB, (i + 1) * EMB)
                        v.scalar_tensor_tensor(o_tok[0:TP, c], f_ps[i % 2][0:TP, 0:EMB], 1.0 / WSCALE,
                                               h2_tok[0:TP, par, c], ALU.mult, ALU.add).then_inc(o_set, 1)
                    if st["norm2"] is not None:
                        n2 = st["norm2"]
                        if 0 <= s - 1 - H2_SLOT < NPAIR:
                            residual(s - 1 - H2_SLOT)
                        if s == STAT2_SLOT:
                            dve.wait_ge(bn2_set, NPAIR * (n2 + 1))
                            v.tensor_tensor(sum2[:, :], bn2[:, :, 1], bn2[:, :, 4], ALU.add)
                            variance(bn2, st2s, var2, part2_set, sq2_set, n2).then_inc(var2_set, 1)
                            v.tensor_scalar(mean2[:, :], sum2[:, :], 0.5, None, ALU.mult).then_inc(mean2_set, 1)
                        if s == XHAT_SLOT:
                            dve.wait_ge(rstd2_set, n2 + 1)
                            dve.wait_ge(mean2_set, n2 + 1)
                            wait(dve, cls_out, 32 * GI * n2)
                            wait(dve, x_lo_set, n2)
                            for k in range(NT):
                                c = slice(k * EMB, (k + 1) * EMB)
                                last = v.tensor_scalar(xhat[0:TP, c], h2_tok[0:TP, 1 - par, c], mean2[:, k:k + 1],
                                                       rstd2[:, k:k + 1], ALU.subtract, ALU.mult)
                            last.then_inc(xhat_set, 1)
                    if st["pool_cur"] is not None and s in SUM_CUR:
                        window_sums(st["pool_cur"], SUM_CUR[s], 1 - par)
                    if st["pool_next"] is not None and s in SUM_NEXT:
                        window_sums(st["pool_next"], SUM_NEXT[s], par)
                    if st["norm1"] is not None:
                        n1 = st["norm1"]
                        if s == U_SLOT:
                            sums = pooled[:, 1 - par, :, :].unsqueeze(2).broadcast_to([TP, NT, 2, NCH])
                            dve.wait_ge(x_pooled, NHALF * (n1 + 1))
                            wait(dve, ut_full, n1)
                            v.tensor_copy(u_tok[:, :, 0:4:2, 0:NCH], sums).then_inc(u_hi_set, 1)
                            dve.wait_ge(u_hi_set, n1 + 1)
                            v.tensor_tensor(u_tok[:, :, 1:4:2, 0:NCH], sums,
                                            u_tok[:, :, 0:1, 0:NCH].broadcast_to([TP, NT, 2, NCH]),
                                            ALU.subtract).then_inc(u_tok_set, 1)
                        if 0 <= s - H1_SLOT - 1 < NPAIR:
                            i = s - H1_SLOT - 1
                            dve.wait_ge(h_set, NPAIR * n1 + i + 1)
                            for k in range(2 * i, min(2 * i + 2, NT)):
                                last = v.bn_stats(bn1[:, k, :], h_tok[0:TP, 1 - par, k * EMB:(k + 1) * EMB])
                            last.then_inc(bn1_set, 1)
                        if s == STAT1_SLOT:
                            dve.wait_ge(bn1_set, NPAIR * (n1 + 1))
                            variance(bn1, st1s, var1, part1_set, sq1_set, n1).then_inc(var1_set, 1)
                        if s == PN_SLOT:
                            dve.wait_ge(rstd1_set, n1 + 1)
                            v.tensor_tensor(pn[:, :, :], pooled[:, 1 - par, :, :],
                                            rstd1[:, :].unsqueeze(2).broadcast_to([TP, NT, NCH]),
                                            ALU.mult).then_inc(pn_set, 1)
                            p4 = pn[:, :, :].unsqueeze(2).broadcast_to([TP, NT, 4, NCH])
                            dve.wait_ge(pn_set, n1 + 1)
                            wait(dve, pt_full, n1)
                            v.tensor_copy(p_tok[:, :, 0:8:2, 0:NCH], p4).then_inc(p_hi_set, 1)
                            dve.wait_ge(p_hi_set, n1 + 1)
                            v.tensor_tensor(p_tok[:, :, 1:8:2, 0:NCH], p4,
                                            p_tok[:, :, 0:1, 0:NCH].broadcast_to([TP, NT, 4, NCH]),
                                            ALU.subtract).then_inc(p_tok_set, 1)

            iterations(dve, body)

            done = [0]

            def link(ins):
                done[0] += 1
                ins.then_inc(cls_v, 1)
                dve.wait_ge(cls_v, done[0])

            dve.wait_ge(cls_in, 32)
            dve.wait_ge(cls_w_in, 16 * 6)
            dve.wait_ge(h2_full, NPAIR * NG)
            link(v.tensor_tensor(gate_tmp[:, 0:NCLS, :], cx, cx, ALU.mult))
            link(v.tensor_reduce(ss[:, 0:NCLS], gate_tmp[:, 0:NCLS, :], AX.X, ALU.add))
            link(v.tensor_tensor(gate_tmp, gate_w, gate_w, ALU.mult))
            link(v.tensor_reduce(ss[:, NCLS:3 * NCLS], gate_tmp, AX.X, ALU.add))
            assert done[0] == CLS_SS
            by_route = gate_tmp.rearrange("p (n r) e -> p n r e", r=2)
            link(v.tensor_tensor(by_route, cx.unsqueeze(2).broadcast_to([128, NCLS, 2, EMB]),
                                 gate_w.rearrange("p (n r) e -> p n r e", r=2), ALU.mult))
            link(v.tensor_reduce(lg[:, :, :].rearrange("p n r -> p (n r)"), gate_tmp, AX.X, ALU.add))
            dve.wait_ge(cls_pow, 1)
            link(v.tensor_scalar(nrm[:, :], nrm[:, :], 1e-12, None, ALU.max))
            link(v.reciprocal(nrm[:, :], nrm[:, :]))
            flat = lg[:, :, :].rearrange("p n r -> p (n r)")
            link(v.tensor_tensor(flat, flat, nrm[:, NCLS:3 * NCLS], ALU.mult))
            link(v.tensor_tensor(lg[:, :, :], lg[:, :, :], nrm[:, 0:NCLS].unsqueeze(2).broadcast_to([128, NCLS, 2]), ALU.mult))
            link(v.tensor_tensor(flat, flat, bal[:, :], ALU.add))
            link(v.tensor_tensor(gs[:, 0, :], lg[:, :, 0], lg[:, :, 1], ALU.max))
            link(v.tensor_tensor(lg[:, :, :], lg[:, :, :], gs[:, 0, :].unsqueeze(2).broadcast_to([128, NCLS, 2]), ALU.subtract))
            assert done[0] == CLS_LG
            dve.wait_ge(cls_exp, 1)
            link(v.tensor_tensor(gs[:, 1, :], pr[:, :, 0], pr[:, :, 1], ALU.add))
            link(v.reciprocal(gs[:, 2, :], gs[:, 1, :]))
            link(v.tensor_tensor(pr[:, :, :], pr[:, :, :], gs[:, 2, :].unsqueeze(2).broadcast_to([128, NCLS, 2]), ALU.mult))
            link(v.tensor_tensor(gs[:, 3, :], pr[:, :, 1], pr[:, :, 0], ALU.is_gt))
            link(v.tensor_scalar(gs[:, 4, :], gs[:, 3, :], -1.0, 1.0, ALU.mult, ALU.add))
            link(v.tensor_tensor(wgt[:, :, 1], pr[:, :, 1], gs[:, 3, :], ALU.mult))
            link(v.tensor_tensor(wgt[:, :, 0], pr[:, :, 0], gs[:, 4, :], ALU.mult))
            dve.wait_ge(out_done, 16 * NG)
            dve.wait_ge(x_lo_set, NG)
            dve.wait_ge(cls_out, 32 * GI * NG)
            for a in range(NATOM):
                r = 0 if a < 3 else 1
                for j, n in enumerate(ATOM_TOKENS[a]):
                    u = CANDS_BEFORE[a] + j
                    dve.wait_ge(cand_full, u + 1)
                    wait(dve, cand_set, u)
                    v.tensor_tensor(c_tmp[:, u % 2, :], s_ps[u % 2][:, 0:EMB], b_out[:, DST[n][r], :],
                                    ALU.add).then_inc(cand_tmp, 1)
                    dve.wait_ge(cand_tmp, u + 1)
                    base = ch[:, n, :] if r == 0 else c_acc[:, n, :]
                    v.scalar_tensor_tensor(c_acc[:, n, :], c_tmp[:, u % 2, :], wgt[:, n, r:r + 1], base,
                                           ALU.mult, ALU.add).then_inc(cand_set, 1)


def kernel(x, L0_tok_channel_weights, L0_attn_W_attn, L0_attn_b_attn, L0_ffn_fc1_w, L0_ffn_fc1_b, L0_ffn_fc2_w,
           L0_ffn_fc2_b, L0_ffn_gate_pair, L0_ffn_atom_in_w, L0_ffn_atom_in_b, L0_ffn_atom_out_w, L0_ffn_atom_out_b,
           L0_ffn_balance_bias):
    import concourse.bacc as bacc
    from concourse.bass_utils import run_bass_kernel_spmd

    def lay(a):
        return np.ascontiguousarray(a)

    f = np.float32
    rows = np.arange(128)
    head_sel = np.zeros((128, 64), np.float16)
    for j in range(4):
        for k in range(HD):
            head_sel[32 * j + k, HD * j + k] = 1
    causal = (np.arange(TOK)[None, :] >= rows[:, None]).astype(f)
    spread = np.zeros((NCH, 64), f)
    bias_row = np.zeros((1, 64), f)
    for part in range(4):
        for c in range(NCH):
            spread[c, 16 * part + c] = 1
        bias_row[0, 16 * part + NCH] = 1
    ones_pad = np.zeros((128, TP), np.float16)
    ones_pad[0] = ones_pad[32] = 1
    arrays = {
        "ident16": np.eye(128, dtype=np.float16), "ident32": np.eye(128, dtype=f), "head_sel": head_sel,
        "mask_k0": np.concatenate([causal, causal], 1),
        "neg_lo": -((rows // 32) % 2).astype(f)[:, None], "spread": spread, "bias_row": bias_row, "ones_pad": ones_pad,
        "x": lay(np.asarray(x).reshape(NIMG, NCH, SIDE, PATCH, SIDE, PATCH).transpose(0, 2, 4, 1, 3, 5)).reshape(
            NIMG * TOK, ROW),
        "cw": lay(L0_tok_channel_weights),
        "wa_t": lay(np.asarray(L0_attn_W_attn).T), "b_attn": lay(np.asarray(L0_attn_b_attn).reshape(1, 3 * EMB)),
        "w1_t": lay(np.asarray(L0_ffn_fc1_w).T), "w2_t": lay(np.asarray(L0_ffn_fc2_w).T),
        "b1": lay(np.asarray(L0_ffn_fc1_b).reshape(MT, 128).T), "b2": lay(np.asarray(L0_ffn_fc2_b).reshape(1, EMB)),
        "gate": lay(np.asarray(L0_ffn_gate_pair).reshape(-1)),
        "a_in_t": lay(np.asarray(L0_ffn_atom_in_w).reshape(NATOM * HID, EMB).T),
        "b_in": lay(np.asarray(L0_ffn_atom_in_b).reshape(NATOM * MT, 128).T),
        "a_out_t": lay(np.asarray(L0_ffn_atom_out_w).transpose(2, 0, 1)).reshape(HID, NATOM * EMB),
        "b_out": lay(np.asarray(L0_ffn_atom_out_b).reshape(-1)),
        "bal": lay(np.asarray(L0_ffn_balance_bias).reshape(-1)),
    }
    nc = bacc.Bacc("TRN2", target_bir_lowering=False, num_devices=1)
    d = {n: nc.dram_tensor("in_" + n, a.shape, mybir.dt.from_np(a.dtype), kind="ExternalInput").ap() for n, a in arrays.items()}
    out = nc.dram_tensor("out", (NIMG * TOK, EMB), F32, kind="ExternalOutput").ap()
    cls_x = nc.dram_tensor("cls_x", (NIMG * NCLS, EMB), F32, kind="Internal").ap()
    cls_h = nc.dram_tensor("cls_h", (NIMG * NCLS, EMB), F32, kind="Internal").ap()
    vit_tower_kernel(nc, d, out, cls_x, cls_h)
    r = run_bass_kernel_spmd(nc, [{"in_" + n: a for n, a in arrays.items()}], core_ids=[0])
    return r.results[0]["out"].reshape(NIMG, TOK, EMB)
```

```python
from contextlib import ExitStack

import numpy as np

import concourse.bass as bass
from concourse import mybir

F32 = mybir.dt.float32
F16 = mybir.dt.float16
BF16 = mybir.dt.bfloat16
ACT = mybir.ActivationFunctionType
ALU = mybir.AluOpType
AX = mybir.AxisListType

NIMG, NCH, SIDE, PATCH = 128, 12, 14, 16
TOK = SIDE * SIDE
PIX = PATCH * PATCH
EMB = 192
HEADS, HD = 12, 16
HID = 768
NCLS, NATOM = 6, 5
EPS = 1e-5

GI = 4
GT = GI * TOK
TP = 112
NT = GT // TP
NG = NIMG // GI
NHALF = 2 * NT
HCH = NCH // 2
RING = 7
ROW = NCH * PIX
K0, K1 = 128, TOK - 128
PAIRS = HEADS // 2
QUADS = HEADS // 4
SLOTS = GI * PAIRS
NQUAD = GI * QUADS
MT = HID // 128
EH = EMB // 2
HALF_T = GT // 2
CHUNKS = 2 * MT
WSCALE = 64.0

CUR_SLOTS, CUR_SUM_SLOTS = (0, 1), (2, 3)
NEXT_SLOTS = (3, 4, 6, 7, 9, 10, 12, 13, 15, 17, 19, 21)
NEXT_SUM_SLOTS = (7, 9, 11, 13, 14, 15, 16, 17, 18, 19, 21, 23)
POOL_CUR = {s: len(NEXT_SLOTS) + i for i, s in enumerate(CUR_SLOTS)}
POOL_NEXT = {s: i for i, s in enumerate(NEXT_SLOTS)}
SUM_CUR = {s: len(NEXT_SLOTS) + i for i, s in enumerate(CUR_SUM_SLOTS)}
SUM_NEXT = {s: i for i, s in enumerate(NEXT_SUM_SLOTS)}
V_SLOTS = (0, 5, 14, 18)
NPAIR = (NT + 1) // 2
H2_SLOT = 1
STAT2_SLOT = 5
XHAT_SLOT, XHAT_ACT = 7, 4
X_HI_SLOT, X_LO_SLOT = 8, 9
X_LO_POOL = 4
XT_SLOTS = (11, 12, 13)
U_SLOT, UT_SLOT, H1_SLOT = 6, 7, 8
STAT1_SLOT, PN_SLOT, PT_SLOT = 12, 14, 15
FC1_SLOT = 14
FC2_SLOTS = (2, 4, 5, 7, 9, 10, 12)
ACT_RELU = (2, 3, 4, 5, 6, 9, 10, 11, 12)
NR_A, NR_V = len(ACT_RELU), SLOTS - len(ACT_RELU)
BIG = 2.0 ** 60

SRC = [[n // 2, 3 + n % 2] for n in range(NCLS)]
DST = [[3 + n % 2, n // 2] for n in range(NCLS)]


def stages(t, python_t):
    def there(d):
        return 0 <= python_t + d < NG
    return {
        "pool_next": t + 2 if there(2) else None,
        "pool_cur": t + 1 if there(1) else None,
        "norm1": t + 1 if there(1) else None,
        "attend": t if there(0) else None,
        "last_av": t - 1 if there(-1) else None,
        "norm2": t - 1 if there(-1) else None,
        "fc1": t - 1 if there(-1) else None,
        "load_next": there(3),
        "fc2": t - 2 if there(-2) else None,
        "par": python_t % 2,
    }


ATOM_TOKENS = [[0, 1], [2, 3], [4, 5], [0, 2, 4], [1, 3, 5]]
CANDS_BEFORE = [0, 2, 4, 6, 9, 12]
CLS_SS, CLS_LG = 4, 13


def shared_uses(st):
    uses = []
    for s in range(SLOTS):
        if st["attend"] is not None and s in V_SLOTS:
            uses.append((s, "v", V_SLOTS.index(s), "attend"))
        if st["norm2"] is not None and 0 <= s - H2_SLOT < NPAIR:
            uses.append((s, "h2", s - H2_SLOT, "norm2"))
        if st["norm1"] is not None and s == UT_SLOT:
            uses.append((s, "ut", 0, "norm1"))
        if st["norm1"] is not None and 0 <= s - H1_SLOT < NPAIR:
            uses.append((s, "h1", s - H1_SLOT, "norm1"))
        if st["norm2"] is not None and s in XT_SLOTS:
            uses.append((s, "xt", XT_SLOTS.index(s), "norm2"))
        if st["norm1"] is not None and s == PT_SLOT:
            uses.append((s, "pt", 0, "norm1"))
    return uses


FIRST_T, LAST_T = -2, NG + 1
LOOP_T0, LOOP_T1 = 2, NG - 4


def iterations(eng, body, between=()):
    for t in range(FIRST_T, LOOP_T0):
        body(t, stages(t, t), stages(t - 1, t - 1))
        if t - FIRST_T < len(between):
            between[t - FIRST_T]()
    with eng.Fori(0, (LOOP_T1 - LOOP_T0) // 2) as turn:
        for half in range(2):
            t = turn * 2 + LOOP_T0
            body(t + half, stages(t + half, LOOP_T0 + half), stages(t + (half - 1), LOOP_T0 + half - 1))
    for t in range(LOOP_T1, LAST_T + 1):
        body(t, stages(t, t), stages(t - 1, t - 1))


def g_pair(st, s, lead):
    nxt, u = divmod((s + lead) // 2, SLOTS // 2)
    group = st["norm1"] if nxt else st["attend"]
    return None if (s + lead) % 2 or group is None else (group, u, nxt)


def by_act(n):
    return sum(s < n for s in ACT_RELU)


def fc1_chunk(st, s):
    stage, c = ("fc1", s - FC1_SLOT) if s >= FC1_SLOT else ("fc2", s + SLOTS - FC1_SLOT)
    return (st[stage], c) if st[stage] is not None and c < CHUNKS else None


def gelu_chunk(st, s):
    return fc1_chunk(st, s - 1)


def wait(eng, sem, value):
    if not (isinstance(value, int) and value <= 0):
        eng.wait_ge(sem, value)


def vit_tower_kernel(nc, d, out, cls_x, cls_h):
    with ExitStack() as ctx:
        def sb(name, shape, dt):
            return ctx.enter_context(nc.sbuf_tensor(name, shape, dt))

        def bank(name):
            return ctx.enter_context(nc.psum_tensor(name, [128, 512], F32))

        def sem(name):
            return ctx.enter_context(nc.semaphore(name))

        g_ps = bank("g_ps")
        s_ps = [bank("s_ps0"), bank("s_ps1")]
        k1_ps = bank("k1_ps")
        y_ps = bank("y_ps")
        f_ps = [bank("f_ps0"), bank("f_ps1")]
        m_ps = bank("m_ps")
        m_ps16 = m_ps[:, :].bitcast(F16)

        ident16 = sb("ident16", [128, 128], F16)
        ident32 = sb("ident32", [128, 128], F32)
        head_sel = sb("head_sel", [128, 64], F16)
        mask_k0 = sb("mask_k0", [128, 2 * TOK], F32)
        mask_big = sb("mask_big", [128, 128], BF16)
        ident_big = sb("ident_big", [128, 128], BF16)
        neg_lo = sb("neg_lo", [128, 1], F32)
        spread = sb("spread", [NCH, 64], F32)
        bias_row = sb("bias_row", [1, 64], F32)
        ones_pad = sb("ones_pad", [128, TP], F16)
        minus_half = sb("minus_half", [128, NT], F32)

        c_raw = sb("c_raw", [NCH, EMB], F32)
        c_cen = sb("c_cen", [NCH, EMB], F32)
        c_sum = sb("c_sum", [NCH, 2], F32)
        c_stack = sb("c_stack", [128, EMB], F16)
        cct = sb("cct", [128, 2, 64], F32)
        b_attn = sb("b_attn", [1, 3 * EMB], F32)
        mq_t = sb("mq_t", [HD, HEADS, 64], F32)
        mk_t = sb("mk_t", [HD, HEADS, 64], F32)
        a_stack = sb("a_stack", [128, HEADS * 64], F16)
        mv_stack = sb("mv_stack", [128, EMB], F16)
        setup16 = sb("setup16", [64, HEADS * 64], F16)
        w1_hi = sb("w1_hi", [128, 3, HID], F16)
        w1_lo = sb("w1_lo", [128, 2, HID], F16)
        w2_hi = sb("w2_hi", [128, MT, EMB], F16)
        w2_lo = sb("w2_lo", [128, MT, EMB], F16)
        b1 = sb("b1", [128, MT], F32)
        b2_raw = sb("b2_raw", [64, EMB], F32)
        b2_stack = sb("b2_stack", [128, EMB], F16)
        b2_tmp = sb("b2_tmp", [64, EMB], F16)

        x_ring = sb("x_ring", [128, RING, HCH * PIX], F32)
        pooled = sb("pooled", [TP, 2, NT, NCH], F32)
        u_tok = sb("u_tok", [TP, NT, 8, 16], F16)
        u_stack = sb("u_stack", [128, GT], F16)
        h_tok = sb("h_tok", [128, 2, NT * EMB], F32)
        bn1 = sb("bn1", [TP, NT, 6], F32)
        st1s = sb("st1s", [TP, 3, NT], F32)
        var1 = sb("var1", [TP, NT], F32)
        rstd1 = sb("rstd1", [TP, NT], F32)
        pn = sb("pn", [TP, NT, NCH], F32)
        p_tok = sb("p_tok", [TP, NT, 8, 16], F16)
        p_stack = sb("p_stack", [128, 2, 2, GT], F16)
        g_hi = sb("g_hi", [128, 2, 2 * TOK], F16)
        g_stack = sb("g_stack", [128, 3, 2 * TOK], F16)
        st0 = sb("st0", [128, 4, 2 * TOK], F32)
        st1 = sb("st1", [K1, 2, 4 * K1], F32)
        v0 = sb("v0", [128, 2, HEADS, 32], F32)
        v1 = sb("v1", [K1, 2, HEADS, 32], F32)
        y_t = sb("y_t", [128, 2, 2, QUADS, GT], F16)
        h2_tok = sb("h2_tok", [128, 2, NT * EMB], F32)
        bn2 = sb("bn2", [TP, NT, 6], F32)
        st2s = sb("st2s", [TP, 3, NT], F32)
        sum2 = sb("sum2", [TP, NT], F32)
        shift2 = sb("shift2", [TP, NT], F32)
        var2 = sb("var2", [TP, NT], F32)
        rstd2 = sb("rstd2", [TP, NT], F32)
        xhat = sb("xhat", [128, NT * EMB], F32)
        x_tok = sb("x_tok", [TP, NT, 2, EMB], F16)
        x_stack = sb("x_stack", [128, 3, GT], F16)
        gelu32 = sb("gelu32", [128, 3, HALF_T], F32)
        hid = sb("hid", [128, 2, MT, GT], F16)
        o_tok = sb("o_tok", [128, NT * EMB], F32)

        hid32 = hid[:, :, :, :].rearrange("p a m t -> p (a m t)").bitcast(F32)
        w1_raw = hid32[:, 0:3 * HID].rearrange("p (k n) -> p k n", k=3)
        w2_raw = hid32[:, 3 * HID:3 * HID + MT * EMB].rearrange("p (m n) -> p m n", m=MT)
        wa_raw = hid32[:, 3 * HID + MT * EMB:3 * HID + MT * EMB + 2 * 3 * EMB].rearrange("p (k n) -> p k n", k=2)

        x_flat = x_ring[:, :, :].rearrange("p r n -> p (r n)")
        a_in = x_flat[0:EH, 0:2 * NATOM * HID].rearrange("p (k n) -> p k n", k=2)
        a_out_late = x_flat[:, 2 * NATOM * HID:2 * NATOM * HID + MT // 2 * NATOM * EMB].rearrange("p (m n) -> p m n", m=MT // 2)
        a_out_early = sb("a_out_early", [128, MT // 2, NATOM * EMB], F32)
        cx = h_tok[:, 0, 0:NCLS * EMB].rearrange("p (n e) -> p n e", n=NCLS)
        ch = h_tok[:, 1, 0:NCLS * EMB].rearrange("p (n e) -> p n e", n=NCLS)
        y32 = y_t[:, :, :, :, :].rearrange("p a b q t -> p (a b q t)").bitcast(F32)
        gate_w = y32[:, 0:2 * NCLS * EMB].rearrange("p (n e) -> p n e", n=2 * NCLS)
        gate_tmp = y32[:, 2 * NCLS * EMB:4 * NCLS * EMB].rearrange("p (n e) -> p n e", n=2 * NCLS)
        b_out = sb("b_out", [128, NATOM, EMB], F32)
        cx_t = st0[:, :, :].rearrange("p a b -> p (a b)")[:, 0:2 * NCLS * 128].rearrange("p (k n b) -> p k n b", k=2, n=NCLS)
        c_hid = [hid32[:, i * MT * 3 * 128:(i + 1) * MT * 3 * 128].rearrange("p (m n) -> p m n", m=MT) for i in range(2)]
        c_acc = o_tok[:, 0:NCLS * EMB].rearrange("p (n e) -> p n e", n=NCLS)
        c_tmp = xhat[:, 0:2 * EMB].rearrange("p (n e) -> p n e", n=2)
        b_in = sb("b_in", [128, NATOM * MT], F32)
        bal = sb("bal", [128, 2 * NCLS], F32)
        ss = sb("ss", [128, 3 * NCLS], F32)
        nrm = sb("nrm", [128, 3 * NCLS], F32)
        half_c = sb("half_c", [128, 3 * NCLS], F32)
        lg = sb("lg", [128, NCLS, 2], F32)
        pr = sb("pr", [128, NCLS, 2], F32)
        gs = sb("gs", [128, 6, NCLS], F32)
        wgt = sb("wgt", [128, NCLS, 2], F32)

        attn_in = sem("attn_in")
        const_in = sem("const_in")
        wts_in = sem("wts_in")
        const_set = sem("const_set")
        setup_v = sem("setup_v")
        setup_p = sem("setup_p")
        memory_set = sem("memory_set")
        weights_split = sem("weights_split")
        x_in = [sem(f"x_in{i}") for i in range(RING)]
        x_halved = sem("x_halved")
        x_pooled = sem("x_pooled")
        v_full = sem("v_full")
        h2_full = sem("h2_full")
        xt_full = sem("xt_full")
        ut_full = sem("ut_full")
        h1_full = sem("h1_full")
        pt_full = sem("pt_full")
        u_hi_set = sem("u_hi_set")
        u_tok_set = sem("u_tok_set")
        u_stack_set = sem("u_stack_set")
        h_set = sem("h_set")
        bn1_set = sem("bn1_set")
        part1_set = sem("part1_set")
        sq1_set = sem("sq1_set")
        sq2_set = sem("sq2_set")
        var1_set = sem("var1_set")
        rstd1_set = sem("rstd1_set")
        pn_set = sem("pn_set")
        p_hi_set = sem("p_hi_set")
        p_tok_set = sem("p_tok_set")
        p_stack_set = sem("p_stack_set")
        g_full = sem("g_full")
        g_hi_set = sem("g_hi_set")
        g_split = sem("g_split")
        scores_full = sem("scores_full")
        k1_full = sem("k1_full")
        relu0_v = sem("relu0_v")
        relu0_a = sem("relu0_a")
        relu1_set = sem("relu1_set")
        v_set = sem("v_set")
        y_full = sem("y_full")
        y_hi_set = sem("y_hi_set")
        y_lo_set = sem("y_lo_set")
        h2_set = sem("h2_set")
        bn2_set = sem("bn2_set")
        part2_set = sem("part2_set")
        var2_set = sem("var2_set")
        shift2_set = sem("shift2_set")
        rstd2_set = sem("rstd2_set")
        xhat_a = sem("xhat_a")
        xhat_v = sem("xhat_v")
        x_hi_set = sem("x_hi_set")
        x_lo_pool = sem("x_lo_pool")
        x_lo_vector = sem("x_lo_vector")
        x_stack_set = sem("x_stack_set")
        fc1_full = sem("fc1_full")
        gelu_set = sem("gelu_set")
        hid_set = sem("hid_set")
        fc2_full = sem("fc2_full")
        o_set = sem("o_set")
        out_done = sem("out_done")
        cls_out = sem("cls_out")
        cls_w_in = sem("cls_w_in")
        cls_in = sem("cls_in")
        cls_v = sem("cls_v")
        cls_pow = sem("cls_pow")
        cls_exp = sem("cls_exp")
        ct_full = sem("ct_full")
        ct_set = sem("ct_set")
        ch_full = sem("ch_full")
        ch_set = sem("ch_set")
        cand_full = sem("cand_full")
        cand_tmp = sem("cand_tmp")
        cand_set = sem("cand_set")
        cls_done = sem("cls_done")

        CT_PARTS = [(s_ps[0], 0, 0, 4), (s_ps[1], 0, 4, 2), (f_ps[0], 1, 0, 4), (f_ps[1], 1, 4, 2)]
        ATTN = 6
        CONSTS = 5
        WEIGHTS = 9

        def ring_reuse(g, hk):
            return NHALF * g + (hk - RING) + 1

        block = ctx.enter_context(nc.Block())

        @block.sync
        def _(sp):
            def load_x(g, hk):
                wait(sp, x_pooled, ring_reuse(g, hk))
                src = d["x"][bass.ds(g * GT + (hk // 2) * TP, TP), (hk % 2) * HCH * PIX:(hk % 2 + 1) * HCH * PIX]
                sp.dma_start(x_ring[0:TP, hk % RING, :], src).then_inc(x_in[hk % RING], 16)

            for dst, src in ((c_raw[:, :], d["cw"]), (spread[:, :], d["spread"]), (bias_row[:, :], d["bias_row"]),
                             (b_attn[:, :], d["b_attn"]), (wa_raw[:, 0, :], d["wa_t"][0:128, :]),
                             (wa_raw[0:64, 1, :], d["wa_t"][128:EMB, :])):
                sp.dma_start(dst, src).then_inc(attn_in, 16)
            for hk in range(2):
                load_x(0, hk)
            for dst, src in ((ident16[:, :], d["ident16"]), (ident32[:, :], d["ident32"]), (head_sel[:, :], d["head_sel"]),
                             (mask_k0[:, :], d["mask_k0"]), (neg_lo[:, :], d["neg_lo"])):
                sp.dma_start(dst, src).then_inc(const_in, 16)
            for hk in range(2, RING):
                load_x(0, hk)
            def load_weights():
                for dst, src in ((w1_raw[:, 0, :], d["w1_t"][0:128, :]), (w1_raw[0:64, 1, :], d["w1_t"][128:EMB, :]),
                                 (w1_raw[64:128, 1, :], d["w1_t"][0:64, :]), (w1_raw[:, 2, :], d["w1_t"][64:EMB, :]),
                                 (w2_raw[:, :, :], d["w2_t"].rearrange("(m p) n -> p m n", p=128)),
                                 (b1[:, :], d["b1"]), (b2_raw[0:1, :], d["b2"]), (b2_raw[32:33, :], d["b2"]),
                                 (ones_pad[:, :], d["ones_pad"])):
                    sp.dma_start(dst, src).then_inc(wts_in, 16)

            def load_class_weights():
                sp.wait_ge(x_pooled, NHALF * NG)
                for dst, src in ((a_in[:, 0, :], d["a_in_t"][0:EH, :]), (a_in[:, 1, :], d["a_in_t"][EH:EMB, :]),
                                 (a_out_early[:, :, :], d["a_out_t"][0:HID // 2, :].rearrange("(m p) n -> p m n", p=128)),
                                 (a_out_late, d["a_out_t"][HID // 2:HID, :].rearrange("(m p) n -> p m n", p=128)),
                                 (b_in[:, :], d["b_in"]), (bal[:, :], d["bal"].partition_broadcast(128)),
                                 (b_out[:, :, :], d["b_out"].partition_broadcast(128).rearrange("p (a e) -> p a e", e=EMB))):
                    sp.dma_start(dst, src).then_inc(cls_w_in, 16)

            def load_class_tokens():
                sp.wait_ge(h2_set, NPAIR * NG)
                sp.dma_start(gate_w, d["gate"].partition_broadcast(128).rearrange("p (n e) -> p n e", e=EMB)).then_inc(cls_w_in, 16)
                sp.wait_ge(cls_out, 16 * 2 * GI * NG)
                sp.dma_start(cx, cls_x.rearrange("(b n) e -> b n e", n=NCLS)).then_inc(cls_in, 16)
                sp.dma_start(ch, cls_h.rearrange("(b n) e -> b n e", n=NCLS)).then_inc(cls_in, 16)

            def body(t, st, before):
                par = st["par"]
                for s in range(SLOTS):
                    for stage, table in (("pool_cur", SUM_CUR), ("pool_next", SUM_NEXT)):
                        if st[stage] is not None and s in table:
                            g, hk = st[stage], table[s]
                            if hk + RING < NHALF:
                                load_x(g, hk + RING)
                            elif st["load_next"] if stage == "pool_next" else st["pool_next"] is not None:
                                load_x(g + 1, hk + RING - NHALF)
                    if s == FC2_SLOTS[-1] + 1 and st["fc2"] is not None:
                        g = st["fc2"]
                        sp.wait_ge(o_set, NT * g + NT)
                        sp.dma_start(out[bass.ds(g * GT, GT), :].rearrange("(k p) e -> p k e", p=TP),
                                     o_tok[0:TP, :].rearrange("p (k e) -> p k e", k=NT)).then_inc(out_done, 16)
                    if s == X_HI_SLOT and st["norm2"] is not None:
                        g = st["norm2"]
                        sp.wait_ge(xhat_a, g + 1)
                        sp.wait_ge(xhat_v, g + 1)
                        for b in range(GI):
                            k, r = divmod(b * TOK, TP)
                            for buf, dst in ((xhat[:, :], cls_x), (h2_tok[:, (par + 1) % 2, :], cls_h)):
                                sp.dma_start(dst[bass.ds((g * GI + b) * NCLS, NCLS), :],
                                             buf[r:r + NCLS, k * EMB:(k + 1) * EMB]).then_inc(cls_out, 16)

                if isinstance(t, int) and t == NG - 1:
                    load_class_weights()
                if isinstance(t, int) and t == NG:
                    load_class_tokens()

            iterations(sp, body, between=(load_weights,))

            sp.wait_ge(out_done, 16 * NG)
            sp.wait_ge(cand_set, 2 * NCLS)
            sp.dma_start(out.rearrange("(b t) e -> b t e", t=TOK)[:, 0:NCLS, :], c_acc).then_inc(cls_done, 16)
            sp.wait_ge(cls_done, 16)

        @block.gpsimd
        def _(pool):
            def halve(g, hk):
                pool.wait_ge(x_in[hk % RING], 16 * (g * (NHALF // RING) + hk // RING + 1))
                w = x_ring[0:TP, hk % RING, :].rearrange("p (c n) -> p c n", c=HCH)
                nc.gpsimd.tensor_tensor(w[:, :, 0:PIX // 2], w[:, :, 0:PIX // 2], w[:, :, PIX // 2:PIX],
                                        ALU.add).then_inc(x_halved, 1)

            def body(t, st, before):
                for s in range(SLOTS):
                    if st["pool_cur"] is not None and s in POOL_CUR:
                        halve(st["pool_cur"], POOL_CUR[s])
                    if st["pool_next"] is not None and s in POOL_NEXT:
                        halve(st["pool_next"], POOL_NEXT[s])
                    if st["norm2"] is not None and s == STAT2_SLOT + 1:
                        g = st["norm2"]
                        pool.wait_ge(var2_set, g + 1)
                        nc.gpsimd.tensor_tensor(rstd2[:, :], var2[:, :], minus_half[0:TP, :],
                                                ALU.pow).then_inc(rstd2_set, 1)
                    if st["norm2"] is not None and s == X_LO_SLOT:
                        g = st["norm2"]
                        pool.wait_ge(x_hi_set, g + 1)
                        k = slice(0, X_LO_POOL)
                        nc.gpsimd.tensor_tensor(x_tok[:, k, 1, :], xhat[0:TP, :].rearrange("p (k e) -> p k e", k=NT)[:, k, :],
                                                x_tok[:, k, 0, :], ALU.subtract).then_inc(x_lo_pool, 1)
                    if st["norm1"] is not None and s == STAT1_SLOT + 1:
                        g = st["norm1"]
                        pool.wait_ge(var1_set, g + 1)
                        nc.gpsimd.tensor_tensor(rstd1[:, :], var1[:, :], minus_half[0:TP, :],
                                                ALU.pow).then_inc(rstd1_set, 1)
                    if gelu_chunk(st, s) is not None:
                        g, c = gelu_chunk(st, s)
                        m, lo = c % MT, (c // MT) * HALF_T
                        pool.wait_ge(gelu_set, CHUNKS * g + c + 1)
                        nc.gpsimd.tensor_tensor(hid[:, 1, m, lo:lo + HALF_T], gelu32[:, c % 3, :],
                                                hid[:, 0, m, lo:lo + HALF_T], ALU.subtract).then_inc(hid_set, 1)

            iterations(pool, body)
            pool.wait_ge(cls_v, CLS_SS)
            nc.gpsimd.tensor_tensor(nrm[:, :], ss[:, :], half_c[:, :], ALU.pow).then_inc(cls_pow, 1)

        @block.scalar
        def _(act):
            def body(t, st, before):
                par = st["par"]
                g = st["attend"]

                def copy_g_hi(gg, u):
                    act.wait_ge(g_full, SLOTS // 2 * gg + u + 1)
                    wait(act, g_split, SLOTS // 2 * gg + u - 1)
                    nc.scalar.activation(g_hi[:, u % 2, :], g_ps[:, 0:2 * TOK], ACT.Copy).then_inc(g_hi_set, 1)

                def copy_y_hi(gy, q, gpar):
                    act.wait_ge(y_full, NQUAD * gy + q + 1)
                    wait(act, h2_set, NPAIR * (gy - 1))
                    b = q // QUADS
                    nc.scalar.activation(y_t[:, gpar, 0, q % QUADS, b * TOK:(b + 1) * TOK], y_ps[:, 0:TOK],
                                         ACT.Copy).then_inc(y_hi_set, 1)

                def gelu(gf, c):
                    m, lo = c % MT, (c // MT) * HALF_T
                    act.wait_ge(fc1_full, CHUNKS * gf + c + 1)
                    wait(act, hid_set, CHUNKS * gf + c - 2)
                    wait(act, fc2_full, NT * gf)
                    src = f_ps[(c + 1) % 2][:, 0:HALF_T]
                    nc.scalar.activation(gelu32[:, c % 3, :], src, ACT.Gelu, bias=b1[:, m:m + 1], scale=1.0 / WSCALE)
                    nc.scalar.activation(hid[:, 0, m, lo:lo + HALF_T], src, ACT.Gelu, bias=b1[:, m:m + 1],
                                         scale=1.0 / WSCALE).then_inc(gelu_set, 1)

                for s in range(SLOTS):
                    if g_pair(st, s, 3) is not None:
                        copy_g_hi(*g_pair(st, s, 3)[0:2])
                    if gelu_chunk(st, s) is not None:
                        gelu(*gelu_chunk(st, s))
                    if g is not None:
                        if s in ACT_RELU:
                            act.wait_ge(scores_full, SLOTS * g + s + 1)
                            wait(act, y_full, NQUAD * g + s // 2 - 1)
                            nc.scalar.activation(st0[:, s % 4, :], s_ps[s % 2][:, 0:2 * TOK],
                                                 ACT.Relu).then_inc(relu0_a, 1)
                        if s % 2 == 1:
                            q = s // 2
                            act.wait_ge(k1_full, SLOTS * g + s + 1)
                            wait(act, y_full, NQUAD * g + q - 1)
                            nc.scalar.activation(st1[:, q % 2, :], k1_ps[0:K1, 0:4 * K1],
                                                 ACT.Relu).then_inc(relu1_set, 1)
                        if s >= 3 and s % 2 == 1:
                            copy_y_hi(g, s // 2 - 1, par)
                    if s == 0 and st["last_av"] is not None:
                        copy_y_hi(st["last_av"], NQUAD - 1, 1 - par)
                    if g is not None and s in V_SLOTS:
                        b = V_SLOTS.index(s)
                        act.wait_ge(v_full, GI * g + b + 1)
                        wait(act, y_full, NQUAD * g + QUADS * (b - 1))
                        nc.scalar.activation(v0[:, b % 2, :, 0:HD], m_ps[:, 0:EMB].rearrange("p (h d) -> p h d", h=HEADS),
                                             ACT.Copy)
                        nc.scalar.activation(v1[:, b % 2, :, 0:HD],
                                             m_ps[0:K1, EMB:2 * EMB].rearrange("p (h d) -> p h d", h=HEADS),
                                             ACT.Copy).then_inc(v_set, 1)
                    if st["norm1"] is not None:
                        n1 = st["norm1"]
                        if s == UT_SLOT:
                            act.wait_ge(ut_full, n1 + 1)
                            wait(act, h1_full, NPAIR * n1)
                            nc.scalar.activation(u_stack[:, :], m_ps16[:, 0:GT], ACT.Copy).then_inc(u_stack_set, 1)
                        if 0 <= s - H1_SLOT < NPAIR:
                            i = s - H1_SLOT
                            n = min(2, NT - 2 * i) * EMB
                            act.wait_ge(h1_full, NPAIR * n1 + i + 1)
                            wait(act, h2_set, NPAIR * (n1 - 1))
                            nc.scalar.activation(h_tok[0:TP, 1 - par, 2 * i * EMB:2 * i * EMB + n], m_ps[0:TP, 0:n],
                                                 ACT.Copy).then_inc(h_set, 1)
                    if st["norm2"] is not None:
                        n2 = st["norm2"]
                        if s == XHAT_SLOT:
                            act.wait_ge(shift2_set, n2 + 1)
                            wait(act, cls_out, 32 * GI * n2)
                            wait(act, x_lo_pool, n2)
                            for k in range(XHAT_ACT):
                                c = slice(k * EMB, (k + 1) * EMB)
                                last = nc.scalar.activation(xhat[0:TP, c], h2_tok[0:TP, 1 - par, c], ACT.Identity,
                                                            bias=shift2[:, k:k + 1], scale=rstd2[:, k:k + 1])
                            last.then_inc(xhat_a, 1)
                        if s == X_HI_SLOT:
                            act.wait_ge(xhat_a, n2 + 1)
                            act.wait_ge(xhat_v, n2 + 1)
                            wait(act, x_lo_vector, n2)
                            wait(act, x_stack_set, 3 * n2)
                            nc.scalar.activation(x_tok[:, :, 0, :], xhat[0:TP, :].rearrange("p (k e) -> p k e", k=NT),
                                                 ACT.Copy).then_inc(x_hi_set, 1)
                    if st["norm2"] is not None:
                        n2 = st["norm2"]
                        if s in XT_SLOTS:
                            c = XT_SLOTS.index(s)
                            act.wait_ge(xt_full, 3 * n2 + c + 1)
                            wait(act, fc1_full, CHUNKS * n2)
                            nc.scalar.activation(x_stack[:, c, :], m_ps16[:, 0:GT], ACT.Copy).then_inc(x_stack_set, 1)
                    if st["norm1"] is not None:
                        n1 = st["norm1"]
                        if s == PT_SLOT:
                            act.wait_ge(pt_full, n1 + 1)
                            for j in range(2):
                                r = slice(64 * j, 64 * j + 64)
                                last = nc.scalar.activation(p_stack[r, 1 - par, j, :], m_ps16[r, 0:GT], ACT.Copy)
                            last.then_inc(p_stack_set, 1)

            iterations(act, body)

            act.wait_ge(y_full, NQUAD * NG)
            for i, (ps, k, n0, nn) in enumerate(CT_PARTS):
                act.wait_ge(ct_full, i + 1)
                nc.scalar.activation(cx_t[0:EH, k, n0:n0 + nn, :],
                                     ps[0:EH, 0:nn * 128].rearrange("p (n b) -> p n b", n=nn), ACT.Copy).then_inc(ct_set, 1)
            act.wait_ge(fc2_full, NT * NG)
            for a in range(NATOM):
                n = 128 * len(ATOM_TOKENS[a])
                if a == 2:
                    act.wait_ge(cls_v, CLS_LG)
                    nc.scalar.activation(pr[:, :, :], lg[:, :, :], ACT.Exp).then_inc(cls_exp, 1)
                if a >= 2:
                    act.wait_ge(cand_full, CANDS_BEFORE[a - 1])
                for m in range(MT):
                    u = a * MT + m
                    act.wait_ge(ch_full, u + 1)
                    nc.scalar.activation(c_hid[a % 2][:, m, 0:n], f_ps[u % 2][:, 0:n], ACT.Gelu,
                                         bias=b_in[:, u:u + 1]).then_inc(ch_set, 1)

        @block.tensor
        def _(pe):
            def mm(o, lhs_t, rhs, start=True, stop=True):
                return nc.tensor.matmul(o, lhs_t, rhs, start=start, stop=stop)

            pe.wait_ge(attn_in, 16 * ATTN)
            pe.wait_ge(setup_v, 3)
            mm(g_ps[0:64, 0:EMB], spread[:, :], c_raw[:, :])
            mm(s_ps[0][:, 0:64], c_cen[:, 0:128], spread[:, :])
            mm(s_ps[0][0:64, 64:128], c_cen[:, 128:EMB], spread[:, :]).then_inc(setup_p, 1)
            pe.wait_ge(setup_v, 8)

            def head_t(o, col):
                mm(o, wa_raw[:, 0, col:col + HD], cct[:, 0, :], stop=False)
                mm(o, wa_raw[0:64, 1, col:col + HD], cct[0:64, 1, :], start=False, stop=False)
                return mm(o, b_attn[0:1, col:col + HD], bias_row[0:1, :], start=False)

            for h in range(HEADS):
                qb = (s_ps[1], 64 * h) if h < 8 else (k1_ps, 64 * (h - 8))
                kb = (k1_ps, 256 + 64 * h) if h < 4 else (y_ps, 64 * (h - 4))
                head_t(qb[0][0:HD, qb[1]:qb[1] + 64], h * HD)
                head_t(kb[0][0:HD, kb[1]:kb[1] + 64], EMB + h * HD)
            vo = f_ps[0][0:64, 0:EMB]
            mm(vo, cct[:, 0, :], wa_raw[:, 0, 2 * EMB:3 * EMB], stop=False)
            mm(vo, cct[0:64, 1, :], wa_raw[0:64, 1, 2 * EMB:3 * EMB], start=False, stop=False)
            mm(vo, bias_row[0:1, :], b_attn[0:1, 2 * EMB:3 * EMB], start=False).then_inc(setup_p, 1)
            pe.wait_ge(setup_v, 15)
            for h in range(HEADS):
                ab = (g_ps, 64 * h) if h < 8 else (s_ps[0], 64 * (h - 8))
                last = mm(ab[0][0:64, ab[1]:ab[1] + 64], mq_t[:, h, :], mk_t[:, h, :])
            last.then_inc(setup_p, 1)

            emptied = {"v": (v_set, GI), "h2": (h2_set, NPAIR), "xt": (x_stack_set, 3), "ut": (u_stack_set, 1),
                       "h1": (h_set, NPAIR), "pt": (p_stack_set, 1)}

            def body(t, st, before):
                par = st["par"]
                g = st["attend"]
                uses = shared_uses(st)
                earlier = shared_uses(before)

                def wait_shared(i):
                    if i > 0:
                        _, what, k, stage = uses[i - 1]
                        grp = st[stage]
                    elif earlier:
                        _, what, k, stage = earlier[-1]
                        grp = before[stage]
                    else:
                        return
                    done, per = emptied[what]
                    pe.wait_ge(done, per * grp + k + 1)

                def g_product(gg, u, nxt):
                    wait(pe, g_split, SLOTS // 2 * gg + u)
                    if u == 0:
                        pe.wait_ge(p_stack_set, gg + 1)
                    for j in range(2):
                        b, p = divmod(2 * u + j, PAIRS)
                        last = mm(g_ps[:, j * TOK:(j + 1) * TOK], a_stack[:, p * 128:(p + 1) * 128],
                                  p_stack[:, (par + nxt) % 2, 0, b * TOK:(b + 1) * TOK])
                    last.then_inc(g_full, 1)

                def g_of(s, lo, hi):
                    return g_stack[:, s // 2 % 3, s % 2 * TOK + lo:s % 2 * TOK + hi]

                def scores_k0(s):
                    b = s // PAIRS
                    pe.wait_ge(g_split, SLOTS // 2 * g + s // 2 + 1)
                    if s < 2:
                        wait(pe, relu0_v, NR_V * (g - 1) + SLOTS + s - 1 - by_act(SLOTS + s - 1))
                    elif s - 2 in ACT_RELU:
                        pe.wait_ge(relu0_a, NR_A * g + by_act(s - 1))
                    else:
                        pe.wait_ge(relu0_v, NR_V * g + s - 1 - by_act(s - 1))
                    masked = s in ACT_RELU
                    for j in range(2):
                        c = j * TOK
                        if masked:
                            mm(s_ps[s % 2][:, c:c + K0], ident_big[:, :], mask_big[:, :], stop=False)
                            mm(s_ps[s % 2][:, c:c + K0], p_stack[:, par, j, b * TOK:b * TOK + K0],
                               g_of(s, 0, K0), start=False)
                            last = mm(s_ps[s % 2][:, c + K0:c + TOK], p_stack[:, par, j, b * TOK:b * TOK + K0],
                                      g_of(s, K0, TOK))
                        else:
                            last = mm(s_ps[s % 2][:, c:c + TOK], p_stack[:, par, j, b * TOK:b * TOK + K0],
                                      g_of(s, 0, TOK))
                    last.then_inc(scores_full, 1)

                def scores_k1(s):
                    b, q = s // PAIRS, s // 2
                    if s % 2 == 0:
                        wait(pe, relu1_set, NQUAD * g + q)
                    for j in range(2):
                        c = (2 * (s % 2) + j) * K1
                        mm(k1_ps[0:K1, c:c + K1], ident_big[0:K1, 0:K1], mask_big[0:K1, 0:K1], stop=False)
                        last = mm(k1_ps[0:K1, c:c + K1], p_stack[:, par, j, b * TOK + K0:(b + 1) * TOK],
                                  g_of(s, K0, TOK), start=False)
                    last.then_inc(k1_full, 1)

                def attend_v(gy, q):
                    b, qd = divmod(q, QUADS)
                    pe.wait_ge(relu0_v, NR_V * gy + 2 * q + 2 - by_act(2 * q + 2))
                    wait(pe, relu0_a, NR_A * gy + by_act(2 * q + 2))
                    pe.wait_ge(relu1_set, NQUAD * gy + q + 1)
                    pe.wait_ge(v_set, GI * gy + b + 1)
                    wait(pe, y_lo_set, NQUAD * gy + q)
                    for j in range(4):
                        w = st0[:, (2 * q + j // 2) % 4, (j % 2) * TOK:(j % 2 + 1) * TOK]
                        mm(y_ps[32 * j:32 * j + 32, 0:TOK], v0[:, b % 2, 4 * qd + j, :], w, stop=False)
                    for j in range(4):
                        last = mm(y_ps[32 * j:32 * j + 32, K0:TOK], v1[:, b % 2, 4 * qd + j, :],
                                  st1[:, q % 2, j * K1:(j + 1) * K1], start=False)
                    last.then_inc(y_full, 1)

                def v_product(b):
                    mm(m_ps[:, 0:EMB], p_stack[:, par, 0, b * TOK:b * TOK + K0], mv_stack[:, :])
                    mm(m_ps[0:K1, EMB:2 * EMB], p_stack[:, par, 0, b * TOK + K0:(b + 1) * TOK],
                       mv_stack[:, :]).then_inc(v_full, 1)

                def y_rows(i):
                    pe.wait_ge(y_lo_set, NQUAD * (st["norm2"] + 1))
                    for j, k in enumerate(range(2 * i, min(2 * i + 2, NT))):
                        for qd in range(QUADS):
                            for part in range(2):
                                c = j * EMB + qd * 64
                                last = mm(m_ps[0:TP, c:c + 64], y_t[:, 1 - par, part, qd, k * TP:(k + 1) * TP],
                                          head_sel[:, :], start=part == 0, stop=part == 1)
                    last.then_inc(h2_full, 1)

                def x_columns(c):
                    for done in (x_lo_pool, x_lo_vector) if c > 0 else (x_hi_set,):
                        pe.wait_ge(done, st["norm2"] + 1)
                    flat = x_tok[:, :, :, :].rearrange("p k a e -> p k (a e)")
                    for k in range(NT):
                        last = nc.tensor.transpose(m_ps16[:, k * TP:(k + 1) * TP], flat[:, k, c * 128:(c + 1) * 128],
                                                   ident16[0:TP, 0:TP])
                    last.then_inc(xt_full, 1)

                def u_columns():
                    pe.wait_ge(u_tok_set, st["norm1"] + 1)
                    for k in range(NT):
                        last = nc.tensor.transpose(m_ps16[:, k * TP:(k + 1) * TP],
                                                   u_tok[:, k, :, :].rearrange("p a c -> p (a c)"), ident16[0:TP, 0:TP])
                    last.then_inc(ut_full, 1)

                def h_rows(i):
                    pe.wait_ge(u_stack_set, st["norm1"] + 1)
                    for j, k in enumerate(range(2 * i, min(2 * i + 2, NT))):
                        last = mm(m_ps[0:TP, j * EMB:(j + 1) * EMB], u_stack[:, k * TP:(k + 1) * TP], c_stack[:, :])
                    last.then_inc(h1_full, 1)

                def p_columns():
                    pe.wait_ge(p_tok_set, st["norm1"] + 1)
                    for k in range(NT):
                        last = nc.tensor.transpose(m_ps16[:, k * TP:(k + 1) * TP],
                                                   p_tok[:, k, :, :].rearrange("p a c -> p (a c)"), ident16[0:TP, 0:TP])
                    last.then_inc(pt_full, 1)

                def fc1(gf, c):
                    if isinstance(gf, int) and gf == 0 and c == 0:
                        pe.wait_ge(weights_split, 1)
                    m, lo = c % MT, (c // MT) * HALF_T
                    pe.wait_ge(x_stack_set, 3 * (gf + 1))
                    if c >= 2:
                        pe.wait_ge(gelu_set, CHUNKS * gf + c - 1)
                    else:
                        wait(pe, o_set, NT * gf)
                    o = f_ps[(c + 1) % 2][:, 0:HALF_T]
                    parts = [(w1_hi, 0), (w1_lo, 0), (w1_hi, 1), (w1_lo, 1), (w1_hi, 2)]
                    for i, (w, k) in enumerate(parts):
                        last = mm(o, w[:, k, m * 128:(m + 1) * 128], x_stack[:, k, lo:lo + HALF_T], start=i == 0,
                                  stop=i == len(parts) - 1)
                    last.then_inc(fc1_full, 1)

                def fc2(i):
                    gf = st["fc2"]
                    pe.wait_ge(hid_set, CHUNKS * gf + (MT if (i + 1) * TP <= HALF_T else CHUNKS))
                    if i < 2:
                        pe.wait_ge(gelu_set, CHUNKS * gf + CHUNKS - 1 + i)
                    else:
                        pe.wait_ge(o_set, NT * gf + i - 1)
                    o = f_ps[(i + 1) % 2][0:TP, 0:EMB]
                    mm(o, ones_pad[:, :], b2_stack[:, :], stop=False)
                    for m in range(MT):
                        for part, w in ((0, w2_hi), (0, w2_lo), (1, w2_hi)):
                            last = mm(o, hid[:, part, m, i * TP:(i + 1) * TP], w[:, m, :], start=False,
                                      stop=m == MT - 1 and part == 1)
                    last.then_inc(fc2_full, 1)

                shared = {"v": v_product, "h2": y_rows, "xt": x_columns, "ut": lambda i: u_columns(), "h1": h_rows,
                          "pt": lambda i: p_columns()}
                for s in range(SLOTS):
                    if g_pair(st, s, 3) is not None:
                        g_product(*g_pair(st, s, 3))
                    if g is not None:
                        scores_k0(s)
                        if s >= 3 and s % 2 == 1:
                            attend_v(g, s // 2 - 1)
                        scores_k1(s)
                    if s == 0 and st["last_av"] is not None:
                        attend_v(st["last_av"], NQUAD - 1)
                    due = [(i, what, k) for i, (slot, what, k, _) in enumerate(uses) if slot == s]
                    early = [use for use in due if use[1] in ("v", "ut", "h1", "pt")]
                    for i, what, k in early:
                        wait_shared(i)
                        shared[what](k)
                    if st["fc2"] is not None and s in FC2_SLOTS:
                        fc2(FC2_SLOTS.index(s))
                    for i, what, k in due[len(early):]:
                        wait_shared(i)
                        shared[what](k)
                    if fc1_chunk(st, s) is not None:
                        fc1(*fc1_chunk(st, s))

            iterations(pe, body)

            pe.wait_ge(cls_in, 32)
            pe.wait_ge(relu0_v, NR_V * NG)
            pe.wait_ge(o_set, NT * NG)
            for ps, k, n0, nn in CT_PARTS:
                for j in range(nn):
                    last = nc.tensor.transpose(ps[0:EH, j * 128:(j + 1) * 128], cx[:, n0 + j, k * EH:(k + 1) * EH],
                                               ident32[:, :])
                last.then_inc(ct_full, 1)
            pe.wait_ge(ct_set, len(CT_PARTS))
            pe.wait_ge(cls_w_in, 16 * 8)

            def atom_hidden(a):
                toks = ATOM_TOKENS[a]
                n = 128 * len(toks)
                step = toks[1] - toks[0]
                for m in range(MT):
                    u = a * MT + m
                    if u >= 2:
                        pe.wait_ge(ch_set, u - 1)
                    for k in range(2):
                        last = mm(f_ps[u % 2][:, 0:n], a_in[:, k, a * HID + m * 128:a * HID + (m + 1) * 128],
                                  cx_t[0:EH, k, toks[0]:toks[-1] + 1:step, :], start=k == 0, stop=k == 1)
                    last.then_inc(ch_full, 1)

            def atom_candidates(a):
                pe.wait_ge(ch_set, (a + 1) * MT)
                for j, n in enumerate(ATOM_TOKENS[a]):
                    u = CANDS_BEFORE[a] + j
                    r = 0 if a < 3 else 1
                    if u >= 2:
                        pe.wait_ge(cand_tmp, u - 1)
                    for m in range(MT):
                        w = a_out_early[:, m, :] if m < MT // 2 else a_out_late[:, m - MT // 2, :]
                        last = mm(s_ps[u % 2][:, 0:EMB], c_hid[a % 2][:, m, j * 128:(j + 1) * 128],
                                  w[:, DST[n][r] * EMB:(DST[n][r] + 1) * EMB], start=m == 0, stop=m == MT - 1)
                    last.then_inc(cand_full, 1)

            atom_hidden(0)
            for a in range(NATOM):
                if a + 1 < NATOM:
                    atom_hidden(a + 1)
                atom_candidates(a)

        @block.vector
        def _(dve):
            count = [0]

            def step(ins):
                count[0] += 1
                ins.then_inc(setup_v, 1)
                dve.wait_ge(setup_v, count[0])

            v = nc.vector
            dve.wait_ge(attn_in, 16 * ATTN)
            step(v.tensor_reduce(c_sum[:, 0:1], c_raw[:, :], AX.X, ALU.add))
            step(v.tensor_scalar(c_sum[:, 1:2], c_sum[:, 0:1], -1.0 / EMB, None, ALU.mult))
            step(v.tensor_scalar(c_cen[:, :], c_raw[:, :], c_sum[:, 1:2], None, ALU.add))
            dve.wait_ge(setup_p, 1)

            def split_rows(dst, src, tmp):
                step(v.tensor_copy(tmp, src))
                step(v.tensor_copy(dst[0:32, :], src[0:32, :]))
                step(v.tensor_tensor(dst[32:64, :], src[32:64, :], tmp[32:64, :], ALU.subtract))

            split_rows(c_stack[:, :], g_ps[0:64, 0:EMB], setup16[:, 0:EMB])
            step(v.tensor_copy(cct[:, 0, :], s_ps[0][:, 0:64]))
            step(v.tensor_copy(cct[0:64, 1, :], s_ps[0][0:64, 64:128]))
            dve.wait_ge(const_in, 16 * CONSTS)
            v.memset(u_tok[:, :, :, :], 0.0)
            for stack in (c_stack, a_stack, mv_stack):
                v.memset(stack[64:128, :], 0.0)
            v.memset(p_stack[64:128, :, 0, :], 0.0)
            v.memset(p_stack[0:64, :, 1, :], 0.0)
            v.tensor_scalar(mask_big[:, :], mask_k0[:, 0:128], -1.0, BIG, ALU.add, ALU.mult)
            v.tensor_scalar(ident_big[:, :], ident32[:, :], BIG, None, ALU.mult)
            v.memset(p_tok[:, :, :, :], 0.0).then_inc(memory_set, 1)
            dve.wait_ge(memory_set, 1)
            v.memset(p_tok[:, :, 0:8:2, NCH:NCH + 1], 1.0)
            v.memset(v0[:, :, :, :], 0.0)
            v.memset(v1[:, :, :, :], 0.0)
            v.memset(half_c[:, :], 0.5)
            v.memset(minus_half[:, :], -0.5).then_inc(memory_set, 1)
            dve.wait_ge(memory_set, 2)

            def heads_view(ps, c, n):
                return ps[0:HD, c:c + 64 * n].rearrange("p (h c) -> p h c", h=n)

            def make_head_matrices():
                dve.wait_ge(setup_p, 2)
                step(v.tensor_scalar(mq_t[:, 0:8, :], heads_view(s_ps[1], 0, 8), HD ** -0.5, None, ALU.mult))
                step(v.tensor_scalar(mq_t[:, 8:12, :], heads_view(k1_ps, 0, 4), HD ** -0.5, None, ALU.mult))
                step(v.tensor_copy(mk_t[:, 0:4, :], heads_view(k1_ps, 256, 4)))
                step(v.tensor_copy(mk_t[:, 4:12, :], heads_view(y_ps, 0, 8)))
                split_rows(mv_stack[:, :], f_ps[0][0:64, 0:EMB], setup16[:, 0:EMB])

            def make_a_stack():
                dve.wait_ge(setup_p, 3)
                split_rows(a_stack[:, 0:512], g_ps[0:64, :], setup16[:, 0:512])
                split_rows(a_stack[:, 512:768], s_ps[0][0:64, 0:256], setup16[:, 512:768])

            def split_weights():
                dve.wait_ge(wts_in, 16 * WEIGHTS)
                step(v.tensor_scalar(w1_hi[:, :, :], w1_raw[:, :, :], WSCALE, None, ALU.mult))
                step(v.scalar_tensor_tensor(w1_lo[:, 0, :], w1_raw[:, 0, :], WSCALE, w1_hi[:, 0, :],
                                            ALU.mult, ALU.subtract))
                step(v.scalar_tensor_tensor(w1_lo[0:64, 1, :], w1_raw[0:64, 1, :], WSCALE, w1_hi[0:64, 1, :],
                                            ALU.mult, ALU.subtract))
                step(v.memset(w1_lo[64:128, 1, :], 0.0))
                step(v.tensor_scalar(w2_hi[:, :, :], w2_raw[:, :, :], WSCALE, None, ALU.mult))
                step(v.scalar_tensor_tensor(w2_lo[:, :, :], w2_raw[:, :, :], WSCALE, w2_hi[:, :, :],
                                            ALU.mult, ALU.subtract))
                step(v.memset(b2_stack[:, :], 0.0))
                step(v.tensor_scalar(b2_stack[0:1, :], b2_raw[0:1, :], WSCALE, None, ALU.mult))
                step(v.tensor_scalar(b2_tmp[32:33, :], b2_raw[32:33, :], WSCALE, None, ALU.mult))
                step(v.scalar_tensor_tensor(b2_stack[32:33, :], b2_raw[32:33, :], WSCALE, b2_tmp[32:33, :],
                                            ALU.mult, ALU.subtract))
                v.memset(xhat[:, 0:1], 0.0).then_inc(weights_split, 1)

            def body(t, st, before):
                par = st["par"]
                g = st["attend"]

                def split_g(gg, u):
                    dve.wait_ge(g_hi_set, SLOTS // 2 * gg + u + 1)
                    wait(dve, k1_full, SLOTS * gg + 2 * u - 4)
                    v.scalar_tensor_tensor(g_stack[:, u % 3, :], g_hi[:, u % 2, :], neg_lo[:, 0:1],
                                           g_ps[:, 0:2 * TOK], ALU.mult, ALU.add).then_inc(g_split, 1)

                def relu_k0(s):
                    dve.wait_ge(scores_full, SLOTS * g + s + 1)
                    wait(dve, y_full, NQUAD * g + s // 2 - 1)
                    v.scalar_tensor_tensor(st0[:, s % 4, :], s_ps[s % 2][:, 0:2 * TOK], 0.0, mask_k0[:, :],
                                           ALU.max, ALU.mult).then_inc(relu0_v, 1)

                def y_low(gy, q, gpar):
                    dve.wait_ge(y_hi_set, NQUAD * gy + q + 1)
                    b = q // QUADS
                    c = slice(b * TOK, (b + 1) * TOK)
                    v.tensor_tensor(y_t[:, gpar, 1, q % QUADS, c], y_ps[:, 0:TOK], y_t[:, gpar, 0, q % QUADS, c],
                                    ALU.subtract).then_inc(y_lo_set, 1)

                def window_sums(gp, hk, gpar):
                    dve.wait_ge(x_halved, NHALF * gp + hk + 1)
                    w = x_ring[0:TP, hk % RING, :].rearrange("p (c n) -> p c n", c=HCH)
                    c = (hk % 2) * HCH
                    v.tensor_reduce(pooled[:, gpar, hk // 2, c:c + HCH], w[:, :, 0:PIX // 2], AX.X,
                                    ALU.add).then_inc(x_pooled, 1)

                def variance(bn, tmp, var, part_set, sq_set, gn):
                    v.tensor_tensor(tmp[:, 0, :], bn[:, :, 1], bn[:, :, 4], ALU.subtract)
                    v.scalar_tensor_tensor(tmp[:, 1, :], bn[:, :, 2], EMB * EPS, bn[:, :, 5], ALU.add,
                                           ALU.add).then_inc(part_set, 1)
                    dve.wait_ge(part_set, gn + 1)
                    v.scalar_tensor_tensor(tmp[:, 2, :], tmp[:, 0, :], 0.25, tmp[:, 0, :], ALU.mult,
                                           ALU.mult).then_inc(sq_set, 1)
                    dve.wait_ge(sq_set, gn + 1)
                    return v.scalar_tensor_tensor(var[:, :], tmp[:, 1, :], 1.0 / EMB, tmp[:, 2, :], ALU.mult, ALU.add)

                def residual(i):
                    n2 = st["norm2"]
                    n = min(2, NT - 2 * i)
                    c = slice(2 * i * EMB, (2 * i + n) * EMB)
                    dve.wait_ge(h2_full, NPAIR * n2 + i + 1)
                    if i == 0:
                        dve.wait_ge(h_set, NPAIR * (n2 + 1))
                        wait(dve, cls_out, 32 * GI * (n2 - 1))
                        wait(dve, o_set, NT * (n2 - 1))
                    v.tensor_tensor(h2_tok[0:TP, 1 - par, c], m_ps[0:TP, 0:n * EMB], h_tok[0:TP, 1 - par, c],
                                    ALU.add).then_inc(h2_set, 1)
                    dve.wait_ge(h2_set, NPAIR * n2 + i + 1)
                    for k in range(2 * i, 2 * i + n):
                        last = v.bn_stats(bn2[:, k, :], h2_tok[0:TP, 1 - par, k * EMB:(k + 1) * EMB])
                    last.then_inc(bn2_set, 1)

                for s in range(SLOTS):
                    if isinstance(t, int) and t == FIRST_T and s == NEXT_SUM_SLOTS[-2]:
                        make_head_matrices()
                    if s == 0 and st["last_av"] is not None:
                        y_low(st["last_av"], NQUAD - 2, 1 - par)
                    if s == 1 and st["last_av"] is not None:
                        y_low(st["last_av"], NQUAD - 1, 1 - par)
                    if g_pair(st, s, 2) is not None:
                        split_g(*g_pair(st, s, 2)[0:2])
                    if st["norm2"] is not None:
                        n2 = st["norm2"]
                        if 0 <= s - 1 - H2_SLOT < NPAIR:
                            residual(s - 1 - H2_SLOT)
                        if s == STAT2_SLOT:
                            dve.wait_ge(bn2_set, NPAIR * (n2 + 1))
                            v.tensor_tensor(sum2[:, :], bn2[:, :, 1], bn2[:, :, 4], ALU.add)
                            variance(bn2, st2s, var2, part2_set, sq2_set, n2).then_inc(var2_set, 1)
                        if s == XHAT_SLOT:
                            dve.wait_ge(rstd2_set, n2 + 1)
                            v.scalar_tensor_tensor(shift2[:, :], sum2[:, :], -0.5, rstd2[:, :], ALU.mult,
                                                   ALU.mult).then_inc(shift2_set, 1)
                            dve.wait_ge(shift2_set, n2 + 1)
                            wait(dve, cls_out, 32 * GI * n2)
                            wait(dve, x_hi_set, n2)
                            wait(dve, x_lo_vector, n2)
                            for k in range(XHAT_ACT, NT):
                                c = slice(k * EMB, (k + 1) * EMB)
                                last = v.tensor_scalar(xhat[0:TP, c], h2_tok[0:TP, 1 - par, c], rstd2[:, k:k + 1],
                                                       shift2[:, k:k + 1], ALU.mult, ALU.add)
                            last.then_inc(xhat_v, 1)
                        if s == X_LO_SLOT + 1:
                            k = slice(X_LO_POOL, NT)
                            dve.wait_ge(x_hi_set, n2 + 1)
                            v.tensor_tensor(x_tok[:, k, 1, :], xhat[0:TP, :].rearrange("p (k e) -> p k e", k=NT)[:, k, :],
                                            x_tok[:, k, 0, :], ALU.subtract).then_inc(x_lo_vector, 1)
                    if st["pool_cur"] is not None and s in SUM_CUR:
                        window_sums(st["pool_cur"], SUM_CUR[s], 1 - par)
                    if st["pool_next"] is not None and s in SUM_NEXT:
                        window_sums(st["pool_next"], SUM_NEXT[s], par)
                    if st["fc2"] is not None and s - 1 in FC2_SLOTS:
                        gf, i = st["fc2"], FC2_SLOTS.index(s - 1)
                        dve.wait_ge(fc2_full, NT * gf + i + 1)
                        if i == 0:
                            wait(dve, out_done, 16 * gf)
                        c = slice(i * EMB, (i + 1) * EMB)
                        v.scalar_tensor_tensor(o_tok[0:TP, c], f_ps[(i + 1) % 2][0:TP, 0:EMB], 1.0 / WSCALE,
                                               h2_tok[0:TP, par, c], ALU.mult, ALU.add).then_inc(o_set, 1)
                    if g is not None and s >= 4 and s % 2 == 0:
                        y_low(g, s // 2 - 2, par)
                    if g is not None and s not in ACT_RELU:
                        relu_k0(s)
                    if st["norm1"] is not None:
                        n1 = st["norm1"]
                        if s == U_SLOT:
                            sums = pooled[:, 1 - par, :, :].unsqueeze(2).broadcast_to([TP, NT, 2, NCH])
                            dve.wait_ge(x_pooled, NHALF * (n1 + 1))
                            wait(dve, ut_full, n1)
                            v.tensor_copy(u_tok[:, :, 0:4:2, 0:NCH], sums).then_inc(u_hi_set, 1)
                            dve.wait_ge(u_hi_set, n1 + 1)
                            v.tensor_tensor(u_tok[:, :, 1:4:2, 0:NCH], sums,
                                            u_tok[:, :, 0:1, 0:NCH].broadcast_to([TP, NT, 2, NCH]),
                                            ALU.subtract).then_inc(u_tok_set, 1)
                        if 0 <= s - H1_SLOT - 1 < NPAIR:
                            i = s - H1_SLOT - 1
                            dve.wait_ge(h_set, NPAIR * n1 + i + 1)
                            for k in range(2 * i, min(2 * i + 2, NT)):
                                last = v.bn_stats(bn1[:, k, :], h_tok[0:TP, 1 - par, k * EMB:(k + 1) * EMB])
                            last.then_inc(bn1_set, 1)
                        if s == STAT1_SLOT:
                            dve.wait_ge(bn1_set, NPAIR * (n1 + 1))
                            variance(bn1, st1s, var1, part1_set, sq1_set, n1).then_inc(var1_set, 1)
                        if s == PN_SLOT:
                            dve.wait_ge(rstd1_set, n1 + 1)
                            v.tensor_tensor(pn[:, :, :], pooled[:, 1 - par, :, :],
                                            rstd1[:, :].unsqueeze(2).broadcast_to([TP, NT, NCH]),
                                            ALU.mult).then_inc(pn_set, 1)
                            p4 = pn[:, :, :].unsqueeze(2).broadcast_to([TP, NT, 4, NCH])
                            dve.wait_ge(pn_set, n1 + 1)
                            wait(dve, pt_full, n1)
                            v.tensor_copy(p_tok[:, :, 0:8:2, 0:NCH], p4).then_inc(p_hi_set, 1)
                            dve.wait_ge(p_hi_set, n1 + 1)
                            v.tensor_tensor(p_tok[:, :, 1:8:2, 0:NCH], p4,
                                            p_tok[:, :, 0:1, 0:NCH].broadcast_to([TP, NT, 4, NCH]),
                                            ALU.subtract).then_inc(p_tok_set, 1)

            iterations(dve, body, between=(make_a_stack, split_weights))

            done = [0]

            def link(ins):
                done[0] += 1
                ins.then_inc(cls_v, 1)
                dve.wait_ge(cls_v, done[0])

            dve.wait_ge(cls_in, 32)
            dve.wait_ge(cls_w_in, 16 * 8)
            dve.wait_ge(h2_full, NPAIR * NG)
            link(v.tensor_tensor(gate_tmp[:, 0:NCLS, :], cx, cx, ALU.mult))
            link(v.tensor_reduce(ss[:, 0:NCLS], gate_tmp[:, 0:NCLS, :], AX.X, ALU.add))
            link(v.tensor_tensor(gate_tmp, gate_w, gate_w, ALU.mult))
            link(v.tensor_reduce(ss[:, NCLS:3 * NCLS], gate_tmp, AX.X, ALU.add))
            assert done[0] == CLS_SS
            by_route = gate_tmp.rearrange("p (n r) e -> p n r e", r=2)
            link(v.tensor_tensor(by_route, cx.unsqueeze(2).broadcast_to([128, NCLS, 2, EMB]),
                                 gate_w.rearrange("p (n r) e -> p n r e", r=2), ALU.mult))
            link(v.tensor_reduce(lg[:, :, :].rearrange("p n r -> p (n r)"), gate_tmp, AX.X, ALU.add))
            dve.wait_ge(cls_pow, 1)
            link(v.tensor_scalar(nrm[:, :], nrm[:, :], 1e-12, None, ALU.max))
            link(v.reciprocal(nrm[:, :], nrm[:, :]))
            flat = lg[:, :, :].rearrange("p n r -> p (n r)")
            link(v.tensor_tensor(flat, flat, nrm[:, NCLS:3 * NCLS], ALU.mult))
            link(v.tensor_tensor(lg[:, :, :], lg[:, :, :], nrm[:, 0:NCLS].unsqueeze(2).broadcast_to([128, NCLS, 2]), ALU.mult))
            link(v.tensor_tensor(flat, flat, bal[:, :], ALU.add))
            link(v.tensor_tensor(gs[:, 0, :], lg[:, :, 0], lg[:, :, 1], ALU.max))
            link(v.tensor_tensor(lg[:, :, :], lg[:, :, :], gs[:, 0, :].unsqueeze(2).broadcast_to([128, NCLS, 2]), ALU.subtract))
            assert done[0] == CLS_LG
            dve.wait_ge(cls_exp, 1)
            link(v.tensor_tensor(gs[:, 1, :], pr[:, :, 0], pr[:, :, 1], ALU.add))
            link(v.reciprocal(gs[:, 2, :], gs[:, 1, :]))
            link(v.tensor_tensor(pr[:, :, :], pr[:, :, :], gs[:, 2, :].unsqueeze(2).broadcast_to([128, NCLS, 2]), ALU.mult))
            link(v.tensor_tensor(gs[:, 3, :], pr[:, :, 1], pr[:, :, 0], ALU.is_gt))
            link(v.tensor_scalar(gs[:, 4, :], gs[:, 3, :], -1.0, 1.0, ALU.mult, ALU.add))
            link(v.tensor_tensor(wgt[:, :, 1], pr[:, :, 1], gs[:, 3, :], ALU.mult))
            link(v.tensor_tensor(wgt[:, :, 0], pr[:, :, 0], gs[:, 4, :], ALU.mult))
            dve.wait_ge(out_done, 16 * NG)
            dve.wait_ge(x_lo_pool, NG)
            dve.wait_ge(cls_out, 32 * GI * NG)
            for a in range(NATOM):
                r = 0 if a < 3 else 1
                for j, n in enumerate(ATOM_TOKENS[a]):
                    u = CANDS_BEFORE[a] + j
                    dve.wait_ge(cand_full, u + 1)
                    wait(dve, cand_set, u)
                    v.tensor_tensor(c_tmp[:, u % 2, :], s_ps[u % 2][:, 0:EMB], b_out[:, DST[n][r], :],
                                    ALU.add).then_inc(cand_tmp, 1)
                    dve.wait_ge(cand_tmp, u + 1)
                    base = ch[:, n, :] if r == 0 else c_acc[:, n, :]
                    v.scalar_tensor_tensor(c_acc[:, n, :], c_tmp[:, u % 2, :], wgt[:, n, r:r + 1], base,
                                           ALU.mult, ALU.add).then_inc(cand_set, 1)


def kernel(x, L0_tok_channel_weights, L0_attn_W_attn, L0_attn_b_attn, L0_ffn_fc1_w, L0_ffn_fc1_b, L0_ffn_fc2_w,
           L0_ffn_fc2_b, L0_ffn_gate_pair, L0_ffn_atom_in_w, L0_ffn_atom_in_b, L0_ffn_atom_out_w, L0_ffn_atom_out_b,
           L0_ffn_balance_bias):
    import concourse.bacc as bacc
    from concourse.bass_utils import run_bass_kernel_spmd

    def lay(a):
        return np.ascontiguousarray(a)

    f = np.float32
    rows = np.arange(128)
    head_sel = np.zeros((128, 64), np.float16)
    for j in range(4):
        for k in range(HD):
            head_sel[32 * j + k, HD * j + k] = 1
    causal = (np.arange(TOK)[None, :] >= rows[:, None]).astype(f)
    spread = np.zeros((NCH, 64), f)
    bias_row = np.zeros((1, 64), f)
    for part in range(4):
        for c in range(NCH):
            spread[c, 16 * part + c] = 1
        bias_row[0, 16 * part + NCH] = 1
    ones_pad = np.zeros((128, TP), np.float16)
    ones_pad[0] = ones_pad[32] = 1
    arrays = {
        "ident16": np.eye(128, dtype=np.float16), "ident32": np.eye(128, dtype=f), "head_sel": head_sel,
        "mask_k0": np.concatenate([causal, causal], 1),
        "neg_lo": -((rows // 32) % 2).astype(f)[:, None], "spread": spread, "bias_row": bias_row, "ones_pad": ones_pad,
        "x": lay(np.asarray(x).reshape(NIMG, NCH, SIDE, PATCH, SIDE, PATCH).transpose(0, 2, 4, 1, 3, 5)).reshape(
            NIMG * TOK, ROW),
        "cw": lay(L0_tok_channel_weights),
        "wa_t": lay(np.asarray(L0_attn_W_attn).T), "b_attn": lay(np.asarray(L0_attn_b_attn).reshape(1, 3 * EMB)),
        "w1_t": lay(np.asarray(L0_ffn_fc1_w).T), "w2_t": lay(np.asarray(L0_ffn_fc2_w).T),
        "b1": lay(np.asarray(L0_ffn_fc1_b).reshape(MT, 128).T), "b2": lay(np.asarray(L0_ffn_fc2_b).reshape(1, EMB)),
        "gate": lay(np.asarray(L0_ffn_gate_pair).reshape(-1)),
        "a_in_t": lay(np.asarray(L0_ffn_atom_in_w).reshape(NATOM * HID, EMB).T),
        "b_in": lay(np.asarray(L0_ffn_atom_in_b).reshape(NATOM * MT, 128).T),
        "a_out_t": lay(np.asarray(L0_ffn_atom_out_w).transpose(2, 0, 1)).reshape(HID, NATOM * EMB),
        "b_out": lay(np.asarray(L0_ffn_atom_out_b).reshape(-1)),
        "bal": lay(np.asarray(L0_ffn_balance_bias).reshape(-1)),
    }
    nc = bacc.Bacc("TRN2", target_bir_lowering=False, num_devices=1)
    d = {n: nc.dram_tensor("in_" + n, a.shape, mybir.dt.from_np(a.dtype), kind="ExternalInput").ap() for n, a in arrays.items()}
    out = nc.dram_tensor("out", (NIMG * TOK, EMB), F32, kind="ExternalOutput").ap()
    cls_x = nc.dram_tensor("cls_x", (NIMG * NCLS, EMB), F32, kind="Internal").ap()
    cls_h = nc.dram_tensor("cls_h", (NIMG * NCLS, EMB), F32, kind="Internal").ap()
    vit_tower_kernel(nc, d, out, cls_x, cls_h)
    r = run_bass_kernel_spmd(nc, [{"in_" + n: a for n, a in arrays.items()}], core_ids=[0])
    return r.results[0]["out"].reshape(NIMG, TOK, EMB)
```
